# Optimizing a Trainium2 kernel written in Bass

```python
import numpy as np
import jax
import jax.numpy as jnp

def _softmax(x, axis=-1):
    return jax.nn.softmax(x, axis=axis)

def _gelu(x):
    return jax.nn.gelu(x, approximate=True)

def _silu(x):
    return jax.nn.silu(x)

def _sigmoid(x):
    return jax.nn.sigmoid(x)

def _layernorm(x, axis=-1, eps=1e-05):
    m = jnp.mean(x, axis=axis, keepdims=True)
    v = jnp.var(x, axis=axis, keepdims=True)
    return (x - m) / jnp.sqrt(v + eps)

def _scatter_add(tgt, idx, src, axis=0):
    return tgt.at[idx].add(src)

def _segment_sum(src, seg, n):
    return jax.ops.segment_sum(src, seg, n)
kernel_name = 'mk_xattn_seq_d1_seqx_r4_6f484b'

def setup_inputs(seed: int=0):
    np.random.seed(seed)
    _w = jnp.asarray

    def _rec_inputs():
        import jax
        import jax.numpy as jnp
        _rk = jax.random.key(seed)
        x = -0.0002928 + 1 * jax.random.normal(jax.random.fold_in(_rk, 1), (16, 256, 256), jnp.float32)
        _lenS = 256 - jax.random.randint(jax.random.fold_in(_rk, 7), (16,), 0, max(1, 256 // 4) + 1, jnp.int32)
        _lenS2 = 256 - jax.random.randint(jax.random.fold_in(_rk, 8), (16,), 0, max(1, 256 // 4) + 1, jnp.int32)
        _ctx_1024P = jax.random.normal(jax.random.fold_in(_rk, 11), (16, 16, 256), jnp.float32)
        _ctx_1024c = jax.random.dirichlet(jax.random.fold_in(_rk, 511), 0.3 * jnp.ones((16,), jnp.float32), (16, 256))
        _ctx_1024t = jnp.einsum('bsk,bkd->bsd', _ctx_1024c, _ctx_1024P)
        _ctx_1024t = _ctx_1024t * jax.lax.rsqrt(jnp.mean(jnp.square(_ctx_1024t)) + 1e-12) * 0.953939
        ctx_1024 = -1.39393e-06 + 0.999914 * (_ctx_1024t + 0.3 * jax.random.normal(jax.random.fold_in(_rk, 611), (16, 256, 256), jnp.float32))
        return (x, ctx_1024)
    x, ctx_1024 = _rec_inputs()

    def _L0_xattn_setup():
        import jax, jax.numpy as jnp
        import numpy as np
        B, S, SE, D, H, FF, E, K = (2, 512, 512, 256, 16, 1024, 8, 2)
        HD = D // H

        def _layernorm(x, g, b):
            m = x.mean(-1, keepdims=True)
            v = ((x - m) ** 2).mean(-1, keepdims=True)
            return (x - m) / jnp.sqrt(v + 1e-05) * g + b

        def _attn(q_in, k_in, v_in, wq, bq, wk, bk, wv, bv, wo, bo, causal):
            Bq, Sq, Dm = q_in.shape
            Sk = k_in.shape[1]
            Q = (q_in @ wq + bq).reshape(Bq, Sq, H, HD)
            Kp = (k_in @ wk + bk).reshape(Bq, Sk, H, HD)
            V = (v_in @ wv + bv).reshape(Bq, Sk, H, HD)
            scores = jnp.einsum('bqhd,bkhd->bhqk', Q, Kp) / jnp.sqrt(jnp.float32(HD))
            if causal:
                mask = jnp.tril(jnp.ones((Sq, Sk), bool))
                scores = jnp.where(mask, scores, -jnp.inf)
            a = jax.nn.softmax(scores, axis=-1)
            o = jnp.einsum('bhqk,bkhd->bqhd', a, V).reshape(Bq, Sq, Dm)
            return o @ wo + bo

        def _moe(x, rw, rb, w1, b1, w2, b2):
            T = x.shape[0] * x.shape[1]
            xf = x.reshape(T, D)
            router_weights = jax.nn.softmax(xf @ rw + rb, axis=-1)
            topw, topi = jax.lax.top_k(router_weights, K)
            topw = jax.nn.softmax(topw, axis=-1)
            combine = jnp.zeros((T, E), xf.dtype).at[jnp.arange(T)[:, None], topi].add(topw)
            h = jax.nn.gelu(jnp.einsum('td,edf->etf', xf, w1) + b1[:, None, :], approximate=False)
            eo = jnp.einsum('etf,efd->etd', h, w2) + b2[:, None, :]
            out = jnp.einsum('etd,te->td', eo, combine)
            return out.reshape(x.shape)
        key = jax.random.key(seed)
        ks = jax.random.split(key, 32)
        w = lambda k, shape: jax.random.normal(k, shape, jnp.float32) * 0.02
        inp = {'x': jax.random.normal(ks[0], (B, S, D), jnp.float32), 'encoder_output': jax.random.normal(ks[1], (B, SE, D), jnp.float32), 'sa_wq': w(ks[2], (D, D)), 'sa_bq': jnp.zeros((D,), jnp.float32), 'sa_wk': w(ks[3], (D, D)), 'sa_bk': jnp.zeros((D,), jnp.float32), 'sa_wv': w(ks[4], (D, D)), 'sa_bv': jnp.zeros((D,), jnp.float32), 'sa_wo': w(ks[5], (D, D)), 'sa_bo': jnp.zeros((D,), jnp.float32), 'ca_wq': w(ks[6], (D, D)), 'ca_bq': jnp.zeros((D,), jnp.float32), 'ca_wk': w(ks[7], (D, D)), 'ca_bk': jnp.zeros((D,), jnp.float32), 'ca_wv': w(ks[8], (D, D)), 'ca_bv': jnp.zeros((D,), jnp.float32), 'ca_wo': w(ks[9], (D, D)), 'ca_bo': jnp.zeros((D,), jnp.float32), 'ln1_g': jnp.ones((D,), jnp.float32), 'ln1_b': jnp.zeros((D,), jnp.float32), 'ln2_g': jnp.ones((D,), jnp.float32), 'ln2_b': jnp.zeros((D,), jnp.float32), 'ln3_g': jnp.ones((D,), jnp.float32), 'ln3_b': jnp.zeros((D,), jnp.float32), 'router_w': w(ks[10], (D, E)), 'router_b': jnp.zeros((E,), jnp.float32), 'e_w1': w(ks[11], (E, D, FF)), 'e_b1': jnp.zeros((E, FF), jnp.float32), 'e_w2': w(ks[12], (E, FF, D)), 'e_b2': jnp.zeros((E, D), jnp.float32)}
        return inp
    _L0_xattn_all = _L0_xattn_setup()
    _L0_xattn_in = {k: v for k, v in _L0_xattn_all.items() if k in ('sa_wq', 'sa_bq', 'sa_wk', 'sa_bk', 'sa_wv', 'sa_bv', 'sa_wo', 'sa_bo', 'ca_wq', 'ca_bq', 'ca_wk', 'ca_bk', 'ca_wv', 'ca_bv', 'ca_wo', 'ca_bo', 'ln1_g', 'ln1_b', 'ln2_g', 'ln2_b', 'ln3_g', 'ln3_b', 'router_w', 'router_b', 'e_w1', 'e_b1', 'e_w2', 'e_b2')}
    del _L0_xattn_all
    return {'x': x, 'ctx_1024': ctx_1024, 'L0_xattn_sa_wq': _L0_xattn_in['sa_wq'], 'L0_xattn_sa_bq': _L0_xattn_in['sa_bq'], 'L0_xattn_sa_wk': _L0_xattn_in['sa_wk'], 'L0_xattn_sa_bk': _L0_xattn_in['sa_bk'], 'L0_xattn_sa_wv': _L0_xattn_in['sa_wv'], 'L0_xattn_sa_bv': _L0_xattn_in['sa_bv'], 'L0_xattn_sa_wo': _L0_xattn_in['sa_wo'], 'L0_xattn_sa_bo': _L0_xattn_in['sa_bo'], 'L0_xattn_ca_wq': _L0_xattn_in['ca_wq'], 'L0_xattn_ca_bq': _L0_xattn_in['ca_bq'], 'L0_xattn_ca_wk': _L0_xattn_in['ca_wk'], 'L0_xattn_ca_bk': _L0_xattn_in['ca_bk'], 'L0_xattn_ca_wv': _L0_xattn_in['ca_wv'], 'L0_xattn_ca_bv': _L0_xattn_in['ca_bv'], 'L0_xattn_ca_wo': _L0_xattn_in['ca_wo'], 'L0_xattn_ca_bo': _L0_xattn_in['ca_bo'], 'L0_xattn_ln1_g': _L0_xattn_in['ln1_g'], 'L0_xattn_ln1_b': _L0_xattn_in['ln1_b'], 'L0_xattn_ln2_g': _L0_xattn_in['ln2_g'], 'L0_xattn_ln2_b': _L0_xattn_in['ln2_b'], 'L0_xattn_ln3_g': _L0_xattn_in['ln3_g'], 'L0_xattn_ln3_b': _L0_xattn_in['ln3_b'], 'L0_xattn_router_w': _L0_xattn_in['router_w'], 'L0_xattn_router_b': _L0_xattn_in['router_b'], 'L0_xattn_e_w1': _L0_xattn_in['e_w1'], 'L0_xattn_e_b1': _L0_xattn_in['e_b1'], 'L0_xattn_e_w2': _L0_xattn_in['e_w2'], 'L0_xattn_e_b2': _L0_xattn_in['e_b2']}

def reference(x, ctx_1024, L0_xattn_sa_wq, L0_xattn_sa_bq, L0_xattn_sa_wk, L0_xattn_sa_bk, L0_xattn_sa_wv, L0_xattn_sa_bv, L0_xattn_sa_wo, L0_xattn_sa_bo, L0_xattn_ca_wq, L0_xattn_ca_bq, L0_xattn_ca_wk, L0_xattn_ca_bk, L0_xattn_ca_wv, L0_xattn_ca_bv, L0_xattn_ca_wo, L0_xattn_ca_bo, L0_xattn_ln1_g, L0_xattn_ln1_b, L0_xattn_ln2_g, L0_xattn_ln2_b, L0_xattn_ln3_g, L0_xattn_ln3_b, L0_xattn_router_w, L0_xattn_router_b, L0_xattn_e_w1, L0_xattn_e_b1, L0_xattn_e_w2, L0_xattn_e_b2):
    import jax
    import jax.numpy as jnp

    def _L0_xattn_ref(x, encoder_output, sa_wq, sa_bq, sa_wk, sa_bk, sa_wv, sa_bv, sa_wo, sa_bo, ca_wq, ca_bq, ca_wk, ca_bk, ca_wv, ca_bv, ca_wo, ca_bo, ln1_g, ln1_b, ln2_g, ln2_b, ln3_g, ln3_b, router_w, router_b, e_w1, e_b1, e_w2, e_b2):
        import jax, jax.numpy as jnp
        import numpy as np
        B, S, SE, D, H, FF, E, K = (2, 512, 512, 256, 16, 1024, 8, 2)
        HD = D // H

        def _layernorm(x, g, b):
            m = x.mean(-1, keepdims=True)
            v = ((x - m) ** 2).mean(-1, keepdims=True)
            return (x - m) / jnp.sqrt(v + 1e-05) * g + b

        def _attn(q_in, k_in, v_in, wq, bq, wk, bk, wv, bv, wo, bo, causal):
            Bq, Sq, Dm = q_in.shape
            Sk = k_in.shape[1]
            Q = (q_in @ wq + bq).reshape(Bq, Sq, H, HD)
            Kp = (k_in @ wk + bk).reshape(Bq, Sk, H, HD)
            V = (v_in @ wv + bv).reshape(Bq, Sk, H, HD)
            scores = jnp.einsum('bqhd,bkhd->bhqk', Q, Kp) / jnp.sqrt(jnp.float32(HD))
            if causal:
                mask = jnp.tril(jnp.ones((Sq, Sk), bool))
                scores = jnp.where(mask, scores, -jnp.inf)
            a = jax.nn.softmax(scores, axis=-1)
            o = jnp.einsum('bhqk,bkhd->bqhd', a, V).reshape(Bq, Sq, Dm)
            return o @ wo + bo

        def _moe(x, rw, rb, w1, b1, w2, b2):
            T = x.shape[0] * x.shape[1]
            xf = x.reshape(T, D)
            router_weights = jax.nn.softmax(xf @ rw + rb, axis=-1)
            topw, topi = jax.lax.top_k(router_weights, K)
            topw = jax.nn.softmax(topw, axis=-1)
            combine = jnp.zeros((T, E), xf.dtype).at[jnp.arange(T)[:, None], topi].add(topw)
            h = jax.nn.gelu(jnp.einsum('td,edf->etf', xf, w1) + b1[:, None, :], approximate=False)
            eo = jnp.einsum('etf,efd->etd', h, w2) + b2[:, None, :]
            out = jnp.einsum('etd,te->td', eo, combine)
            return out.reshape(x.shape)
        x = _layernorm(x + _attn(x, x, x, sa_wq, sa_bq, sa_wk, sa_bk, sa_wv, sa_bv, sa_wo, sa_bo, True), ln1_g, ln1_b)
        x = _layernorm(x + _attn(x, encoder_output, encoder_output, ca_wq, ca_bq, ca_wk, ca_bk, ca_wv, ca_bv, ca_wo, ca_bo, False), ln2_g, ln2_b)
        x = _layernorm(x + _moe(x, router_w, router_b, e_w1, e_b1, e_w2, e_b2), ln3_g, ln3_b)
        return x
    x = _L0_xattn_ref(x, ctx_1024, L0_xattn_sa_wq, L0_xattn_sa_bq, L0_xattn_sa_wk, L0_xattn_sa_bk, L0_xattn_sa_wv, L0_xattn_sa_bv, L0_xattn_sa_wo, L0_xattn_sa_bo, L0_xattn_ca_wq, L0_xattn_ca_bq, L0_xattn_ca_wk, L0_xattn_ca_bk, L0_xattn_ca_wv, L0_xattn_ca_bv, L0_xattn_ca_wo, L0_xattn_ca_bo, L0_xattn_ln1_g, L0_xattn_ln1_b, L0_xattn_ln2_g, L0_xattn_ln2_b, L0_xattn_ln3_g, L0_xattn_ln3_b, L0_xattn_router_w, L0_xattn_router_b, L0_xattn_e_w1, L0_xattn_e_b1, L0_xattn_e_w2, L0_xattn_e_b2)
    return x

_drawn_inputs = setup_inputs


def setup_inputs(seed=0):
    import zlib

    import numpy as np

    out = dict(_drawn_inputs(seed))
    spreads = {'L0_xattn_sa_bq': (0.0, 0.8),
     'L0_xattn_sa_bk': (0.0, 0.8),
     'L0_xattn_sa_bv': (0.0, 0.1),
     'L0_xattn_sa_bo': (0.0, 0.1),
     'L0_xattn_ca_bq': (0.0, 0.8),
     'L0_xattn_ca_bk': (0.0, 0.8),
     'L0_xattn_ca_bv': (0.0, 0.1),
     'L0_xattn_ca_bo': (0.0, 0.1),
     'L0_xattn_ln1_g': (1.0, 0.2),
     'L0_xattn_ln1_b': (0.0, 0.1),
     'L0_xattn_ln2_g': (1.0, 0.2),
     'L0_xattn_ln2_b': (0.0, 0.1),
     'L0_xattn_ln3_g': (1.0, 0.2),
     'L0_xattn_ln3_b': (0.0, 0.1),
     'L0_xattn_router_b': (0.0, 0.1),
     'L0_xattn_e_b1': (0.0, 0.341),
     'L0_xattn_e_b2': (0.0, 0.1)}
    factors = {'L0_xattn_sa_wq': 8.0,
     'L0_xattn_sa_wk': 8.0,
     'L0_xattn_sa_wv': 3.009,
     'L0_xattn_ca_wq': 8.0,
     'L0_xattn_ca_wk': 8.0}
    for name, (base, spread) in spreads.items():
        noise = np.random.default_rng([zlib.crc32(name.encode()), seed]).standard_normal(out[name].shape)
        drawn = base * np.exp(spread * noise) if base else spread * noise
        out[name] = jnp.asarray(drawn.astype(out[name].dtype))
    for name, factor in factors.items():
        out[name] = (out[name] * factor).astype(out[name].dtype)
    return out
```

```python
import concourse.bass as bass
from concourse import mybir
from contextlib import ExitStack

F32 = mybir.dt.float32
F32R = mybir.dt.float32r
BF16 = mybir.dt.bfloat16
I32 = mybir.dt.int32
ALU = mybir.AluOpType
ACT = mybir.ActivationFunctionType
AX = mybir.AxisListType

P = 128
B, S, D, H = 16, 256, 256, 16
HD = D // H
ST = S // P
DC = D // P
HC = P // HD
G = 4
GH = H // G
VW = 32
ITEMS = 2 * B
PARTS = 3
MROW = P - 1
SCALE = float(HD) ** -0.5
MASKED = -1.0e30
EPS = 1e-5


def affine(i, times, plus):
    return plus if i is None else i * times + plus


class Item:

    def __init__(self, i, pair, parity, cross):
        self.i, self.pair, self.parity, self.cross = i, pair, parity, cross

    def of_parity(self, per, extra=0):
        return affine(self.i, per, per * self.pair + extra)

    def of_cross(self, per, extra=0):
        return self.of_parity(per, extra - per * B // 2)

    @property
    def batch(self):
        return affine(self.i, 2, 2 * self.pair + self.parity - (B if self.cross else 0))

    def exists(self):
        return self.i is not None or 0 <= 2 * self.pair + self.parity < ITEMS

    def is_number(self, n):
        return self.i is None and 2 * self.pair + self.parity == n


class Cycle:

    def __init__(self, i, pair, parity, cross=None):
        self.i, self.pair, self.parity, self.cross = i, pair, parity, cross

    def item(self, n):
        at = 2 * self.pair + self.parity + n
        return Item(self.i, at // 2, at % 2, at >= B if self.i is None else self.cross)

    def count(self, per, n, extra):
        at = per * (2 * self.pair + self.parity + n) + extra
        return min(at, per * ITEMS) if self.i is None else affine(self.i, 2 * per, at)


def wait(eng, sem, value):
    if not isinstance(value, int) or value > 0:
        eng.wait_ge(sem, value)


def run_cycles(eng, body):
    for c in range(-3, 4):
        body(Cycle(None, c // 2, c % 2))
    with eng.Fori(0, 4) as i:
        body(Cycle(i, 2, 0, False))
        body(Cycle(i, 2, 1, False))
    for c in range(12, 18):
        body(Cycle(None, c // 2, c % 2))
    with eng.Fori(0, 5) as i:
        body(Cycle(i, 9, 0, True))
        body(Cycle(i, 9, 1, True))
    for c in range(28, ITEMS + 2):
        body(Cycle(None, c // 2, c % 2))


def attention_program(nc, x, ctxt, sa, ca, ln1, ln2, out):
    stack = ExitStack()
    with stack:
        def sb(name, shape, dt=F32):
            return stack.enter_context(nc.sbuf_tensor(name, shape, dt))

        def sem(name):
            return stack.enter_context(nc.semaphore(name))

        def two(make, name, *a):
            return [make(f"{name}{k}", *a) for k in range(2)]

        x1 = nc.dram_tensor("x1_scratch", (B, P, ST, D), F32, kind="Internal").ap()
        bounce = nc.dram_tensor("qk_bounce", (2, 2, 2, HD, HC * DC * S), F32, kind="Internal").ap()

        names = ["sq", "sk", "sv", "so", "cq", "ck", "cv", "co"]
        w_in = [sb(f"w_in{k}", [P, DC, D]) for k in range(2)]
        w_hi = {n: sb(f"w_{n}_hi", [P, DC, D], F32R) for n in names}
        w_lo = {n: sb(f"w_{n}_lo", [P, DC, D], F32R) for n in names}
        qk_bias = {n: sb(f"b_{n}", [P, DC]) for n in ("sq", "sk", "cq", "ck")}
        row = {n: sb(f"row_{n}", [P, D]) for n in ("sv", "so", "cv", "co", "g1", "b1", "g2", "b2")}
        ident = sb("ident", [P, P])
        ident_bf = sb("ident_bf", [P, P], BF16)
        mask_qk = sb("mask_qk", [P, P], BF16)
        mask_kq = sb("mask_kq", [P, P], BF16)
        eps = sb("eps", [P, ST])
        minus_half = sb("minus_half", [P, ST])

        x_in = two(sb, "x_in", [P, ST, D])
        c_in = two(sb, "c_in", [P, ST, D])
        x_res = two(sb, "x_res", [P, ST, D])
        xt_hi = two(sb, "xt_hi", [P, DC, S], F32R)
        xt_lo = two(sb, "xt_lo", [P, DC, S], F32R)
        ct_hi = two(sb, "ct_hi", [P, DC, S], F32R)
        ct_lo = two(sb, "ct_lo", [P, DC, S], F32R)
        proj_hi = {n: sb(f"{n}_hi", [P, DC, S], F32R) for n in "qk"}
        proj_lo = {n: sb(f"{n}_lo", [P, DC, S], F32R) for n in "qk"}
        q_stack = two(sb, "q_stack", [P, H, S], F32R)
        k_stack = two(sb, "k_stack", [P, H, S], F32R)
        v_aug = two(sb, "v_aug", [P, ST, H, VW])
        maxima3 = two(sb, "maxima3", [P, 3, H])
        maxima = two(sb, "maxima", [P, ST, H])
        m_neg = [two(sb, f"m_neg{half}", [H // 2, S], F32R) for half in range(2)]
        probs = two(sb, "probs", [P, GH, ST, S])
        heads_t = [sb(f"heads_t{g}", [P, S]) for g in range(G)]
        inv_sum = sb("inv_sum", [P, 16])
        heads = sb("heads", [P, ST, D])
        ot_hi = sb("ot_hi", [P, DC, S], F32R)
        ot_lo = sb("ot_lo", [P, DC, S], F32R)
        y = two(sb, "y", [P, ST, D])
        stats = sb("stats", [P, ST, 6])
        counted = sb("counted", [P, ST])
        mean_var = two(sb, "mean_var", [P, ST, 2])
        var_eps = sb("var_eps", [P, ST])
        rstd = two(sb, "rstd", [P, ST])
        z = two(sb, "z", [P, ST, D])
        x_out = two(sb, "x_out", [P, ST, D])

        def bank(name):
            return stack.enter_context(nc.psum_tensor(name, [P, 512], F32))

        s_bank = [bank("s_bank0"), bank("s_bank1")]
        t_bank = [bank("t_bank0"), bank("t_bank1")]
        av_bank = bank("av_bank")
        misc = [bank("misc0"), bank("misc1"), bank("misc2")]

        ld_w, w_split, w_halved = two(sem, "ld_w"), sem("w_split"), sem("w_halved")
        ld_rows, const_made, zeroed = sem("ld_rows"), sem("const_made"), sem("zeroed")
        pool_chain = sem("pool_chain")
        ld_x, ld_c, ld_r = two(sem, "ld_x"), two(sem, "ld_c"), two(sem, "ld_r")
        bounced = two(sem, "bounced")
        stacked = [two(sem, f"stacked{half}") for half in range(2)]
        m_placed = [two(sem, f"m_placed{half}") for half in range(2)]
        stored = two(sem, "stored")
        pe_xt, pe_ct, pe_q, pe_k, pe_v = sem("pe_xt"), sem("pe_ct"), sem("pe_q"), sem("pe_k"), sem("pe_v")
        pe_s, pe_t, pe_av, pe_mt = sem("pe_s"), sem("pe_t"), sem("pe_av"), sem("pe_mt")
        pe_tr, pe_ot, pe_wo = sem("pe_tr"), sem("pe_ot"), sem("pe_wo")
        act_xt, act_ct, act_q, act_k = sem("act_xt"), sem("act_ct"), sem("act_q"), sem("act_k")
        act_exp, act_av, act_ot = sem("act_exp"), sem("act_av"), sem("act_ot")
        dve_xt, dve_ct, dve_q, dve_k, dve_v = (sem(f"dve_{n}") for n in ("xt", "ct", "q", "k", "v"))
        dve_max, dve_joined, dve_m, dve_inv = sem("dve_max"), sem("dve_joined"), sem("dve_m"), sem("dve_inv")
        dve_tr, dve_ot, dve_y = sem("dve_tr"), sem("dve_ot"), sem("dve_y")
        dve_stats, dve_mean, dve_z = sem("dve_stats"), sem("dve_mean"), sem("dve_z")
        pool_res, pool_eps, pool_rstd = sem("pool_res"), sem("pool_eps"), sem("pool_rstd")
        pool_gain, pool_out = sem("pool_gain"), sem("pool_out")

        w_dram = {"sq": sa[0], "sk": sa[2], "sv": sa[4], "so": sa[6],
                  "cq": ca[0], "ck": ca[2], "cv": ca[4], "co": ca[6]}
        b_dram = {"sq": sa[1], "sk": sa[3], "cq": ca[1], "ck": ca[3]}
        row_dram = {"sv": sa[5], "so": sa[7], "cv": ca[5], "co": ca[7],
                    "g1": ln1[0], "b1": ln1[1], "g2": ln2[0], "b2": ln2[1]}

        def by_head(ap, n):
            return ap.rearrange("p a (g c d) -> p a c g d", c=DC, d=HD) if n[1] in "qk" else ap

        block = stack.enter_context(nc.Block())

        @block.sync
        def _(eng):
            for k, n in enumerate(names):
                wait(eng, w_split, k - 1)
                eng.dma_start(w_in[k % 2][:, :, :], w_dram[n].rearrange("(a p) n -> p a n", p=P)).then_inc(ld_w[k % 2], 16)
                if k == 1:
                    for n2 in qk_bias:
                        for i in range(DC):
                            eng.dma_start(qk_bias[n2][:, i:i + 1],
                                          b_dram[n2].rearrange("(g c d) -> c g d", c=DC, d=HD)[i],
                                          allow_slow_non_contiguous=True).then_inc(ld_rows, 16)
                    for n2 in row:
                        eng.dma_start(row[n2][:, :], row_dram[n2].partition_broadcast(P)).then_inc(ld_rows, 16)
            eng.wait_ge(zeroed, 4)

            def cycle(c):
                load, proj, now, smax, done = (c.item(n) for n in (3, 2, 0, 1, -2))
                j = c.parity
                if now.exists():
                    eng.wait_ge(dve_m, c.count(2, 0, 2))
                    eng.dma_start(q_stack[j][MROW:P, H // 2:H, :].bitcast(F32),
                                  m_neg[1][j][:, :].bitcast(F32)).then_inc(m_placed[1][j], 16)
                if load.exists():
                    if load.cross:
                        wait(eng, pe_ct, c.count(1, 1 - B, 1))
                        eng.dma_start(c_in[load.parity][:, :, :],
                                      ctxt[load.batch].rearrange("(t p) d -> p t d", p=P)).then_inc(ld_c[load.parity], 16)
                        if c.i is None:
                            wait(eng, pe_xt, c.count(1, 1, 1))
                        eng.wait_ge(stored[load.parity], load.of_cross(16, 16))
                        eng.dma_start(x_in[load.parity][:, :, :], x1[load.batch]).then_inc(ld_x[load.parity], 16)
                    else:
                        wait(eng, pe_xt, c.count(1, 1, 1))
                        eng.dma_start(x_in[load.parity][:, :, :],
                                      x[load.batch].rearrange("(t p) d -> p t d", p=P)).then_inc(ld_x[load.parity], 16)
                if now.exists():
                    wait(eng, dve_y, c.count(1, -2, 1))
                    eng.dma_start(x_res[j][:, :, :], x1[now.batch] if now.cross else
                                  x[now.batch].rearrange("(t p) d -> p t d", p=P)).then_inc(ld_r[j], 16)
                if proj.exists():
                    for n, (q, ready) in enumerate((("q", dve_q), ("k", dve_k))):
                        eng.wait_ge(ready, c.count(1, 2, 1))
                        for part, src in enumerate((proj_hi, proj_lo)):
                            if n and part:
                                wait(eng, pe_t, c.count(H, 0, H // 2))
                            eng.dma_start(bounce[j, n, part].rearrange("d (g t) -> g d t", g=HC),
                                          src[q][:, :, :].rearrange("p c t -> p (c t)").bitcast(F32)).then_inc(bounced[j], 16)
                    eng.wait_ge(bounced[j], proj.of_parity(64, 64))
                for half in range(2):
                    if half == 1:
                        if smax.exists():
                            eng.wait_ge(dve_m, c.count(2, 1, 1))
                            eng.dma_start(q_stack[1 - j][MROW:P, 0:H // 2, :].bitcast(F32),
                                          m_neg[0][1 - j][:, :].bitcast(F32)).then_inc(m_placed[0][1 - j], 16)
                        if done.exists():
                            eng.wait_ge(pool_out, c.count(1, -2, 1))
                            eng.dma_start(out[done.batch] if done.cross else x1[done.batch],
                                          x_out[j][:, :, :]).then_inc(stored[j], 16)
                    if proj.exists():
                        if half == 1:
                            wait(eng, pe_t, c.count(H, 0, H))
                        hs = slice(half * H // 2, (half + 1) * H // 2)
                        for n, (dst, parts) in enumerate(((q_stack[j], ((0, 1, 1), (HD, 0, 1), (2 * HD, 0, 1))),
                                                          (k_stack[j], ((0, 0, 1), (HD, 0, 2))))):
                            for at, part, m in parts:
                                eng.dma_start(dst[at:at + m * HD, hs, :].rearrange("p h t -> p (h t)").bitcast(F32),
                                              bounce[j, n, part:part + m, :, half * (H // 2) * S:(half + 1) * (H // 2) * S]
                                              .rearrange("a d t -> (a d) t")).then_inc(stacked[half][j], 16)

            run_cycles(eng, cycle)
            for k in range(2):
                eng.wait_ge(stored[k], ITEMS // 2 * 16)

        @block.gpsimd
        def _(eng):
            g = nc.gpsimd
            g.memset(ident[:, :], 0.0).then_inc(pool_chain, 1)
            g.memset(mask_qk[:, :], 0.0).then_inc(pool_chain, 1)
            g.memset(mask_kq[:, :], 0.0).then_inc(pool_chain, 1)
            g.memset(eps[:, :], EPS).then_inc(const_made, 1)
            g.memset(minus_half[:, :], -0.5).then_inc(const_made, 1)
            eng.wait_ge(pool_chain, 3)
            g.affine_select(out=ident[:, :], in_=ident[:, :], compare_op=ALU.not_equal, fill=1.0, base=0,
                            pattern=[[-1, P]], channel_multiplier=1).then_inc(pool_chain, 1)
            g.affine_select(out=mask_qk[:, :], in_=mask_qk[:, :], compare_op=ALU.is_ge, fill=MASKED, base=0,
                            pattern=[[-1, P]], channel_multiplier=1).then_inc(const_made, 1)
            g.affine_select(out=mask_kq[:, :], in_=mask_kq[:, :], compare_op=ALU.is_ge, fill=MASKED, base=0,
                            pattern=[[1, P]], channel_multiplier=-1).then_inc(const_made, 1)
            eng.wait_ge(pool_chain, 4)
            g.tensor_copy(ident_bf[:, :], ident[:, :]).then_inc(const_made, 1)
            eng.wait_ge(const_made, 5)
            eng.wait_ge(ld_rows, 16 * 16)

            def cycle(c):
                now, fin, done = c.item(0), c.item(-1), c.item(-2)
                j = c.parity
                if now.exists():
                    eng.wait_ge(ld_r[j], now.of_parity(16, 16))
                    bo = row["co" if now.cross else "so"]
                    for t in range(ST):
                        last = g.tensor_tensor(x_res[j][:, t, :], x_res[j][:, t, :], bo[:, :], ALU.add)
                    last.then_inc(pool_res, 1)
                if done.exists():
                    k = "2" if done.cross else "1"
                    eng.wait_ge(dve_z, c.count(1, -2, 1))
                    for t in range(ST):
                        last = g.tensor_tensor(z[j][:, t, :], z[j][:, t, :], row["g" + k][:, :], ALU.mult)
                    last.then_inc(pool_gain, 1)
                    eng.wait_ge(pool_gain, c.count(1, -2, 1))
                    if not (done.is_number(0) or done.is_number(1)):
                        eng.wait_ge(stored[j], done.of_parity(16))
                    for t in range(ST):
                        last = g.tensor_tensor(x_out[j][:, t, :], z[j][:, t, :], row["b" + k][:, :], ALU.add)
                    last.then_inc(pool_out, 1)
                if fin.exists():
                    k = 1 - j
                    eng.wait_ge(dve_mean, c.count(1, -1, 1))
                    g.tensor_tensor(var_eps[:, :], mean_var[k][:, :, 1], eps[:, :], ALU.add).then_inc(pool_eps, 1)
                    eng.wait_ge(pool_eps, c.count(1, -1, 1))
                    g.tensor_tensor(rstd[k][:, :], var_eps[:, :], minus_half[:, :], ALU.pow).then_inc(pool_rstd, 1)

            run_cycles(eng, cycle)

        @block.scalar
        def _(eng):
            a = nc.scalar
            for k, n in enumerate(names):
                eng.wait_ge(ld_w[k % 2], 16 * (k // 2 + 1))
                for i in range(DC):
                    last = a.activation(w_hi[n][:, i:i + 1, :].rearrange("p a (c g d) -> p a c g d", c=DC, d=HD)[:, 0]
                                        if n[1] in "qk" else w_hi[n][:, i, :],
                                        by_head(w_in[k % 2][:, i:i + 1, :], n)[:, 0] if n[1] in "qk" else w_in[k % 2][:, i, :],
                                        ACT.Copy)
                last.then_inc(w_halved, 1)
            eng.wait_ge(ld_rows, 16 * 16)

            def cycle(c):
                proj, now, fin = c.item(2), c.item(0), c.item(-1)
                j = c.parity
                p = proj.parity
                for g in range(G):
                    if now.exists():
                        cols = S + P if not now.cross else 2 * S
                        for h in range(GH * g, GH * g + GH):
                            if h % GH == 0:
                                wait(eng, pe_av, c.count(G, 0, g - 1))
                            eng.wait_ge(pe_t, c.count(H, 0, h + 1))
                            pr = probs[g % 2][:, h % GH].rearrange("p a s -> p (a s)")
                            a.activation(pr[:, 0:cols], t_bank[h % 2][:, 0:cols], ACT.Exp, scale=SCALE).then_inc(act_exp, 1)
                    src, k = (fin, G - 1) if g == 0 else (now, g - 1)
                    if src.exists():
                        n = -1 if g == 0 else 0
                        eng.wait_ge(pe_av, c.count(G, n, k + 1))
                        wait(eng, pe_tr, c.count(2, n - 1, 1 + k // 2))
                        a.activation(heads_t[k][:, :], av_bank[:, 0:S], ACT.Copy).then_inc(act_av, 1)
                    if g == 0 and proj.exists():
                        eng.wait_ge(pe_xt, c.count(1, 2, 1))
                        wait(eng, pe_v, c.count(1, 0, 1))
                        a.activation(xt_hi[p][:, :, :], misc[1][:, :].rearrange("p (c t) -> p c t", c=DC), ACT.Copy).then_inc(act_xt, 1)
                        if proj.cross:
                            eng.wait_ge(pe_ct, c.count(1, 2 - B, 1))
                            a.activation(ct_hi[p][:, :, :], misc[2][:, :].rearrange("p (c t) -> p c t", c=DC), ACT.Copy).then_inc(act_ct, 1)
                    if g == 1 and proj.exists():
                        w = "c" if proj.cross else "s"
                        if not proj.is_number(0):
                            prev = c.item(1)
                            eng.wait_ge(bounced[prev.parity], prev.of_parity(64, 64))
                        for q, bk, ready, done in (("q", 1, pe_q, act_q), ("k", 2, pe_k, act_k)):
                            eng.wait_ge(ready, c.count(1, 2, 1))
                            for i in range(DC):
                                last = a.activation(proj_hi[q][:, i, :], misc[bk][:, i * S:(i + 1) * S], ACT.Identity,
                                                    bias=qk_bias[w + q][:, i:i + 1])
                            last.then_inc(done, 1)
                    if g == 2 and fin.exists():
                        eng.wait_ge(pe_ot, c.count(1, -1, 1))
                        wait(eng, pe_wo, c.count(1, -2, 1))
                        a.activation(ot_hi[:, :, :], misc[1][:, :].rearrange("p (c t) -> p c t", c=DC), ACT.Copy).then_inc(act_ot, 1)

            run_cycles(eng, cycle)

        @block.vector
        def _(eng):
            v = nc.vector
            for k in range(2):
                v.memset(q_stack[k][:, :, :].bitcast(F32), 0.0).then_inc(zeroed, 1)
                v.memset(v_aug[k][:, :, :, :], 1.0)
                v.memset(k_stack[k][96:P, :, :].bitcast(F32), 1.0).then_inc(dve_inv, 1)
            eng.wait_ge(dve_inv, 2)
            for k in range(2):
                v.memset(k_stack[k][0:96, :, :].bitcast(F32), 0.0)
                v.memset(k_stack[k][96:MROW, :, :].bitcast(F32), 0.0).then_inc(zeroed, 1)
            for k, n in enumerate(names):
                eng.wait_ge(w_halved, k + 1)
                for i in range(DC):
                    hi = w_hi[n][:, i:i + 1, :].bitcast(F32)
                    lo = w_lo[n][:, i:i + 1, :]
                    src = w_in[k % 2][:, i:i + 1, :]
                    if n[1] in "qk":
                        hi = hi.rearrange("p a (c g d) -> p a c g d", c=DC, d=HD)[:, 0]
                        lo = lo.rearrange("p a (c g d) -> p a c g d", c=DC, d=HD)[:, 0]
                        src = by_head(src, n)[:, 0]
                    last = v.tensor_tensor(lo, src, hi, ALU.subtract)
                last.then_inc(w_split, 1)
            eng.wait_ge(ld_rows, 16 * 16)

            def cycle(c):
                proj, smax, now, fin, done = (c.item(n) for n in (2, 1, 0, -1, -2))
                j = c.parity
                p, s = proj.parity, smax.parity

                def minus_max(half, n, par):
                    eng.wait_ge(pe_mt, c.count(2, n, 1 + half))
                    it = c.item(n)
                    if not (it.is_number(0) or it.is_number(1)):
                        eng.wait_ge(m_placed[half][par], it.of_parity(16))
                    v.tensor_scalar(m_neg[half][par][:, :], misc[0][0:H // 2, 0:S], -1.0, None, ALU.mult).then_inc(dve_m, 1)

                def divide(n, pair):
                    eng.wait_ge(pe_tr, c.count(2, n, pair + 1))
                    got = misc[0][:, :].rearrange("p (k w) -> p k w", w=VW)
                    v.reciprocal(inv_sum[:, :], got[:, :, HD]).then_inc(dve_inv, 1)
                    eng.wait_ge(dve_inv, c.count(2, n, 2 + pair + 1) if c.i is not None else 2 + c.count(2, n, pair + 1))
                    wait(eng, pe_ot, c.count(1, n, 0))
                    for t in range(ST):
                        last = v.tensor_tensor(
                            heads[:, t, pair * P:(pair + 1) * P].rearrange("p (k d) -> p k d", d=HD),
                            got[:, 8 * t:8 * t + 8, 0:HD],
                            inv_sum[:, 8 * t:8 * t + 8].unsqueeze(2).to_broadcast([P, 8, HD]), ALU.mult)
                    last.then_inc(dve_tr, 1)

                for g in range(G):
                    if smax.exists():
                        for h in range(GH * g, GH * g + GH):
                            eng.wait_ge(pe_s, c.count(H, 1, h + 1))
                            if smax.cross:
                                v.tensor_reduce(maxima[s][:, :, h], s_bank[h % 2][:, :].rearrange("p (q k) -> p q k", q=ST),
                                                axis=AX.X, op=ALU.max).then_inc(dve_max, 1)
                            else:
                                v.tensor_reduce(maxima3[s][:, :, h], s_bank[h % 2][:, 0:3 * P].rearrange("p (q k) -> p q k", q=3),
                                                axis=AX.X, op=ALU.max).then_inc(dve_max, 1)
                        if g % 2 == 1 and not smax.cross:
                            hs = slice(H // 2 * (g // 2), H // 2 * (g // 2 + 1))
                            eng.wait_ge(dve_max, c.count(H, 1, GH * g + GH))
                            v.tensor_copy(maxima[s][:, 0, hs], maxima3[s][:, 0, hs])
                            v.tensor_tensor(maxima[s][:, 1, hs], maxima3[s][:, 1, hs], maxima3[s][:, 2, hs],
                                            ALU.max).then_inc(dve_joined, 1)
                    if g == 0:
                        if now.exists():
                            minus_max(1, 0, j)
                        if proj.exists():
                            eng.wait_ge(act_xt, c.count(1, 2, 1))
                            wait(eng, pe_v, c.count(1, 0, 1))
                            v.tensor_tensor(xt_lo[p][:, :, :], misc[1][:, :].rearrange("p (c t) -> p c t", c=DC),
                                            xt_hi[p][:, :, :].bitcast(F32), ALU.subtract).then_inc(dve_xt, 1)
                            if proj.cross:
                                eng.wait_ge(act_ct, c.count(1, 2 - B, 1))
                                v.tensor_tensor(ct_lo[p][:, :, :], misc[2][:, :].rearrange("p (c t) -> p c t", c=DC),
                                                ct_hi[p][:, :, :].bitcast(F32), ALU.subtract).then_inc(dve_ct, 1)
                        if done.exists():
                            eng.wait_ge(pool_rstd, c.count(1, -2, 1))
                            for t in range(ST):
                                last = v.tensor_scalar(z[j][:, t, :], y[j][:, t, :], mean_var[j][:, t, 0:1], rstd[j][:, t:t + 1],
                                                       ALU.subtract, ALU.mult)
                            last.then_inc(dve_z, 1)
                    if g == 1:
                        if fin.exists():
                            divide(-1, 1)
                        if proj.exists():
                            w = "c" if proj.cross else "s"
                            if not proj.is_number(0):
                                prev = c.item(1)
                                eng.wait_ge(bounced[prev.parity], prev.of_parity(64, 64))
                            for q, bk, ready, fine in (("q", 1, act_q, dve_q), ("k", 2, act_k, dve_k)):
                                eng.wait_ge(ready, c.count(1, 2, 1))
                                for i in range(DC):
                                    last = v.scalar_tensor_tensor(
                                        out=proj_lo[q][:, i, :], in0=misc[bk][:, i * S:(i + 1) * S],
                                        scalar=qk_bias[w + q][:, i:i + 1], in1=proj_hi[q][:, i, :].bitcast(F32),
                                        op0=ALU.add, op1=ALU.subtract)
                                last.then_inc(fine, 1)
                    if g == 2:
                        if smax.exists():
                            minus_max(0, 1, s)
                        if fin.exists():
                            eng.wait_ge(act_ot, c.count(1, -1, 1))
                            wait(eng, pe_wo, c.count(1, -2, 1))
                            v.tensor_tensor(ot_lo[:, :, :], misc[1][:, :].rearrange("p (c t) -> p c t", c=DC),
                                            ot_hi[:, :, :].bitcast(F32), ALU.subtract).then_inc(dve_ot, 1)
                        if smax.exists():
                            bv = row["cv" if smax.cross else "sv"]
                            eng.wait_ge(pe_v, c.count(1, 1, 1))
                            wait(eng, pe_av, c.count(G, 0, 0))
                            for t in range(ST):
                                last = v.tensor_tensor(v_aug[s][:, t, :, 0:HD],
                                                       misc[2][:, t * D:(t + 1) * D].rearrange("p (h d) -> p h d", d=HD),
                                                       bv[:, :].rearrange("p (h d) -> p h d", d=HD), ALU.add)
                            last.then_inc(dve_v, 1)
                    if g == 3:
                        if now.exists():
                            divide(0, 0)
                        if fin.exists():
                            k = 1 - j
                            eng.wait_ge(pe_wo, c.count(1, -1, 1))
                            eng.wait_ge(pool_res, c.count(1, -1, 1))
                            v.tensor_tensor(y[k][:, :, :], misc[1][:, :].rearrange("p (t d) -> p t d", t=ST),
                                            x_res[k][:, :, :], ALU.add).then_inc(dve_y, 1)
                            eng.wait_ge(dve_y, c.count(1, -1, 1))
                            for t in range(ST):
                                last = v.bn_stats(stats[:, t, :], y[k][:, t, :])
                            last.then_inc(dve_stats, 1)
                            eng.wait_ge(dve_stats, c.count(1, -1, 1))
                            v.tensor_copy(counted[:, :], stats[:, :, 0])
                            for t in range(ST):
                                last = v.bn_aggr(mean_var[k][:, t, :], stats[:, t, :])
                            last.then_inc(dve_mean, 1)

            run_cycles(eng, cycle)

        @block.tensor
        def _(eng):
            pe = nc.tensor
            eng.wait_ge(const_made, 5)
            eng.wait_ge(w_split, len(names))

            def split_product(dst, left_hi, left_lo, right_hi, right_lo):
                for i in range(DC):
                    for n, (l, r) in enumerate(((left_hi, right_hi), (left_hi, right_lo), (left_lo, right_hi))):
                        last = pe.matmul(dst, l(i), r(i), start=(i == 0 and n == 0), stop=(i == DC - 1 and n == 2))
                return last

            def cycle(c):
                proj, smax, now, fin = (c.item(n) for n in (2, 1, 0, -1))
                j = c.parity
                p, s = proj.parity, smax.parity

                def values(n, g):
                    it = c.item(n)
                    k = it.parity
                    eng.wait_ge(act_exp, c.count(H, n, GH * (g + 1)))
                    wait(eng, act_av, c.count(G, n, g))
                    if g == 0:
                        eng.wait_ge(dve_v, c.count(1, n, 1))
                    for t in range(ST):
                        q0 = P * t if not it.cross else 0
                        for hh in range(GH):
                            last = pe.matmul(av_bank[VW * hh:VW * hh + VW, q0:S], v_aug[k][:, t, GH * g + hh, :],
                                             probs[g % 2][:, hh, t, 0:S - q0] if t else probs[g % 2][:, hh, t, :],
                                             start=(t == 0), stop=(t == ST - 1), tile_position=(0, VW * hh))
                    last.then_inc(pe_av, 1)

                def max_rows(n, half, free, count):
                    it = c.item(n)
                    eng.wait_ge(dve_max, c.count(H, n, H // 2 * (half + 1)))
                    if not it.cross:
                        eng.wait_ge(dve_joined, c.count(2, n, half + 1))
                    wait(eng, free, count)
                    for t in range(ST):
                        last = pe.transpose(misc[0][0:H // 2, t * P:(t + 1) * P],
                                            maxima[it.parity][:, t, half * H // 2:(half + 1) * H // 2], ident[:, :])
                    last.then_inc(pe_mt, 1)

                def head_rows(n, pair, count):
                    eng.wait_ge(act_av, c.count(G, n, 2 * pair + 2))
                    wait(eng, dve_m, count)
                    wait(eng, dve_tr, c.count(2, n, pair))
                    for t in range(ST):
                        for gi in range(2):
                            last = pe.transpose(misc[0][:, (2 * t + gi) * P:(2 * t + gi + 1) * P],
                                                heads_t[2 * pair + gi][:, t * P:(t + 1) * P], ident[:, :])
                    last.then_inc(pe_tr, 1)

                for g in range(G):
                    for h in range(GH * g, GH * g + GH):
                        if smax.exists():
                            if h % (H // 2) == 0:
                                eng.wait_ge(stacked[h // (H // 2)][s], smax.of_parity(80, 80))
                            wait(eng, dve_max, c.count(H, 1, h - 1))
                            qs, ks, sbk = q_stack[s], k_stack[s], s_bank[h % 2]
                            if smax.cross:
                                for t in range(ST):
                                    last = pe.matmul(sbk[:, t * S:(t + 1) * S], qs[0:MROW, h, t * P:(t + 1) * P],
                                                     ks[0:MROW, h, :], start=True, stop=True)
                            else:
                                pe.matmul(sbk[:, 0:P], qs[0:MROW, h, 0:P], ks[0:MROW, h, 0:P], start=True, stop=False)
                                pe.matmul(sbk[:, 0:P], ident_bf[:, :], mask_qk[:, :], start=False, stop=True)
                                pe.matmul(sbk[:, P:3 * P], qs[0:MROW, h, P:S], ks[0:MROW, h, :], start=True, stop=False)
                                last = pe.matmul(sbk[:, 2 * P:3 * P], ident_bf[:, :], mask_qk[:, :], start=False, stop=True)
                            last.then_inc(pe_s, 1)
                        if now.exists():
                            if h % (H // 2) == 0:
                                eng.wait_ge(m_placed[h // (H // 2)][j], now.of_parity(16, 16))
                            wait(eng, act_exp, c.count(H, 0, h - 1))
                            qs, ks, tbk = q_stack[j], k_stack[j], t_bank[h % 2]
                            if now.cross:
                                for t in range(ST):
                                    last = pe.matmul(tbk[:, t * S:(t + 1) * S], ks[:, h, t * P:(t + 1) * P], qs[:, h, :],
                                                     start=True, stop=True)
                            else:
                                pe.matmul(tbk[:, 0:S], ks[:, h, 0:P], qs[:, h, :], start=True, stop=False)
                                pe.matmul(tbk[:, 0:P], ident_bf[:, :], mask_kq[:, :], start=False, stop=True)
                                pe.matmul(tbk[:, S:S + P], ks[:, h, P:S], qs[:, h, P:S], start=True, stop=False)
                                last = pe.matmul(tbk[:, S:S + P], ident_bf[:, :], mask_kq[:, :], start=False, stop=True)
                            last.then_inc(pe_t, 1)
                    if g == 0:
                        if fin.exists():
                            values(-1, G - 1)
                        if now.exists():
                            max_rows(0, 1, dve_tr, c.count(2, -1, 1))
                        if proj.exists():
                            eng.wait_ge(ld_x[p], proj.of_parity(16, 16))
                            wait(eng, dve_y, c.count(1, -2, 1))
                            for i in range(DC):
                                for t in range(ST):
                                    last = pe.transpose(misc[1][:, i * S + t * P:i * S + (t + 1) * P],
                                                        x_in[p][:, t, i * P:(i + 1) * P], ident[:, :])
                            last.then_inc(pe_xt, 1)
                            if proj.cross:
                                eng.wait_ge(ld_c[p], proj.of_cross(16, 16))
                                wait(eng, dve_v, c.count(1, 0, 1))
                                for i in range(DC):
                                    for t in range(ST):
                                        last = pe.transpose(misc[2][:, i * S + t * P:i * S + (t + 1) * P],
                                                            c_in[p][:, t, i * P:(i + 1) * P], ident[:, :])
                                last.then_inc(pe_ct, 1)
                    if g == 1:
                        if now.exists():
                            values(0, 0)
                        if fin.exists():
                            head_rows(-1, 1, c.count(2, 0, 2))
                        if proj.exists():
                            w = "c" if proj.cross else "s"
                            kv_hi, kv_lo = (ct_hi[p], ct_lo[p]) if proj.cross else (xt_hi[p], xt_lo[p])
                            eng.wait_ge(dve_xt, c.count(1, 2, 1))
                            for i in range(DC):
                                last = split_product(
                                    misc[1][:, i * S:(i + 1) * S],
                                    lambda a: w_hi[w + "q"][:, a, i * P:(i + 1) * P], lambda a: w_lo[w + "q"][:, a, i * P:(i + 1) * P],
                                    lambda a: xt_hi[p][:, a, :], lambda a: xt_lo[p][:, a, :])
                            last.then_inc(pe_q, 1)
                            if proj.cross:
                                eng.wait_ge(dve_ct, c.count(1, 2 - B, 1))
                            wait(eng, dve_v, c.count(1, 0, 1))
                            for i in range(DC):
                                last = split_product(
                                    misc[2][:, i * S:(i + 1) * S],
                                    lambda a: w_hi[w + "k"][:, a, i * P:(i + 1) * P], lambda a: w_lo[w + "k"][:, a, i * P:(i + 1) * P],
                                    lambda a: kv_hi[:, a, :], lambda a: kv_lo[:, a, :])
                            last.then_inc(pe_k, 1)
                    if g == 2:
                        if now.exists():
                            values(0, 1)
                        if smax.exists():
                            max_rows(1, 0, dve_tr, c.count(2, -1, 2))
                        if fin.exists():
                            eng.wait_ge(dve_tr, c.count(2, -1, 2))
                            wait(eng, dve_q, c.count(1, 2, 1))
                            wait(eng, dve_y, c.count(1, -2, 1))
                            for i in range(DC):
                                for t in range(ST):
                                    last = pe.transpose(misc[1][:, i * S + t * P:i * S + (t + 1) * P],
                                                        heads[:, t, i * P:(i + 1) * P], ident[:, :])
                            last.then_inc(pe_ot, 1)
                        if smax.exists():
                            w = "c" if smax.cross else "s"
                            kv_hi, kv_lo = (ct_hi[s], ct_lo[s]) if smax.cross else (xt_hi[s], xt_lo[s])
                            wait(eng, dve_k, c.count(1, 2, 1))
                            wait(eng, dve_v, c.count(1, 0, 1))
                            for t in range(ST):
                                last = split_product(
                                    misc[2][:, t * D:(t + 1) * D],
                                    lambda a: kv_hi[:, a, t * P:(t + 1) * P], lambda a: kv_lo[:, a, t * P:(t + 1) * P],
                                    lambda a: w_hi[w + "v"][:, a, :], lambda a: w_lo[w + "v"][:, a, :])
                            last.then_inc(pe_v, 1)
                    if g == 3:
                        if now.exists():
                            values(0, 2)
                            head_rows(0, 0, c.count(2, 1, 1))
                        if fin.exists():
                            w = "c" if fin.cross else "s"
                            eng.wait_ge(dve_ot, c.count(1, -1, 1))
                            for t in range(ST):
                                last = split_product(
                                    misc[1][:, t * D:(t + 1) * D],
                                    lambda a: ot_hi[:, a, t * P:(t + 1) * P], lambda a: ot_lo[:, a, t * P:(t + 1) * P],
                                    lambda a: w_hi[w + "o"][:, a, :], lambda a: w_lo[w + "o"][:, a, :])
                            last.then_inc(pe_wo, 1)

            run_cycles(eng, cycle)


E, FF, K = 8, 1024, 2
T = B * S
NT = T // P
BLK = 512
BT = BLK // P
FJ = FF // P
NBLK = (T * K + E * (BLK - 1)) // BLK
LOGB = BLK.bit_length() - 1
LAG = 2
WCOLS = DC * FF + FJ * D


def moe_program(nc, x2, rw, rb, w1, b1, w2, b2, g3, b3, out):
    sorted_x = nc.dram_tensor("sorted_x", (NBLK * BLK, D), F32, kind="Internal").ap()
    sorted_y = nc.dram_tensor("sorted_y", (NBLK * BLK, D), F32, kind="Internal").ap()
    b1_cols = nc.dram_tensor("b1_cols", (P, E, FJ), F32, kind="Internal").ap()
    outer = ExitStack()
    with outer:
        def keep(name, shape, dt=F32):
            return outer.enter_context(nc.sbuf_tensor(name, shape, dt))
        x2_sb = keep("x2_sb", [P, NT, D])
        slot = [keep(f"slot{k}", [P, NT], I32) for k in range(K)]
        weight = [keep(f"weight{k}", [P, NT]) for k in range(K)]
        expert_of = keep("expert_of", [1, NBLK], I32)
        ident = keep("ident_m", [P, P])
        route(nc, x2, rw, rb, b1, x2_sb, slot, weight, expert_of, ident, sorted_x, b1_cols)
        experts(nc, w1, w2, b2, expert_of, ident, sorted_x, sorted_y, b1_cols)
        combine(nc, x2_sb, slot, weight, sorted_y, g3, b3, out)


def route(nc, x2, rw, rb, b1, x2_sb, slot, weight, expert_of, ident, sorted_x, b1_cols):
    stack = ExitStack()
    with stack:
        def sb(name, shape, dt=F32):
            return stack.enter_context(nc.sbuf_tensor(name, shape, dt))

        def sem(name):
            return stack.enter_context(nc.semaphore(name))

        GT = 4
        NG = NT // GT
        rw_sb = sb("rw_sb", [P, DC, E])
        rb_sb = sb("rb_sb", [E, 1])
        b1_rows = sb("b1_rows", [E * FJ, P])
        b1_turned = sb("b1_turned", [P, E * FJ])
        zero_rows = sb("zero_rows", [P, 8 * D])
        x2t = [sb(f"x2t{k}", [P, DC, GT * P]) for k in range(2)]
        logits_t = [sb(f"logits_t{k}", [E, GT * P]) for k in range(2)]
        lg = sb("lg", [P, NT, E])
        prob = sb("prob", [P, NT, E])
        rest = sb("rest", [P, NT, E])
        top = [sb(f"top{k}", [P, NT]) for k in range(K)]
        pick = [sb(f"pick{k}", [P, NT]) for k in range(K)]
        chosen = [sb(f"chosen{k}", [P, NT, E]) for k in range(K)]
        both = sb("both", [P, NT, E], BF16)
        score = sb("score", [P, NT, E])
        rank_w = sb("rank_w", [P, E])
        mx = sb("mx", [P, NT])
        sm = sb("sm", [P, NT])
        scan = [sb(f"scan{k}", [P, NT, E]) for k in range(2)]
        totals = sb("totals", [P, NT, E])
        place = sb("place", [P, NT, E])
        cap = sb("cap", [P, E])
        cap_i = sb("cap_i", [P, E], I32)
        ends = [sb(f"ends{k}", [P, E]) for k in range(2)]
        starts = sb("starts", [P, E])
        slot_f = [sb(f"slot_f{k}", [P, NT]) for k in range(K)]
        tri = sb("tri", [P, P], BF16)
        tri_f = sb("tri_f", [P, P])
        ones = sb("ones", [P, P], BF16)
        blk_at = sb("blk_at", [1, NBLK, E])
        past = sb("past", [1, NBLK, E])
        count_f = sb("count_f", [1, NBLK])

        def bank(name):
            return stack.enter_context(nc.psum_tensor(name, [P, 512], F32))
        xt_bank = [[bank(f"xt_bank{k}{c}") for c in range(DC)] for k in range(2)]
        lt_bank, lg_bank = bank("lt_bank"), bank("lg_bank")
        prefix_bank, total_bank = bank("prefix_bank"), bank("total_bank")

        ld, ldx, const, zero_made, zeroed = sem("r_ld"), sem("r_ldx"), sem("r_const"), sem("r_zero"), sem("r_zeroed")
        chain_p = sem("r_chain_p")
        xt_done, xt_out, lt_done, lt_out, lg_done, lg_out = (sem(f"r_{n}") for n in ("xt", "xto", "lt", "lto", "lg", "lgo"))
        centred, exped, both_done, counted, slots_done = (sem(f"r_{n}") for n in ("cen", "exp", "both", "cnt", "slot"))
        gap_c, gap_e = sem("r_gap_c"), sem("r_gap_e")
        scattered, b1t_done, b1t_out, b1_stored = sem("r_scat"), sem("r_b1t"), sem("r_b1o"), sem("r_b1s")
        dv = sem("r_dv")

        block = stack.enter_context(nc.Block())

        @block.sync
        def _(eng):
            for q in range(4):
                eng.dma_start(x2_sb[:, q * NT // 4:(q + 1) * NT // 4, :].rearrange("p (b t) d -> p b t d", t=ST),
                              x2[q * B // 4:(q + 1) * B // 4].rearrange("b p t d -> p b t d")).then_inc(ldx, 16)
            eng.dma_start(rw_sb[:, :, :], rw.rearrange("(c p) e -> p c e", p=P)).then_inc(ld, 16)
            eng.dma_start(rb_sb[:, :], rb.rearrange("(e a) -> e a", a=1), allow_slow_non_contiguous=True).then_inc(ld, 16)
            eng.dma_start(b1_rows[:, :], b1.rearrange("e (j p) -> (e j) p", p=P)).then_inc(ld, 16)
            eng.wait_ge(zero_made, 1)
            rows = NBLK * BLK
            per = 8 * P
            for r in range(0, rows, per):
                n = min(per, rows - r) // P
                eng.dma_start(sorted_x[r:r + n * P, :].rearrange("(p n) d -> p n d", n=n),
                              zero_rows[:, 0:n * D].rearrange("p (n d) -> p n d", n=n)).then_inc(zeroed, 16)
            eng.wait_ge(b1t_out, 1)
            eng.dma_start(b1_cols.rearrange("p e j -> p (e j)"), b1_turned[:, :]).then_inc(b1_stored, 16)
            eng.wait_ge(b1_stored, 16)

        @block.gpsimd
        def _(eng):
            g = nc.gpsimd
            g.memset(ident[:, :], 0.0).then_inc(chain_p, 1)
            g.memset(tri_f[:, :], 0.0).then_inc(chain_p, 1)
            g.memset(ones[:, :], 1.0).then_inc(const, 1)
            g.iota(blk_at[:, :, :], [[BLK, NBLK], [0, E]], base=0, channel_multiplier=0,
                   allow_small_or_imprecise_dtypes=True).then_inc(const, 1)
            g.iota(rank_w[:, :], [[-1, E]], base=E, channel_multiplier=0,
                   allow_small_or_imprecise_dtypes=True).then_inc(const, 1)
            eng.wait_ge(chain_p, 2)
            g.affine_select(out=ident[:, :], in_=ident[:, :], compare_op=ALU.not_equal, fill=1.0, base=0,
                            pattern=[[-1, P]], channel_multiplier=1).then_inc(const, 1)
            g.affine_select(out=tri_f[:, :], in_=tri_f[:, :], compare_op=ALU.is_ge, fill=1.0, base=0,
                            pattern=[[-1, P]], channel_multiplier=1).then_inc(chain_p, 1)
            eng.wait_ge(chain_p, 3)
            g.tensor_copy(tri[:, :], tri_f[:, :]).then_inc(const, 1)
            n_zero = -(-NBLK * BLK // (8 * P))
            eng.wait_ge(slots_done, 1)
            eng.wait_ge(zeroed, 16 * n_zero)
            for i in range(NT):
                for k in range(K):
                    g.indirect_dma_start(sorted_x, bass.IndirectOffsetOnAxis(ap=slot[k][:, i:i + 1], axis=0),
                                         x2_sb[:, i, :], None, bounds_check=NBLK * BLK - 1).then_inc(scattered, 16)
            eng.wait_ge(scattered, 16 * NT * K)

        @block.scalar
        def _(eng):
            a = nc.scalar
            for q in range(NG):
                eng.wait_ge(xt_done, q + 1)
                for c in range(DC):
                    last = a.activation(x2t[q % 2][:, c, :], xt_bank[q % 2][c][:, :], ACT.Copy)
                last.then_inc(xt_out, 1)
            eng.wait_ge(b1t_done, 1)
            a.activation(b1_turned[:, :], lt_bank[:, 0:E * FJ], ACT.Copy).then_inc(b1t_out, 1)
            eng.wait_ge(centred, 1)
            a.activation(prob[:, :, :], prob[:, :, :], ACT.Exp).then_inc(exped, 1)
            eng.wait_ge(gap_c, 1)
            a.activation(weight[1][:, :], weight[1][:, :], ACT.Exp).then_inc(gap_e, 1)

        @block.tensor
        def _(eng):
            pe = nc.tensor
            eng.wait_ge(const, 5)
            eng.wait_ge(ld, 48)
            eng.wait_ge(ldx, 64)
            for q in range(NG):
                wait(eng, xt_out, q - 1)
                for c in range(DC):
                    for i in range(GT):
                        last = pe.transpose(xt_bank[q % 2][c][:, i * P:(i + 1) * P],
                                            x2_sb[:, q * GT + i, c * P:(c + 1) * P], ident[:, :])
                last.then_inc(xt_done, 1)
                for r in ([q - 1] if q else []) + ([q] if q == NG - 1 else []):
                    eng.wait_ge(xt_out, r + 1)
                    wait(eng, lt_out, r)
                    for c in range(DC):
                        last = pe.matmul(lt_bank[0:E, :], rw_sb[:, c, :], x2t[r % 2][:, c, :],
                                         start=(c == 0), stop=(c == DC - 1))
                    last.then_inc(lt_done, 1)
                    eng.wait_ge(lt_out, r + 1)
                    for i in range(GT):
                        last = pe.transpose(lg_bank[:, (r * GT + i) * E:(r * GT + i + 1) * E],
                                            logits_t[r % 2][:, i * P:(i + 1) * P], ident[0:E, 0:E])
                    last.then_inc(lg_done, 1)
            pe.transpose(lt_bank[:, 0:E * FJ], b1_rows[:, :], ident[0:E * FJ, 0:E * FJ]).then_inc(b1t_done, 1)
            eng.wait_ge(both_done, 1)
            every = both[:, :, :].rearrange("p n e -> p (n e)")
            pe.matmul(prefix_bank[:, 0:NT * E], tri[:, :], every, start=True, stop=True)
            pe.matmul(total_bank[:, 0:NT * E], ones[:, :], every, start=True, stop=True).then_inc(counted, 1)

        @block.vector
        def _(eng):
            v = nc.vector
            n_done = [0]

            def then(ins):
                n_done[0] += 1
                ins.then_inc(dv, 1)
                eng.wait_ge(dv, n_done[0])

            v.memset(zero_rows[:, :], 0.0).then_inc(zero_made, 1)
            eng.wait_ge(ld, 48)
            for q in range(NG):
                eng.wait_ge(lt_done, q + 1)
                v.tensor_scalar(logits_t[q % 2][:, :], lt_bank[0:E, :], rb_sb[:, 0:1], None, ALU.add).then_inc(lt_out, 1)
            eng.wait_ge(const, 5)
            eng.wait_ge(lg_done, NG)
            wide = [P, NT, E]
            then(v.tensor_copy(lg[:, :, :].rearrange("p n e -> p (n e)"), lg_bank[:, 0:NT * E]))
            then(v.tensor_reduce(mx[:, :], lg[:, :, :], axis=AX.X, op=ALU.max))
            v.tensor_tensor(prob[:, :, :], lg[:, :, :], mx[:, :].unsqueeze(2).to_broadcast(wide), ALU.subtract).then_inc(centred, 1)
            eng.wait_ge(exped, 1)
            then(v.tensor_reduce(sm[:, :], prob[:, :, :], axis=AX.X, op=ALU.add))
            then(v.reciprocal(sm[:, :], sm[:, :]))
            then(v.tensor_tensor(prob[:, :, :], prob[:, :, :], sm[:, :].unsqueeze(2).to_broadcast(wide), ALU.mult))
            src = prob
            for k in range(K):
                then(v.tensor_reduce(top[k][:, :], src[:, :, :], axis=AX.X, op=ALU.max))
                then(v.tensor_tensor(score[:, :, :], src[:, :, :], top[k][:, :].unsqueeze(2).to_broadcast(wide), ALU.is_ge))
                then(v.tensor_tensor(score[:, :, :], score[:, :, :], rank_w[:, :].unsqueeze(1).to_broadcast(wide), ALU.mult))
                then(v.tensor_reduce(pick[k][:, :], score[:, :, :], axis=AX.X, op=ALU.max))
                then(v.tensor_tensor(chosen[k][:, :, :], score[:, :, :], pick[k][:, :].unsqueeze(2).to_broadcast(wide), ALU.is_equal))
                if k == 0:
                    then(v.scalar_tensor_tensor(out=rest[:, :, :], in0=chosen[0][:, :, :], scalar=-2.0, in1=prob[:, :, :],
                                                op0=ALU.mult, op1=ALU.add))
                    src = rest
            v.tensor_tensor(both[:, :, :], chosen[0][:, :, :], chosen[1][:, :, :], ALU.add).then_inc(both_done, 1)
            v.tensor_tensor(weight[1][:, :], top[1][:, :], top[0][:, :], ALU.subtract).then_inc(gap_c, 1)
            eng.wait_ge(gap_e, 1)
            then(v.tensor_scalar(sm[:, :], weight[1][:, :], 1.0, None, ALU.add))
            then(v.reciprocal(weight[0][:, :], sm[:, :]))
            then(v.tensor_tensor(weight[1][:, :], weight[1][:, :], weight[0][:, :], ALU.mult))
            eng.wait_ge(counted, 1)
            then(v.tensor_copy(totals[:, :, :].rearrange("p n e -> p (n e)"), total_bank[:, 0:NT * E]))
            at, step = totals, 1
            n = 0
            while step < NT:
                to = scan[n % 2]
                v.tensor_copy(to[:, 0:step, :], at[:, 0:step, :])
                then(v.tensor_tensor(to[:, step:NT, :], at[:, step:NT, :], at[:, 0:NT - step, :], ALU.add))
                at, step, n = to, step * 2, n + 1
            then(v.tensor_scalar(cap_i[:, :], at[:, NT - 1, :], float(BLK - 1), None, ALU.add))
            then(v.tensor_scalar(cap_i[:, :], cap_i[:, :], LOGB, LOGB, ALU.logical_shift_right, ALU.logical_shift_left))
            then(v.tensor_copy(cap[:, :], cap_i[:, :]))
            end, step, m = cap, 1, 0
            while step < E:
                to = ends[m % 2]
                v.tensor_copy(to[:, 0:step], end[:, 0:step])
                then(v.tensor_tensor(to[:, step:E], end[:, step:E], end[:, 0:E - step], ALU.add))
                end, step, m = to, step * 2, m + 1
            then(v.tensor_tensor(starts[:, :], end[:, :], cap[:, :], ALU.subtract))
            then(v.tensor_tensor(place[:, :, :], at[:, :, :], totals[:, :, :], ALU.subtract))
            then(v.tensor_tensor(place[:, :, :].rearrange("p n e -> p (n e)"), prefix_bank[:, 0:NT * E],
                                 place[:, :, :].rearrange("p n e -> p (n e)"), ALU.add))
            then(v.tensor_tensor(place[:, :, :], place[:, :, :], starts[:, :].unsqueeze(1).to_broadcast(wide), ALU.add))
            for k in range(K):
                then(v.tensor_tensor(score[:, :, :], place[:, :, :], chosen[k][:, :, :], ALU.mult))
                then(v.tensor_reduce(slot_f[k][:, :], score[:, :, :], axis=AX.X, op=ALU.add))
                then(v.tensor_copy(slot[k][:, :], slot_f[k][:, :]))
            then(v.tensor_tensor(past[:, :, :], blk_at[:, :, :], end[0:1, :].unsqueeze(1).to_broadcast([1, NBLK, E]), ALU.is_ge))
            then(v.tensor_reduce(count_f[:, :], past[:, :, :], axis=AX.X, op=ALU.add))
            v.tensor_scalar(expert_of[:, :], count_f[:, :], float(E - 1), None, ALU.min).then_inc(slots_done, 1)


class Turn:

    def __init__(self, i, pair, parity):
        self.i, self.pair, self.parity = i, pair, parity

    def count(self, per, n, extra):
        at = per * (2 * self.pair + self.parity + n) + extra
        return min(at, per * NBLK) if self.i is None else affine(self.i, 2 * per, at)

    def of_parity(self, per, extra=0):
        return affine(self.i, per, per * self.pair + extra)

    def block(self, n):
        at = 2 * self.pair + self.parity + n
        return Turn(self.i, at // 2, at % 2)

    @property
    def number(self):
        return affine(self.i, 2, 2 * self.pair + self.parity)

    def exists(self):
        return self.i is not None or 0 <= self.number < NBLK


def run_blocks(eng, body):
    end = (NBLK - 2) // 2
    for n in range(-2, 2):
        body(Turn(None, n // 2, n % 2))
    with eng.Fori(0, end - 1) as i:
        body(Turn(i, 1, 0))
        body(Turn(i, 1, 1))
    for n in range(2 * end, NBLK + 1):
        body(Turn(None, n // 2, n % 2))


def experts(nc, w1, w2, b2, expert_of, ident, sorted_x, sorted_y, b1_cols):
    stack = ExitStack()
    with stack:
        def sb(name, shape, dt=F32):
            return stack.enter_context(nc.sbuf_tensor(name, shape, dt))

        def sem(name):
            return stack.enter_context(nc.semaphore(name))

        def two(make, name, *a):
            return [make(f"{name}{k}", *a) for k in range(2)]

        HS = 4
        PIECE = WCOLS // FJ
        w_raw = sb("w_raw", [P, WCOLS])
        wh = two(sb, "wh", [P, WCOLS], F32R)
        wl = two(sb, "wl", [P, WCOLS], F32R)
        x_rows = two(sb, "x_rows", [P, BT, D])
        xh = two(sb, "xh", [P, DC, BLK], F32R)
        xl = two(sb, "xl", [P, DC, BLK], F32R)
        b1_sb = two(sb, "b1_sb", [P, FJ])
        b2_sb = two(sb, "b2_sb", [P, D])
        h = [sb(f"h{k}", [P, BLK]) for k in range(2)]
        hh = [sb(f"hh{k}", [P, BLK], F32R) for k in range(HS)]
        hl = [sb(f"hl{k}", [P, BLK], F32R) for k in range(HS)]
        y_rows = sb("y_rows", [P, BT, D])

        def bank(name):
            return stack.enter_context(nc.psum_tensor(name, [P, 512], F32))
        h_bank = [bank(f"h_bank{k}") for k in range(2)]
        y_bank = [bank(f"y_bank{k}") for k in range(BT)]
        x_bank = [bank(f"x_bank{k}") for k in range(DC)]

        ld_w1, ld_w2 = two(sem, "m_ldw1"), two(sem, "m_ldw2")
        ld_x, ld_b1, ld_b2 = two(sem, "m_ldx"), two(sem, "m_ldb1"), two(sem, "m_ldb2")
        y_stored = sem("m_stored")
        pe_x, pe_h, pe_y = sem("m_pe_x"), sem("m_pe_h"), sem("m_pe_y")
        act_w, act_x, act_h = sem("m_act_w"), sem("m_act_x"), sem("m_act_h")
        dve_w, dve_x, dve_hh, dve_hl, dve_y = (sem(f"m_dve_{n}") for n in ("w", "x", "hh", "hl", "y"))

        block = stack.enter_context(nc.Block())

        def piece(t, k):
            return t[:, k * PIECE:(k + 1) * PIECE]

        @block.sync
        def _(eng):
            def expert(b):
                return eng.value_load(expert_of[0:1, bass.ds(b.number, 1)], min_val=0, max_val=E - 1)

            def cycle(c):
                far, near, now, was = (c.block(n) for n in (2, 1, 0, -1))
                if near.exists():
                    e = expert(near)
                    wait(eng, act_h, c.count(FJ, 0, 0))
                    eng.dma_start(b1_sb[near.parity][:, :], b1_cols[:, e, :]).then_inc(ld_b1[near.parity], 16)
                if now.exists():
                    e = expert(now)
                    wait(eng, dve_y, c.count(1, -1, 0))
                    eng.dma_start(b2_sb[now.parity][:, :], b2[e].partition_broadcast(P)).then_inc(ld_b2[now.parity], 16)
                if was.exists():
                    eng.wait_ge(dve_y, c.count(1, -1, 1))
                    eng.dma_start(sorted_y.rearrange("(n t p) d -> n p t d", p=P, t=BT)[was.number],
                                  y_rows[:, :, :]).then_inc(y_stored, 16)
                if far.exists():
                    e = expert(far)
                    wait(eng, dve_w, c.count(FJ, 1, FJ // 2))
                    eng.dma_start(w_raw[:, 0:DC * FF].rearrange("p (a f) -> p a f", a=DC),
                                  w1[e].rearrange("(a p) f -> p a f", p=P)).then_inc(ld_w1[far.parity], 16)
                    wait(eng, pe_x, c.count(1, 0, 1))
                    eng.dma_start(x_rows[far.parity][:, :, :],
                                  sorted_x.rearrange("(n t p) d -> n p t d", p=P, t=BT)[far.number]).then_inc(ld_x[far.parity], 16)
                    wait(eng, dve_w, c.count(FJ, 1, FJ))
                    eng.dma_start(w_raw[:, DC * FF:WCOLS].rearrange("p (j d) -> p j d", j=FJ),
                                  w2[e].rearrange("(j p) d -> p j d", p=P)).then_inc(ld_w2[far.parity], 16)
            run_blocks(eng, cycle)
            eng.wait_ge(y_stored, 16 * NBLK)

        @block.scalar
        def _(eng):
            a = nc.scalar

            def cycle(c):
                near, now = c.block(1), c.block(0)
                j2 = c.parity
                for j in range(FJ):
                    if now.exists():
                        if j == 0:
                            eng.wait_ge(ld_b1[j2], now.of_parity(16, 16))
                        eng.wait_ge(pe_h, c.count(FJ, 0, j + 1))
                        wait(eng, dve_hl, c.count(FJ, 0, j - 1))
                        a.activation(h[j % 2][:, :], h_bank[j % 2][:, :], ACT.Gelu,
                                     bias=b1_sb[j2][:, j:j + 1]).then_inc(act_h, 1)
                    if near.exists():
                        if j == 0:
                            eng.wait_ge(ld_w1[near.parity], near.of_parity(16, 16))
                            wait(eng, pe_h, c.count(FJ, 0, 0))
                        if j == FJ // 2:
                            eng.wait_ge(ld_w2[near.parity], near.of_parity(16, 16))
                            wait(eng, pe_y, c.count(FJ, 0, 0))
                        a.activation(piece(wh[near.parity], j), piece(w_raw, j), ACT.Copy).then_inc(act_w, 1)
                        if j == 3:
                            eng.wait_ge(pe_x, c.count(1, 1, 1))
                            for k in range(DC):
                                last = a.activation(xh[near.parity][:, k, :], x_bank[k][:, :], ACT.Copy)
                            last.then_inc(act_x, 1)
            run_blocks(eng, cycle)

        @block.vector
        def _(eng):
            v = nc.vector

            def cycle(c):
                near, now, was = c.block(1), c.block(0), c.block(-1)
                for j in range(FJ):
                    if now.exists():
                        eng.wait_ge(act_h, c.count(FJ, 0, j + 1))
                        wait(eng, pe_y, c.count(FJ, 0, j + 1 - HS))
                        v.tensor_copy(hh[j % HS][:, :], h[j % 2][:, :]).then_inc(dve_hh, 1)
                        eng.wait_ge(dve_hh, c.count(FJ, 0, j + 1))
                        v.tensor_tensor(hl[j % HS][:, :], h[j % 2][:, :], hh[j % HS][:, :].bitcast(F32),
                                        ALU.subtract).then_inc(dve_hl, 1)
                    if j == LAG and was.exists():
                        eng.wait_ge(pe_y, c.count(FJ, -1, FJ))
                        eng.wait_ge(ld_b2[was.parity], was.of_parity(16, 16))
                        wait(eng, y_stored, c.count(16, -1, 0))
                        for t in range(BT):
                            last = v.tensor_tensor(y_rows[:, t, :], y_bank[t][:, 0:D], b2_sb[was.parity][:, :], ALU.add)
                        last.then_inc(dve_y, 1)
                    if near.exists():
                        wait(eng, pe_h if j < FJ // 2 else pe_y, c.count(FJ, 0, 0))
                        eng.wait_ge(act_w, c.count(FJ, 1, j + 1))
                        v.tensor_tensor(piece(wl[near.parity], j), piece(w_raw, j), piece(wh[near.parity], j).bitcast(F32),
                                        ALU.subtract).then_inc(dve_w, 1)
                        if j == 3:
                            eng.wait_ge(act_x, c.count(1, 1, 1))
                            for k in range(DC):
                                last = v.tensor_tensor(xl[near.parity][:, k, :], x_bank[k][:, :],
                                                       xh[near.parity][:, k, :].bitcast(F32), ALU.subtract)
                            last.then_inc(dve_x, 1)
            run_blocks(eng, cycle)

        @block.tensor
        def _(eng):
            pe = nc.tensor

            def second(c, back, m):
                b = c.block(-back)
                w = [t[b.parity][:, DC * FF + m * D:DC * FF + (m + 1) * D] for t in (wh, wl)]
                eng.wait_ge(dve_hl, c.count(FJ, -back, m + 1))
                if m == 0:
                    wait(eng, dve_y, c.count(1, -1, 1))
                    eng.wait_ge(dve_w, c.count(FJ, 0, FJ))
                for t in range(BT):
                    ts = slice(t * P, (t + 1) * P)
                    for n, (l, r) in enumerate(((hh, w[0]), (hh, w[1]), (hl, w[0]))):
                        last = pe.matmul(y_bank[t][:, 0:D], l[m % HS][:, ts], r,
                                         start=(m == 0 and n == 0), stop=(m == FJ - 1 and n == 2))
                last.then_inc(pe_y, 1)

            def cycle(c):
                near, now, was = c.block(1), c.block(0), c.block(-1)
                p = c.parity
                for j in range(FJ):
                    if now.exists():
                        if j == 0:
                            eng.wait_ge(dve_w, c.count(FJ, 0, FJ // 2))
                            eng.wait_ge(dve_x, c.count(1, 0, 1))
                        wait(eng, act_h, c.count(FJ, 0, j - 1))
                        n = 0
                        for a in range(DC):
                            cols = slice(a * FF + j * P, a * FF + (j + 1) * P)
                            for l, r in ((wh, xh), (wh, xl), (wl, xh)):
                                last = pe.matmul(h_bank[j % 2][:, :], l[p][:, cols], r[p][:, a, :],
                                                 start=(n == 0), stop=(n == 3 * DC - 1))
                                n += 1
                        last.then_inc(pe_h, 1)
                    if j < LAG:
                        if was.exists():
                            second(c, 1, FJ - LAG + j)
                    elif now.exists():
                        second(c, 0, j - LAG)
                    if j == 2 and near.exists():
                        eng.wait_ge(ld_x[near.parity], near.of_parity(16, 16))
                        wait(eng, dve_x, c.count(1, 0, 1))
                        for a in range(DC):
                            for t in range(BT):
                                last = pe.transpose(x_bank[a][:, t * P:(t + 1) * P],
                                                    x_rows[near.parity][:, t, a * P:(a + 1) * P], ident[:, :])
                        last.then_inc(pe_x, 1)
            run_blocks(eng, cycle)


def combine(nc, x2_sb, slot, weight, sorted_y, g3, b3, out):
    stack = ExitStack()
    with stack:
        def sb(name, shape, dt=F32):
            return stack.enter_context(nc.sbuf_tensor(name, shape, dt))

        def sem(name):
            return stack.enter_context(nc.semaphore(name))

        R = 4
        g_row, b_row = sb("g3_row", [P, D]), sb("b3_row", [P, D])
        got = [[sb(f"got{r}{k}", [P, ST, D]) for k in range(K)] for r in range(R)]
        stats = sb("stats3", [P, ST, 6])
        mv = [sb(f"mv3{k}", [P, ST, 2]) for k in range(2)]
        ve, rstd = sb("ve3", [P, ST]), [sb(f"rstd3{k}", [P, ST]) for k in range(2)]
        shift = [sb(f"shift3{k}", [P, ST]) for k in range(2)]
        eps, half = sb("eps3", [P, ST]), sb("half3", [P, ST])
        o = [sb(f"o3{k}", [P, ST, D]) for k in range(2)]
        ld, const = sem("f_ld"), sem("f_const")
        landed = [sem(f"f_landed{r}") for r in range(R)]
        normed, scaled, ve_done, rs = (sem(f"f_{n}") for n in ("norm", "scale", "ve", "rs"))
        stored = [sem(f"f_stored{k}") for k in range(2)]
        add0, add1, st_d, mean_d, gained = (sem(f"f_{n}") for n in ("add0", "add1", "st", "mean", "gain"))
        block = stack.enter_context(nc.Block())

        @block.sync
        def _(eng):
            eng.dma_start(g_row[:, :], g3.partition_broadcast(P)).then_inc(ld, 16)
            eng.dma_start(b_row[:, :], b3.partition_broadcast(P)).then_inc(ld, 16)
            for b in range(B):
                eng.wait_ge(scaled, b + 1)
                eng.dma_start(out[b].rearrange("(t p) d -> p t d", p=P), o[b % 2][:, :, :]).then_inc(stored[b % 2], 16)
            for k in range(2):
                eng.wait_ge(stored[k], 16 * B // 2)

        @block.gpsimd
        def _(eng):
            g = nc.gpsimd
            g.memset(eps[:, :], EPS).then_inc(const, 1)
            g.memset(half[:, :], -0.5).then_inc(const, 1)
            eng.wait_ge(const, 2)

            def gather(b):
                if b >= R:
                    eng.wait_ge(normed, b - R + 1)
                for t in range(ST):
                    for k in range(K):
                        g.indirect_dma_start(got[b % R][k][:, t, :], None, sorted_y,
                                             bass.IndirectOffsetOnAxis(ap=slot[k][:, b * ST + t:b * ST + t + 1], axis=0),
                                             bounds_check=NBLK * BLK - 1).then_inc(landed[b % R], 16)
            for b in range(B + 1):
                if b < B:
                    gather(b)
                if b >= 1:
                    d = b - 1
                    eng.wait_ge(mean_d, d + 1)
                    wait(eng, rs, d)
                    g.tensor_tensor(ve[:, :], mv[d % 2][:, :, 1], eps[:, :], ALU.add).then_inc(ve_done, 1)
                    eng.wait_ge(ve_done, d + 1)
                    g.tensor_tensor(rstd[d % 2][:, :], ve[:, :], half[:, :], ALU.pow).then_inc(rs, 1)

        @block.vector
        def _(eng):
            v = nc.vector
            eng.wait_ge(ld, 32)

            def first(b):
                eng.wait_ge(landed[b % R], 64 * (b // R + 1))
                y = got[b % R][0]
                for t in range(ST):
                    i = b * ST + t
                    last = v.scalar_tensor_tensor(out=y[:, t, :], in0=y[:, t, :], scalar=weight[0][:, i:i + 1],
                                                  in1=x2_sb[:, i, :], op0=ALU.mult, op1=ALU.add)
                last.then_inc(add0, 1)
                eng.wait_ge(add0, b + 1)
                for t in range(ST):
                    i = b * ST + t
                    last = v.scalar_tensor_tensor(out=y[:, t, :], in0=got[b % R][1][:, t, :], scalar=weight[1][:, i:i + 1],
                                                  in1=y[:, t, :], op0=ALU.mult, op1=ALU.add)
                last.then_inc(add1, 1)
                eng.wait_ge(add1, b + 1)
                for t in range(ST):
                    last = v.bn_stats(stats[:, t, :], y[:, t, :])
                last.then_inc(st_d, 1)
                eng.wait_ge(st_d, b + 1)
                for t in range(ST):
                    last = v.bn_aggr(mv[b % 2][:, t, :], stats[:, t, :])
                last.then_inc(mean_d, 1)

            def second(b):
                y = got[b % R][0]
                eng.wait_ge(rs, b + 1)
                if b >= 2:
                    eng.wait_ge(stored[b % 2], 16 * (b // 2))
                for t in range(ST):
                    last = v.tensor_scalar(o[b % 2][:, t, :], y[:, t, :], mv[b % 2][:, t, 0:1], rstd[b % 2][:, t:t + 1],
                                           ALU.subtract, ALU.mult)
                last.then_inc(normed, 1)
                eng.wait_ge(normed, b + 1)
                wide = [P, ST, D]
                v.tensor_tensor(o[b % 2][:, :, :], o[b % 2][:, :, :], g_row[:, :].unsqueeze(1).to_broadcast(wide), ALU.mult).then_inc(gained, 1)
                eng.wait_ge(gained, b + 1)
                v.tensor_tensor(o[b % 2][:, :, :], o[b % 2][:, :, :], b_row[:, :].unsqueeze(1).to_broadcast(wide), ALU.add).then_inc(scaled, 1)

            for b in range(B + 1):
                if b < B:
                    first(b)
                if b >= 1:
                    second(b - 1)


def layer_program(nc, x, ctxt, sa, ca, norms, router, expert_w, out):
    x2 = nc.dram_tensor("x2_scratch", (B, P, ST, D), F32, kind="Internal").ap()
    attention_program(nc, x, ctxt, sa, ca, norms[0], norms[1], x2)
    moe_program(nc, x2, *router, *expert_w, *norms[2], out)


_PRE = "L0_xattn_"
_ATT = ["wq", "bq", "wk", "bk", "wv", "bv", "wo", "bo"]
_OUTS = [((B, S, D), "float32")]


def kernel(**inputs):
    import numpy as _np
    import concourse.bacc as _bacc
    from concourse import mybir as _mybir
    from concourse.bass_utils import run_bass_kernel_spmd as _run

    nc = _bacc.Bacc("TRN2", target_bir_lowering=False, num_devices=1)
    arrays = {}

    def given(name):
        a = _np.ascontiguousarray(inputs[name])
        arrays[f"in_{name}_dram"] = a
        return nc.dram_tensor(f"in_{name}_dram", a.shape, _mybir.dt.from_np(a.dtype), kind="ExternalInput").ap()

    x, ctxt = given("x"), given("ctx_1024")
    sa = [given(_PRE + "sa_" + n) for n in _ATT]
    ca = [given(_PRE + "ca_" + n) for n in _ATT]
    norms = [(given(f"{_PRE}ln{k}_g"), given(f"{_PRE}ln{k}_b")) for k in (1, 2, 3)]
    router = [given(_PRE + "router_w"), given(_PRE + "router_b")]
    expert_w = [given(_PRE + n) for n in ("e_w1", "e_b1", "e_w2", "e_b2")]
    out = nc.dram_tensor("out_0_dram", _OUTS[0][0], F32, kind="ExternalOutput").ap()
    layer_program(nc, x, ctxt, sa, ca, norms, router, expert_w, out)
    r = _run(nc, [arrays], core_ids=[0])
    return r.results[0]["out_0_dram"]
```

```python
import concourse.bass as bass
from concourse import mybir
from contextlib import ExitStack

F32 = mybir.dt.float32
F32R = mybir.dt.float32r
BF16 = mybir.dt.bfloat16
I32 = mybir.dt.int32
ALU = mybir.AluOpType
ACT = mybir.ActivationFunctionType
AX = mybir.AxisListType

P = 128
B, S, D, H = 16, 256, 256, 16
HD = D // H
ST = S // P
DC = D // P
HC = P // HD
G = 4
GH = H // G
VW = 32
ITEMS = 2 * B
PARTS = 3
MROW = P - 1
SCALE = float(HD) ** -0.5
MASKED = -1.0e30
EPS = 1e-5


def affine(i, times, plus):
    return plus if i is None else i * times + plus


class Item:

    def __init__(self, i, pair, parity, cross):
        self.i, self.pair, self.parity, self.cross = i, pair, parity, cross

    def of_parity(self, per, extra=0):
        return affine(self.i, per, per * self.pair + extra)

    def of_cross(self, per, extra=0):
        return self.of_parity(per, extra - per * B // 2)

    @property
    def batch(self):
        return affine(self.i, 2, 2 * self.pair + self.parity - (B if self.cross else 0))

    def exists(self):
        return self.i is not None or 0 <= 2 * self.pair + self.parity < ITEMS

    def is_number(self, n):
        return self.i is None and 2 * self.pair + self.parity == n


class Cycle:

    def __init__(self, i, pair, parity, cross=None):
        self.i, self.pair, self.parity, self.cross = i, pair, parity, cross

    def is_number(self, n):
        return self.i is None and 2 * self.pair + self.parity == n

    def item(self, n):
        at = 2 * self.pair + self.parity + n
        return Item(self.i, at // 2, at % 2, at >= B if self.i is None else self.cross)

    def count(self, per, n, extra):
        at = per * (2 * self.pair + self.parity + n) + extra
        return min(at, per * ITEMS) if self.i is None else affine(self.i, 2 * per, at)


def wait(eng, sem, value):
    if not isinstance(value, int) or value > 0:
        eng.wait_ge(sem, value)


def run_cycles(eng, body):
    for c in range(-3, 4):
        body(Cycle(None, c // 2, c % 2))
    with eng.Fori(0, 4) as i:
        body(Cycle(i, 2, 0, False))
        body(Cycle(i, 2, 1, False))
    for c in range(12, 18):
        body(Cycle(None, c // 2, c % 2))
    with eng.Fori(0, 5) as i:
        body(Cycle(i, 9, 0, True))
        body(Cycle(i, 9, 1, True))
    for c in range(28, ITEMS + 2):
        body(Cycle(None, c // 2, c % 2))


def attention_program(nc, x, ctxt, sa, ca, ln1, ln2, out):
    stack = ExitStack()
    with stack:
        def sb(name, shape, dt=F32):
            return stack.enter_context(nc.sbuf_tensor(name, shape, dt))

        def sem(name):
            return stack.enter_context(nc.semaphore(name))

        def two(make, name, *a):
            return [make(f"{name}{k}", *a) for k in range(2)]

        x1 = nc.dram_tensor("x1_scratch", (B, P, ST, D), F32, kind="Internal").ap()
        bounce = nc.dram_tensor("qk_bounce", (2, 2, 2, HD, HC * DC * S), F32, kind="Internal").ap()

        names = ["sq", "sk", "sv", "so", "cq", "ck", "cv", "co"]
        w_in = [sb(f"w_in{k}", [P, DC, D]) for k in range(2)]
        w_hi = {n: sb(f"w_{n}_hi", [P, DC, D], F32R) for n in names}
        w_lo = {n: sb(f"w_{n}_lo", [P, DC, D], F32R) for n in names}
        qk_bias = {n: sb(f"b_{n}", [P, DC]) for n in ("sq", "sk", "cq", "ck")}
        row = {n: sb(f"row_{n}", [P, D]) for n in ("sv", "so", "cv", "co", "g1", "b1", "g2", "b2")}
        ident = sb("ident", [P, P])
        ident_bf = sb("ident_bf", [P, P], BF16)
        mask_qk = sb("mask_qk", [P, P], BF16)
        mask_kq = sb("mask_kq", [P, P], BF16)
        eps = sb("eps", [P, ST])
        minus_half = sb("minus_half", [P, ST])

        x_in = two(sb, "x_in", [P, ST, D])
        c_in = two(sb, "c_in", [P, ST, D])
        staged = w_in + c_in + w_in + w_in
        staging = [0, 1, 2, 3, 0, 1, 0, 1]
        landing = [1, 1, 1, 1, 2, 2, 3, 3]
        x_res = two(sb, "x_res", [P, ST, D])
        xt_hi = two(sb, "xt_hi", [P, DC, S], F32R)
        xt_lo = two(sb, "xt_lo", [P, DC, S], F32R)
        ct_hi = two(sb, "ct_hi", [P, DC, S], F32R)
        ct_lo = two(sb, "ct_lo", [P, DC, S], F32R)
        proj_hi = {n: sb(f"{n}_hi", [P, DC, S], F32R) for n in "qk"}
        proj_lo = {n: sb(f"{n}_lo", [P, DC, S], F32R) for n in "qk"}
        q_stack = two(sb, "q_stack", [P, H, S], F32R)
        k_stack = two(sb, "k_stack", [P, H, S], F32R)
        v_aug = two(sb, "v_aug", [P, ST, H, VW])
        maxima3 = two(sb, "maxima3", [P, 3, H])
        maxima = two(sb, "maxima", [P, ST, H])
        ones_row = sb("ones_row", [H, S])
        m_neg = [two(sb, f"m_neg{half}", [H // 2, S], F32R) for half in range(2)]
        probs = two(sb, "probs", [P, GH, ST, S])
        heads_t = [sb(f"heads_t{g}", [P, S]) for g in range(G)]
        inv_sum = sb("inv_sum", [P, 16])
        heads = sb("heads", [P, ST, D])
        ot_hi = sb("ot_hi", [P, DC, S], F32R)
        ot_lo = sb("ot_lo", [P, DC, S], F32R)
        y = two(sb, "y", [P, ST, D])
        stats = sb("stats", [P, ST, 6])
        counted = sb("counted", [P, ST])
        mean_var = two(sb, "mean_var", [P, ST, 2])
        var_eps = sb("var_eps", [P, ST])
        rstd = two(sb, "rstd", [P, ST])
        minus_mean = sb("minus_mean", [P, ST])
        minus_one = sb("minus_one", [P, ST])
        shift = two(sb, "shift", [P, ST])
        z = two(sb, "z", [P, ST, D])
        x_out = two(sb, "x_out", [P, ST, D])

        def bank(name):
            return stack.enter_context(nc.psum_tensor(name, [P, 512], F32))

        s_bank = [bank("s_bank0"), bank("s_bank1")]
        t_bank = [bank("t_bank0"), bank("t_bank1")]
        av_bank = bank("av_bank")
        misc = [bank("misc0"), bank("misc1"), bank("misc2")]

        ld_w, w_split, w_halved = [sem(f"ld_w{k}") for k in range(4)], sem("w_split"), sem("w_halved")
        ld_qk_bias, ld_rows, const_made = sem("ld_qk_bias"), sem("ld_rows"), sem("const_made")
        zeroed, ones_made, ones_placed = two(sem, "zeroed"), sem("ones_made"), sem("ones_placed")
        pool_chain = sem("pool_chain")
        ld_x, ld_c, ld_r = two(sem, "ld_x"), two(sem, "ld_c"), two(sem, "ld_r")
        bounced = two(sem, "bounced")
        stacked = [two(sem, f"stacked{half}") for half in range(2)]
        m_placed = [two(sem, f"m_placed{half}") for half in range(2)]
        stored = two(sem, "stored")
        pe_xt, pe_ct, pe_q, pe_k, pe_v = sem("pe_xt"), sem("pe_ct"), sem("pe_q"), sem("pe_k"), sem("pe_v")
        pe_s, pe_t, pe_av, pe_mt = sem("pe_s"), sem("pe_t"), sem("pe_av"), sem("pe_mt")
        pe_tr, pe_ot, pe_wo = sem("pe_tr"), sem("pe_ot"), sem("pe_wo")
        act_xt, act_ct, act_q, act_k = sem("act_xt"), sem("act_ct"), sem("act_q"), sem("act_k")
        act_exp, act_av, act_ot = sem("act_exp"), sem("act_av"), sem("act_ot")
        act_m, act_z = sem("act_m"), sem("act_z")
        dve_xt, dve_ct, dve_q, dve_k, dve_v = (sem(f"dve_{n}") for n in ("xt", "ct", "q", "k", "v"))
        dve_max, dve_joined, dve_inv = sem("dve_max"), sem("dve_joined"), sem("dve_inv")
        dve_tr, dve_ot, dve_y = sem("dve_tr"), sem("dve_ot"), sem("dve_y")
        dve_stats, dve_mean = sem("dve_stats"), sem("dve_mean")
        pool_res, pool_eps, pool_rstd = sem("pool_res"), sem("pool_eps"), sem("pool_rstd")
        pool_mean, pool_shift = sem("pool_mean"), sem("pool_shift")
        pool_gain, pool_out = sem("pool_gain"), sem("pool_out")

        w_dram = {"sq": sa[0], "sk": sa[2], "sv": sa[4], "so": sa[6],
                  "cq": ca[0], "ck": ca[2], "cv": ca[4], "co": ca[6]}
        b_dram = {"sq": sa[1], "sk": sa[3], "cq": ca[1], "ck": ca[3]}
        row_dram = {"sv": sa[5], "so": sa[7], "cv": ca[5], "co": ca[7],
                    "g1": ln1[0], "b1": ln1[1], "g2": ln2[0], "b2": ln2[1]}

        def by_head(ap, n):
            return ap.rearrange("p a (g c d) -> p a c g d", c=DC, d=HD) if n[1] in "qk" else ap

        block = stack.enter_context(nc.Block())

        @block.sync
        def _(eng):
            def load_weight(k):
                eng.dma_start(staged[k][:, :, :], w_dram[names[k]].rearrange("(a p) n -> p a n", p=P)).then_inc(ld_w[staging[k]], 16)

            def load_bias(n, ready):
                for i in range(DC):
                    eng.dma_start(qk_bias[n][:, i:i + 1], b_dram[n].rearrange("(g c d) -> c g d", c=DC, d=HD)[i],
                                  allow_slow_non_contiguous=True).then_inc(ready, 16)

            eng.dma_start(x_in[0][:, :, :], x[0].rearrange("(t p) d -> p t d", p=P)).then_inc(ld_x[0], 16)
            for k in range(4):
                load_weight(k)
            load_bias("sq", ld_qk_bias)
            load_bias("sk", ld_qk_bias)

            def cycle(c):
                load, proj, now, smax, done = (c.item(n) for n in (3, 2, 0, 1, -2))
                j = c.parity
                if c.is_number(-2):
                    for n in row:
                        eng.dma_start(row[n][:, :], row_dram[n].partition_broadcast(P)).then_inc(ld_rows, 16)
                    load_bias("cq", ld_rows)
                    load_bias("ck", ld_rows)
                if c.is_number(-1) or c.is_number(0):
                    eng.wait_ge(w_split, 4)
                    load_weight(4 if c.is_number(-1) else 5)
                if c.is_number(2) or c.is_number(3):
                    k = 6 if c.is_number(2) else 7
                    eng.wait_ge(w_split, k - 1)
                    load_weight(k)
                if now.exists():
                    eng.wait_ge(act_m, c.count(2, 0, 2))
                    eng.dma_start(q_stack[j][MROW:P, H // 2:H, :].bitcast(F32),
                                  m_neg[1][j][:, :].bitcast(F32)).then_inc(m_placed[1][j], 16)
                if load.exists() and not load.is_number(0):
                    if load.cross:
                        wait(eng, pe_ct, c.count(1, 1 - B, 1))
                        eng.dma_start(c_in[load.parity][:, :, :],
                                      ctxt[load.batch].rearrange("(t p) d -> p t d", p=P)).then_inc(ld_c[load.parity], 16)
                        if c.i is None:
                            wait(eng, pe_xt, c.count(1, 1, 1))
                        eng.wait_ge(stored[load.parity], load.of_cross(16, 16))
                        eng.dma_start(x_in[load.parity][:, :, :], x1[load.batch]).then_inc(ld_x[load.parity], 16)
                    else:
                        wait(eng, pe_xt, c.count(1, 1, 1))
                        eng.dma_start(x_in[load.parity][:, :, :],
                                      x[load.batch].rearrange("(t p) d -> p t d", p=P)).then_inc(ld_x[load.parity], 16)
                if now.exists():
                    wait(eng, dve_y, c.count(1, -2, 1))
                    eng.dma_start(x_res[j][:, :, :], x1[now.batch] if now.cross else
                                  x[now.batch].rearrange("(t p) d -> p t d", p=P)).then_inc(ld_r[j], 16)
                if proj.exists():
                    for n, (q, ready) in enumerate((("q", dve_q), ("k", dve_k))):
                        eng.wait_ge(ready, c.count(1, 2, 1))
                        for part, src in enumerate((proj_hi, proj_lo)):
                            if n and part:
                                wait(eng, pe_t, c.count(H, 0, H // 2))
                            eng.dma_start(bounce[j, n, part].rearrange("d (g t) -> g d t", g=HC),
                                          src[q][:, :, :].rearrange("p c t -> p (c t)").bitcast(F32)).then_inc(bounced[j], 16)
                    eng.wait_ge(bounced[j], proj.of_parity(64, 64))
                    if proj.is_number(0) or proj.is_number(1):
                        eng.wait_ge(zeroed[j], 2)
                        eng.wait_ge(ones_made, 1)
                        eng.dma_start(k_stack[j][MROW:P, :, :].bitcast(F32), ones_row[:, :]).then_inc(ones_placed, 16)
                for half in range(2):
                    if half == 1:
                        if smax.exists():
                            eng.wait_ge(act_m, c.count(2, 1, 1))
                            eng.dma_start(q_stack[1 - j][MROW:P, 0:H // 2, :].bitcast(F32),
                                          m_neg[0][1 - j][:, :].bitcast(F32)).then_inc(m_placed[0][1 - j], 16)
                        if done.exists():
                            eng.wait_ge(pool_out, c.count(1, -2, 1))
                            eng.dma_start(out[done.batch] if done.cross else x1[done.batch],
                                          x_out[j][:, :, :]).then_inc(stored[j], 16)
                    if proj.exists():
                        if half == 1:
                            wait(eng, pe_t, c.count(H, 0, H))
                        hs = slice(half * H // 2, (half + 1) * H // 2)
                        for n, (dst, parts) in enumerate(((q_stack[j], ((0, 1, 1), (HD, 0, 1), (2 * HD, 0, 1))),
                                                          (k_stack[j], ((0, 0, 1), (HD, 0, 2))))):
                            for at, part, m in parts:
                                eng.dma_start(dst[at:at + m * HD, hs, :].rearrange("p h t -> p (h t)").bitcast(F32),
                                              bounce[j, n, part:part + m, :, half * (H // 2) * S:(half + 1) * (H // 2) * S]
                                              .rearrange("a d t -> (a d) t")).then_inc(stacked[half][j], 16)

            run_cycles(eng, cycle)
            for k in range(2):
                eng.wait_ge(stored[k], ITEMS // 2 * 16)

        @block.gpsimd
        def _(eng):
            g = nc.gpsimd
            g.memset(ident[:, :], 0.0).then_inc(pool_chain, 1)
            g.memset(mask_qk[:, :], 0.0).then_inc(pool_chain, 1)
            g.memset(mask_kq[:, :], 0.0).then_inc(pool_chain, 1)
            g.memset(eps[:, :], EPS).then_inc(const_made, 1)
            g.memset(minus_half[:, :], -0.5).then_inc(const_made, 1)
            g.memset(minus_one[:, :], -1.0).then_inc(const_made, 1)
            eng.wait_ge(pool_chain, 3)
            g.affine_select(out=ident[:, :], in_=ident[:, :], compare_op=ALU.not_equal, fill=1.0, base=0,
                            pattern=[[-1, P]], channel_multiplier=1).then_inc(pool_chain, 1)
            g.affine_select(out=mask_qk[:, :], in_=mask_qk[:, :], compare_op=ALU.is_ge, fill=MASKED, base=0,
                            pattern=[[-1, P]], channel_multiplier=1).then_inc(const_made, 1)
            g.affine_select(out=mask_kq[:, :], in_=mask_kq[:, :], compare_op=ALU.is_ge, fill=MASKED, base=0,
                            pattern=[[1, P]], channel_multiplier=-1).then_inc(const_made, 1)
            eng.wait_ge(pool_chain, 4)
            g.tensor_copy(ident_bf[:, :], ident[:, :]).then_inc(const_made, 1)
            g.memset(ones_row[:, :], 1.0).then_inc(ones_made, 1)
            g.memset(q_stack[0][:, :, :].bitcast(F32), 0.0).then_inc(zeroed[0], 1)
            g.memset(q_stack[1][:, :, :].bitcast(F32), 0.0).then_inc(zeroed[1], 1)
            eng.wait_ge(const_made, 6)
            eng.wait_ge(ld_rows, 12 * 16)

            def cycle(c):
                now, fin, done = c.item(0), c.item(-1), c.item(-2)
                j = c.parity
                if now.exists():
                    eng.wait_ge(ld_r[j], now.of_parity(16, 16))
                    bo = row["co" if now.cross else "so"]
                    for t in range(ST):
                        last = g.tensor_tensor(x_res[j][:, t, :], x_res[j][:, t, :], bo[:, :], ALU.add)
                    last.then_inc(pool_res, 1)
                if done.exists():
                    k = "2" if done.cross else "1"
                    eng.wait_ge(act_z, c.count(1, -2, 1))
                    for t in range(ST):
                        last = g.tensor_tensor(z[j][:, t, :], z[j][:, t, :], row["g" + k][:, :], ALU.mult)
                    last.then_inc(pool_gain, 1)
                    eng.wait_ge(pool_gain, c.count(1, -2, 1))
                    if not (done.is_number(0) or done.is_number(1)):
                        eng.wait_ge(stored[j], done.of_parity(16))
                    for t in range(ST):
                        last = g.tensor_tensor(x_out[j][:, t, :], z[j][:, t, :], row["b" + k][:, :], ALU.add)
                    last.then_inc(pool_out, 1)
                if fin.exists():
                    k = 1 - j
                    eng.wait_ge(dve_mean, c.count(1, -1, 1))
                    g.tensor_tensor(var_eps[:, :], mean_var[k][:, :, 1], eps[:, :], ALU.add).then_inc(pool_eps, 1)
                    g.tensor_tensor(minus_mean[:, :], mean_var[k][:, :, 0], minus_one[:, :], ALU.mult).then_inc(pool_mean, 1)
                    eng.wait_ge(pool_eps, c.count(1, -1, 1))
                    g.tensor_tensor(rstd[k][:, :], var_eps[:, :], minus_half[:, :], ALU.pow).then_inc(pool_rstd, 1)
                    eng.wait_ge(pool_rstd, c.count(1, -1, 1))
                    g.tensor_tensor(shift[k][:, :], minus_mean[:, :], rstd[k][:, :], ALU.mult).then_inc(pool_shift, 1)

            run_cycles(eng, cycle)

        @block.scalar
        def _(eng):
            a = nc.scalar

            def halve(k):
                n = names[k]
                eng.wait_ge(ld_w[staging[k]], 16 * landing[k])
                for i in range(DC):
                    if n[1] in "qk":
                        last = a.activation(w_hi[n][:, i:i + 1, :].rearrange("p a (c g d) -> p a c g d", c=DC, d=HD)[:, 0],
                                            by_head(staged[k][:, i:i + 1, :], n)[:, 0], ACT.Copy)
                    else:
                        last = a.activation(w_hi[n][:, i, :], staged[k][:, i, :], ACT.Copy)
                last.then_inc(w_halved, 1)

            for k in range(4):
                halve(k)

            def cycle(c):
                proj, smax, now, fin, done = (c.item(n) for n in (2, 1, 0, -1, -2))
                j = c.parity
                p = proj.parity
                for k in range(4):
                    if c.is_number(k):
                        halve(4 + k)

                def from_values(n, g):
                    eng.wait_ge(pe_av, c.count(G, n, g + 1))
                    wait(eng, pe_tr, c.count(2, n - 1, 1 + g // 2))
                    a.activation(heads_t[g][:, :], av_bank[:, 0:S], ACT.Copy).then_inc(act_av, 1)

                def minus_max(half, n):
                    eng.wait_ge(pe_mt, c.count(2, n, 1 + half))
                    it = c.item(n)
                    if not (it.is_number(0) or it.is_number(1)):
                        eng.wait_ge(m_placed[half][it.parity], it.of_parity(16))
                    a.activation(m_neg[half][it.parity][:, :], misc[0][0:H // 2, 0:S], ACT.Copy, scale=-1.0).then_inc(act_m, 1)

                def project(q, bk, ready, done):
                    w = "c" if proj.cross else "s"
                    eng.wait_ge(ready, c.count(1, 2, 1))
                    if q == "q" and not proj.is_number(0):
                        prev = c.item(1)
                        eng.wait_ge(bounced[prev.parity], prev.of_parity(64, 64))
                    for i in range(DC):
                        last = a.activation(proj_hi[q][:, i, :], misc[bk][:, i * S:(i + 1) * S], ACT.Identity,
                                            bias=qk_bias[w + q][:, i:i + 1])
                    last.then_inc(done, 1)

                for h in range(H):
                    if now.exists():
                        cols = S + P if not now.cross else 2 * S
                        if h % GH == 0:
                            wait(eng, pe_av, c.count(G, 0, h // GH - 1))
                        eng.wait_ge(pe_t, c.count(H, 0, h + 1))
                        pr = probs[h // GH % 2][:, h % GH].rearrange("p a s -> p (a s)")
                        a.activation(pr[:, 0:cols], t_bank[h % 2][:, 0:cols], ACT.Exp, scale=SCALE).then_inc(act_exp, 1)
                    if h == 0 and proj.exists():
                        eng.wait_ge(pe_xt, c.count(1, 2, 1))
                        wait(eng, pe_v, c.count(1, 0, 1))
                        a.activation(xt_hi[p][:, :, :], misc[1][:, :].rearrange("p (c t) -> p c t", c=DC), ACT.Copy).then_inc(act_xt, 1)
                    if h == 1 and proj.exists() and proj.cross:
                        eng.wait_ge(pe_ct, c.count(1, 2 - B, 1))
                        a.activation(ct_hi[p][:, :, :], misc[2][:, :].rearrange("p (c t) -> p c t", c=DC), ACT.Copy).then_inc(act_ct, 1)
                    if h == 2 and now.exists():
                        minus_max(1, 0)
                    if h == 2 and fin.exists():
                        from_values(-1, G - 1)
                    if h == 4 and proj.exists():
                        if proj.is_number(0):
                            eng.wait_ge(ld_qk_bias, 64)
                        project("q", 1, pe_q, act_q)
                    if h == 6 and proj.exists():
                        project("k", 2, pe_k, act_k)
                    if h == 7 and now.exists():
                        from_values(0, 0)
                    if h == 9 and fin.exists():
                        eng.wait_ge(pe_ot, c.count(1, -1, 1))
                        wait(eng, pe_wo, c.count(1, -2, 1))
                        a.activation(ot_hi[:, :, :], misc[1][:, :].rearrange("p (c t) -> p c t", c=DC), ACT.Copy).then_inc(act_ot, 1)
                    if h == 11 and now.exists():
                        from_values(0, 1)
                    if h == 12 and smax.exists():
                        minus_max(0, 1)
                    if h == 13 and done.exists():
                        eng.wait_ge(pool_shift, c.count(1, -2, 1))
                        for t in range(ST):
                            last = a.activation(z[j][:, t, :], y[j][:, t, :], ACT.Identity, scale=rstd[j][:, t:t + 1],
                                                bias=shift[j][:, t:t + 1])
                        last.then_inc(act_z, 1)
                    if h == 15 and now.exists():
                        from_values(0, 2)

            run_cycles(eng, cycle)

        @block.vector
        def _(eng):
            v = nc.vector

            def split(k):
                n = names[k]
                eng.wait_ge(w_halved, k + 1)
                for i in range(DC):
                    hi = w_hi[n][:, i:i + 1, :].bitcast(F32)
                    lo = w_lo[n][:, i:i + 1, :]
                    src = staged[k][:, i:i + 1, :]
                    if n[1] in "qk":
                        hi = hi.rearrange("p a (c g d) -> p a c g d", c=DC, d=HD)[:, 0]
                        lo = lo.rearrange("p a (c g d) -> p a c g d", c=DC, d=HD)[:, 0]
                        src = by_head(src, n)[:, 0]
                    last = v.tensor_tensor(lo, src, hi, ALU.subtract)
                last.then_inc(w_split, 1)

            v.memset(k_stack[0][:, :, :].bitcast(F32), 0.0).then_inc(zeroed[0], 1)
            for k in range(2):
                v.memset(v_aug[k][:, :, :, :], 1.0)
            for k in range(4):
                split(k)

            def cycle(c):
                proj, smax, now, fin = (c.item(n) for n in (2, 1, 0, -1))
                p, s = proj.parity, smax.parity
                if c.is_number(-2):
                    v.memset(k_stack[1][:, :, :].bitcast(F32), 0.0).then_inc(zeroed[1], 1)
                for k in range(4):
                    if c.is_number(k):
                        split(4 + k)

                def divide(n, pair):
                    eng.wait_ge(pe_tr, c.count(2, n, pair + 1))
                    got = misc[0][:, :].rearrange("p (k w) -> p k w", w=VW)
                    v.reciprocal(inv_sum[:, :], got[:, :, HD]).then_inc(dve_inv, 1)
                    eng.wait_ge(dve_inv, c.count(2, n, pair + 1))
                    wait(eng, pe_ot, c.count(1, n, 0))
                    for t in range(ST):
                        last = v.tensor_tensor(
                            heads[:, t, pair * P:(pair + 1) * P].rearrange("p (k d) -> p k d", d=HD),
                            got[:, 8 * t:8 * t + 8, 0:HD],
                            inv_sum[:, 8 * t:8 * t + 8].unsqueeze(2).to_broadcast([P, 8, HD]), ALU.mult)
                    last.then_inc(dve_tr, 1)

                def low_part(q, bk, ready, fine):
                    w = "c" if proj.cross else "s"
                    eng.wait_ge(ready, c.count(1, 2, 1))
                    if q == "q" and not proj.is_number(0):
                        prev = c.item(1)
                        eng.wait_ge(bounced[prev.parity], prev.of_parity(64, 64))
                    for i in range(DC):
                        last = v.scalar_tensor_tensor(
                            out=proj_lo[q][:, i, :], in0=misc[bk][:, i * S:(i + 1) * S],
                            scalar=qk_bias[w + q][:, i:i + 1], in1=proj_hi[q][:, i, :].bitcast(F32),
                            op0=ALU.add, op1=ALU.subtract)
                    last.then_inc(fine, 1)

                for h in range(H):
                    if smax.exists():
                        eng.wait_ge(pe_s, c.count(H, 1, h + 1))
                        if smax.cross:
                            v.tensor_reduce(maxima[s][:, :, h], s_bank[h % 2][:, :].rearrange("p (q k) -> p q k", q=ST),
                                            axis=AX.X, op=ALU.max).then_inc(dve_max, 1)
                        else:
                            v.tensor_reduce(maxima3[s][:, :, h], s_bank[h % 2][:, 0:3 * P].rearrange("p (q k) -> p q k", q=3),
                                            axis=AX.X, op=ALU.max).then_inc(dve_max, 1)
                        if h % (H // 2) == H // 2 - 1 and not smax.cross:
                            hs = slice(h + 1 - H // 2, h + 1)
                            eng.wait_ge(dve_max, c.count(H, 1, h + 1))
                            v.tensor_copy(maxima[s][:, 0, hs], maxima3[s][:, 0, hs])
                            v.tensor_tensor(maxima[s][:, 1, hs], maxima3[s][:, 1, hs], maxima3[s][:, 2, hs],
                                            ALU.max).then_inc(dve_joined, 1)
                    if h == 1 and proj.exists():
                        eng.wait_ge(act_xt, c.count(1, 2, 1))
                        wait(eng, pe_v, c.count(1, 0, 1))
                        v.tensor_tensor(xt_lo[p][:, :, :], misc[1][:, :].rearrange("p (c t) -> p c t", c=DC),
                                        xt_hi[p][:, :, :].bitcast(F32), ALU.subtract).then_inc(dve_xt, 1)
                    if h == 2 and proj.exists() and proj.cross:
                        eng.wait_ge(act_ct, c.count(1, 2 - B, 1))
                        v.tensor_tensor(ct_lo[p][:, :, :], misc[2][:, :].rearrange("p (c t) -> p c t", c=DC),
                                        ct_hi[p][:, :, :].bitcast(F32), ALU.subtract).then_inc(dve_ct, 1)
                    if h == 5 and proj.exists():
                        low_part("q", 1, act_q, dve_q)
                    if h == 6 and fin.exists():
                        divide(-1, 1)
                    if h == 7 and proj.exists():
                        low_part("k", 2, act_k, dve_k)
                    if h == 10 and fin.exists():
                        eng.wait_ge(act_ot, c.count(1, -1, 1))
                        wait(eng, pe_wo, c.count(1, -2, 1))
                        v.tensor_tensor(ot_lo[:, :, :], misc[1][:, :].rearrange("p (c t) -> p c t", c=DC),
                                        ot_hi[:, :, :].bitcast(F32), ALU.subtract).then_inc(dve_ot, 1)
                    if h == 11 and smax.exists():
                        if smax.is_number(0):
                            eng.wait_ge(ld_rows, 12 * 16)
                        bv = row["cv" if smax.cross else "sv"]
                        eng.wait_ge(pe_v, c.count(1, 1, 1))
                        wait(eng, pe_av, c.count(G, 0, 0))
                        for t in range(ST):
                            last = v.tensor_tensor(v_aug[s][:, t, :, 0:HD],
                                                   misc[2][:, t * D:(t + 1) * D].rearrange("p (h d) -> p h d", d=HD),
                                                   bv[:, :].rearrange("p (h d) -> p h d", d=HD), ALU.add)
                        last.then_inc(dve_v, 1)
                    if fin.exists():
                        k = fin.parity
                        if h == 13:
                            eng.wait_ge(pe_wo, c.count(1, -1, 1))
                            eng.wait_ge(pool_res, c.count(1, -1, 1))
                            wait(eng, act_z, c.count(1, -3, 1))
                            v.tensor_tensor(y[k][:, :, :], misc[1][:, :].rearrange("p (t d) -> p t d", t=ST),
                                            x_res[k][:, :, :], ALU.add).then_inc(dve_y, 1)
                        if h == 14:
                            eng.wait_ge(dve_y, c.count(1, -1, 1))
                            for t in range(ST):
                                last = v.bn_stats(stats[:, t, :], y[k][:, t, :])
                            last.then_inc(dve_stats, 1)
                        if h == 15:
                            eng.wait_ge(dve_stats, c.count(1, -1, 1))
                            v.tensor_copy(counted[:, :], stats[:, :, 0])
                            for t in range(ST):
                                last = v.bn_aggr(mean_var[k][:, t, :], stats[:, t, :])
                            last.then_inc(dve_mean, 1)
                    if h == 14 and now.exists():
                        divide(0, 0)

            run_cycles(eng, cycle)

        @block.tensor
        def _(eng):
            pe = nc.tensor
            eng.wait_ge(const_made, 6)

            def split_product(dst, left_hi, left_lo, right_hi, right_lo):
                for i in range(DC):
                    for n, (l, r) in enumerate(((left_hi, right_hi), (left_hi, right_lo), (left_lo, right_hi))):
                        last = pe.matmul(dst, l(i), r(i), start=(i == 0 and n == 0), stop=(i == DC - 1 and n == 2))
                return last

            def cycle(c):
                proj, smax, now, fin = (c.item(n) for n in (2, 1, 0, -1))
                j = c.parity
                p, s = proj.parity, smax.parity

                def values(n, g):
                    it = c.item(n)
                    k = it.parity
                    eng.wait_ge(act_exp, c.count(H, n, GH * (g + 1)))
                    wait(eng, act_av, c.count(G, n, g))
                    if g == 0:
                        eng.wait_ge(dve_v, c.count(1, n, 1))
                    for t in range(ST):
                        q0 = P * t if not it.cross else 0
                        for hh in range(GH):
                            last = pe.matmul(av_bank[VW * hh:VW * hh + VW, q0:S], v_aug[k][:, t, GH * g + hh, :],
                                             probs[g % 2][:, hh, t, 0:S - q0] if t else probs[g % 2][:, hh, t, :],
                                             start=(t == 0), stop=(t == ST - 1), tile_position=(0, VW * hh))
                    last.then_inc(pe_av, 1)

                def max_rows(n, half, free, count):
                    it = c.item(n)
                    eng.wait_ge(dve_max, c.count(H, n, H // 2 * (half + 1)))
                    if not it.cross:
                        eng.wait_ge(dve_joined, c.count(2, n, half + 1))
                    wait(eng, free, count)
                    for t in range(ST):
                        last = pe.transpose(misc[0][0:H // 2, t * P:(t + 1) * P],
                                            maxima[it.parity][:, t, half * H // 2:(half + 1) * H // 2], ident[:, :])
                    last.then_inc(pe_mt, 1)

                def head_rows(n, pair, count):
                    eng.wait_ge(act_av, c.count(G, n, 2 * pair + 2))
                    wait(eng, act_m, count)
                    wait(eng, dve_tr, c.count(2, n, pair))
                    for t in range(ST):
                        for gi in range(2):
                            last = pe.transpose(misc[0][:, (2 * t + gi) * P:(2 * t + gi + 1) * P],
                                                heads_t[2 * pair + gi][:, t * P:(t + 1) * P], ident[:, :])
                    last.then_inc(pe_tr, 1)

                for h in range(H):
                    if smax.exists():
                        if h % (H // 2) == 0:
                            eng.wait_ge(stacked[h // (H // 2)][s], smax.of_parity(80, 80))
                        wait(eng, dve_max, c.count(H, 1, h - 1))
                        qs, ks, sbk = q_stack[s], k_stack[s], s_bank[h % 2]
                        if smax.cross:
                            for t in range(ST):
                                last = pe.matmul(sbk[:, t * S:(t + 1) * S], qs[0:MROW, h, t * P:(t + 1) * P],
                                                 ks[0:MROW, h, :], start=True, stop=True)
                        else:
                            pe.matmul(sbk[:, 0:P], qs[0:MROW, h, 0:P], ks[0:MROW, h, 0:P], start=True, stop=False)
                            pe.matmul(sbk[:, 0:P], ident_bf[:, :], mask_qk[:, :], start=False, stop=True)
                            pe.matmul(sbk[:, P:3 * P], qs[0:MROW, h, P:S], ks[0:MROW, h, :], start=True, stop=False)
                            last = pe.matmul(sbk[:, 2 * P:3 * P], ident_bf[:, :], mask_qk[:, :], start=False, stop=True)
                        last.then_inc(pe_s, 1)
                    if now.exists():
                        if h % (H // 2) == 0:
                            if now.is_number(0) or now.is_number(1):
                                eng.wait_ge(ones_placed, 16 * (j + 1))
                            eng.wait_ge(m_placed[h // (H // 2)][j], now.of_parity(16, 16))
                        wait(eng, act_exp, c.count(H, 0, h - 1))
                        qs, ks, tbk = q_stack[j], k_stack[j], t_bank[h % 2]
                        if now.cross:
                            for t in range(ST):
                                last = pe.matmul(tbk[:, t * S:(t + 1) * S], ks[:, h, t * P:(t + 1) * P], qs[:, h, :],
                                                 start=True, stop=True)
                        else:
                            pe.matmul(tbk[:, 0:S], ks[:, h, 0:P], qs[:, h, :], start=True, stop=False)
                            pe.matmul(tbk[:, 0:P], ident_bf[:, :], mask_kq[:, :], start=False, stop=True)
                            pe.matmul(tbk[:, S:S + P], ks[:, h, P:S], qs[:, h, P:S], start=True, stop=False)
                            last = pe.matmul(tbk[:, S:S + P], ident_bf[:, :], mask_kq[:, :], start=False, stop=True)
                        last.then_inc(pe_t, 1)
                    w = "c" if proj.cross else "s"
                    kv_hi, kv_lo = (ct_hi[p], ct_lo[p]) if proj.cross else (xt_hi[p], xt_lo[p])
                    if h == 0 and proj.exists():
                        eng.wait_ge(ld_x[p], proj.of_parity(16, 16))
                        wait(eng, dve_y, c.count(1, -2, 1))
                        for i in range(DC):
                            for t in range(ST):
                                last = pe.transpose(misc[1][:, i * S + t * P:i * S + (t + 1) * P],
                                                    x_in[p][:, t, i * P:(i + 1) * P], ident[:, :])
                        last.then_inc(pe_xt, 1)
                        if proj.cross:
                            eng.wait_ge(ld_c[p], proj.of_cross(16, 16))
                            wait(eng, dve_v, c.count(1, 0, 1))
                            for i in range(DC):
                                for t in range(ST):
                                    last = pe.transpose(misc[2][:, i * S + t * P:i * S + (t + 1) * P],
                                                        c_in[p][:, t, i * P:(i + 1) * P], ident[:, :])
                            last.then_inc(pe_ct, 1)
                    if h == 1 and now.exists():
                        max_rows(0, 1, dve_tr, c.count(2, -1, 1))
                    if h == 1 and fin.exists():
                        values(-1, G - 1)
                    if h in (2, 3) and proj.exists():
                        if proj.is_number(0) or proj.is_number(B):
                            eng.wait_ge(w_split, 4 if proj.is_number(0) else 8)
                        i = h - 2
                        if i == 0:
                            eng.wait_ge(dve_xt, c.count(1, 2, 1))
                        last = split_product(
                            misc[1][:, i * S:(i + 1) * S],
                            lambda a: w_hi[w + "q"][:, a, i * P:(i + 1) * P], lambda a: w_lo[w + "q"][:, a, i * P:(i + 1) * P],
                            lambda a: xt_hi[p][:, a, :], lambda a: xt_lo[p][:, a, :])
                        if i == DC - 1:
                            last.then_inc(pe_q, 1)
                    if h in (4, 5) and proj.exists():
                        i = h - 4
                        if i == 0:
                            if proj.cross:
                                eng.wait_ge(dve_ct, c.count(1, 2 - B, 1))
                            wait(eng, dve_v, c.count(1, 0, 1))
                        last = split_product(
                            misc[2][:, i * S:(i + 1) * S],
                            lambda a: w_hi[w + "k"][:, a, i * P:(i + 1) * P], lambda a: w_lo[w + "k"][:, a, i * P:(i + 1) * P],
                            lambda a: kv_hi[:, a, :], lambda a: kv_lo[:, a, :])
                        if i == DC - 1:
                            last.then_inc(pe_k, 1)
                    if h == 5 and fin.exists():
                        head_rows(-1, 1, c.count(2, 0, 2))
                    if h == 6 and now.exists():
                        values(0, 0)
                    if h == 8 and fin.exists():
                        eng.wait_ge(dve_tr, c.count(2, -1, 2))
                        wait(eng, dve_q, c.count(1, 2, 1))
                        wait(eng, dve_y, c.count(1, -2, 1))
                        for i in range(DC):
                            for t in range(ST):
                                last = pe.transpose(misc[1][:, i * S + t * P:i * S + (t + 1) * P],
                                                    heads[:, t, i * P:(i + 1) * P], ident[:, :])
                        last.then_inc(pe_ot, 1)
                    if h in (8, 9) and smax.exists():
                        w = "c" if smax.cross else "s"
                        kv_hi, kv_lo = (ct_hi[s], ct_lo[s]) if smax.cross else (xt_hi[s], xt_lo[s])
                        t = h - 8
                        if t == 0:
                            wait(eng, dve_k, c.count(1, 2, 1))
                            wait(eng, dve_v, c.count(1, 0, 1))
                        last = split_product(
                            misc[2][:, t * D:(t + 1) * D],
                            lambda a: kv_hi[:, a, t * P:(t + 1) * P], lambda a: kv_lo[:, a, t * P:(t + 1) * P],
                            lambda a: w_hi[w + "v"][:, a, :], lambda a: w_lo[w + "v"][:, a, :])
                        if t == ST - 1:
                            last.then_inc(pe_v, 1)
                    if h == 10 and now.exists():
                        values(0, 1)
                    if h == 11 and smax.exists():
                        max_rows(1, 0, dve_tr, c.count(2, -1, 2))
                    if h in (11, 12) and fin.exists():
                        w = "c" if fin.cross else "s"
                        t = h - 11
                        if t == 0:
                            eng.wait_ge(dve_ot, c.count(1, -1, 1))
                        last = split_product(
                            misc[1][:, t * D:(t + 1) * D],
                            lambda a: ot_hi[:, a, t * P:(t + 1) * P], lambda a: ot_lo[:, a, t * P:(t + 1) * P],
                            lambda a: w_hi[w + "o"][:, a, :], lambda a: w_lo[w + "o"][:, a, :])
                        if t == ST - 1:
                            last.then_inc(pe_wo, 1)
                    if h == 13 and now.exists():
                        head_rows(0, 0, c.count(2, 1, 1))
                    if h == 14 and now.exists():
                        values(0, 2)

            run_cycles(eng, cycle)


E, FF, K = 8, 1024, 2
T = B * S
NT = T // P
BLK = 512
BT = BLK // P
FJ = FF // P
NBLK = (T * K + E * (BLK - 1)) // BLK
LOGB = BLK.bit_length() - 1
LAG = 2
WCOLS = DC * FF + FJ * D


def moe_program(nc, x2, rw, rb, w1, b1, w2, b2, g3, b3, out):
    sorted_x = nc.dram_tensor("sorted_x", (NBLK * BLK, D), F32, kind="Internal").ap()
    sorted_y = nc.dram_tensor("sorted_y", (NBLK * BLK, D), F32, kind="Internal").ap()
    b1_cols = nc.dram_tensor("b1_cols", (P, E, FJ), F32, kind="Internal").ap()
    outer = ExitStack()
    with outer:
        def keep(name, shape, dt=F32):
            return outer.enter_context(nc.sbuf_tensor(name, shape, dt))
        x2_sb = keep("x2_sb", [P, NT, D])
        slot = [keep(f"slot{k}", [P, NT], I32) for k in range(K)]
        weight = [keep(f"weight{k}", [P, NT]) for k in range(K)]
        expert_of = keep("expert_of", [1, NBLK], I32)
        ident = keep("ident_m", [P, P])
        route(nc, x2, rw, rb, b1, x2_sb, slot, weight, expert_of, ident, sorted_x, b1_cols)
        experts(nc, w1, w2, b2, expert_of, ident, sorted_x, sorted_y, b1_cols)
        combine(nc, x2_sb, slot, weight, sorted_y, g3, b3, out)


def route(nc, x2, rw, rb, b1, x2_sb, slot, weight, expert_of, ident, sorted_x, b1_cols):
    stack = ExitStack()
    with stack:
        def sb(name, shape, dt=F32):
            return stack.enter_context(nc.sbuf_tensor(name, shape, dt))

        def sem(name):
            return stack.enter_context(nc.semaphore(name))

        GT = 4
        NG = NT // GT
        rw_sb = sb("rw_sb", [P, DC, E])
        rb_sb = sb("rb_sb", [E, 1])
        b1_rows = sb("b1_rows", [E * FJ, P])
        b1_turned = sb("b1_turned", [P, E * FJ])
        zero_rows = sb("zero_rows", [P, 8 * D])
        x2t = [sb(f"x2t{k}", [P, DC, GT * P]) for k in range(2)]
        logits_t = [sb(f"logits_t{k}", [E, GT * P]) for k in range(2)]
        lg = sb("lg", [P, NT, E])
        prob = sb("prob", [P, NT, E])
        rest = sb("rest", [P, NT, E])
        top = [sb(f"top{k}", [P, NT]) for k in range(K)]
        pick = [sb(f"pick{k}", [P, NT]) for k in range(K)]
        chosen = [sb(f"chosen{k}", [P, NT, E]) for k in range(K)]
        both = sb("both", [P, NT, E], BF16)
        score = sb("score", [P, NT, E])
        rank_w = sb("rank_w", [P, E])
        mx = sb("mx", [P, NT])
        sm = sb("sm", [P, NT])
        scan = [sb(f"scan{k}", [P, NT, E]) for k in range(2)]
        totals = sb("totals", [P, NT, E])
        place = sb("place", [P, NT, E])
        cap = sb("cap", [P, E])
        cap_i = sb("cap_i", [P, E], I32)
        ends = [sb(f"ends{k}", [P, E]) for k in range(2)]
        starts = sb("starts", [P, E])
        slot_f = [sb(f"slot_f{k}", [P, NT]) for k in range(K)]
        tri = sb("tri", [P, P], BF16)
        tri_f = sb("tri_f", [P, P])
        ones = sb("ones", [P, P], BF16)
        blk_at = sb("blk_at", [1, NBLK, E])
        past = sb("past", [1, NBLK, E])
        count_f = sb("count_f", [1, NBLK])

        def bank(name):
            return stack.enter_context(nc.psum_tensor(name, [P, 512], F32))
        xt_bank = [[bank(f"xt_bank{k}{c}") for c in range(DC)] for k in range(2)]
        lt_bank, lg_bank = bank("lt_bank"), bank("lg_bank")
        prefix_bank, total_bank = bank("prefix_bank"), bank("total_bank")

        ld, ldx, const, zero_made, zeroed = sem("r_ld"), sem("r_ldx"), sem("r_const"), sem("r_zero"), sem("r_zeroed")
        chain_p = sem("r_chain_p")
        xt_done, xt_out, lt_done, lt_out, lg_done, lg_out = (sem(f"r_{n}") for n in ("xt", "xto", "lt", "lto", "lg", "lgo"))
        centred, exped, both_done, counted, slots_done = (sem(f"r_{n}") for n in ("cen", "exp", "both", "cnt", "slot"))
        gap_c, gap_e = sem("r_gap_c"), sem("r_gap_e")
        scattered, b1t_done, b1t_out, b1_stored = sem("r_scat"), sem("r_b1t"), sem("r_b1o"), sem("r_b1s")
        dv = sem("r_dv")

        block = stack.enter_context(nc.Block())

        @block.sync
        def _(eng):
            for q in range(4):
                eng.dma_start(x2_sb[:, q * NT // 4:(q + 1) * NT // 4, :].rearrange("p (b t) d -> p b t d", t=ST),
                              x2[q * B // 4:(q + 1) * B // 4].rearrange("b p t d -> p b t d")).then_inc(ldx, 16)
            eng.dma_start(rw_sb[:, :, :], rw.rearrange("(c p) e -> p c e", p=P)).then_inc(ld, 16)
            eng.dma_start(rb_sb[:, :], rb.rearrange("(e a) -> e a", a=1), allow_slow_non_contiguous=True).then_inc(ld, 16)
            eng.dma_start(b1_rows[:, :], b1.rearrange("e (j p) -> (e j) p", p=P)).then_inc(ld, 16)
            eng.wait_ge(zero_made, 1)
            rows = NBLK * BLK
            per = 8 * P
            for r in range(0, rows, per):
                n = min(per, rows - r) // P
                eng.dma_start(sorted_x[r:r + n * P, :].rearrange("(p n) d -> p n d", n=n),
                              zero_rows[:, 0:n * D].rearrange("p (n d) -> p n d", n=n)).then_inc(zeroed, 16)
            eng.wait_ge(b1t_out, 1)
            eng.dma_start(b1_cols.rearrange("p e j -> p (e j)"), b1_turned[:, :]).then_inc(b1_stored, 16)
            eng.wait_ge(b1_stored, 16)

        @block.gpsimd
        def _(eng):
            g = nc.gpsimd
            g.memset(ident[:, :], 0.0).then_inc(chain_p, 1)
            g.memset(tri_f[:, :], 0.0).then_inc(chain_p, 1)
            g.memset(ones[:, :], 1.0).then_inc(const, 1)
            g.iota(blk_at[:, :, :], [[BLK, NBLK], [0, E]], base=0, channel_multiplier=0,
                   allow_small_or_imprecise_dtypes=True).then_inc(const, 1)
            g.iota(rank_w[:, :], [[-1, E]], base=E, channel_multiplier=0,
                   allow_small_or_imprecise_dtypes=True).then_inc(const, 1)
            eng.wait_ge(chain_p, 2)
            g.affine_select(out=ident[:, :], in_=ident[:, :], compare_op=ALU.not_equal, fill=1.0, base=0,
                            pattern=[[-1, P]], channel_multiplier=1).then_inc(const, 1)
            g.affine_select(out=tri_f[:, :], in_=tri_f[:, :], compare_op=ALU.is_ge, fill=1.0, base=0,
                            pattern=[[-1, P]], channel_multiplier=1).then_inc(chain_p, 1)
            eng.wait_ge(chain_p, 3)
            g.tensor_copy(tri[:, :], tri_f[:, :]).then_inc(const, 1)
            n_zero = -(-NBLK * BLK // (8 * P))
            eng.wait_ge(slots_done, 1)
            eng.wait_ge(zeroed, 16 * n_zero)
            for i in range(NT):
                for k in range(K):
                    g.indirect_dma_start(sorted_x, bass.IndirectOffsetOnAxis(ap=slot[k][:, i:i + 1], axis=0),
                                         x2_sb[:, i, :], None, bounds_check=NBLK * BLK - 1).then_inc(scattered, 16)
            eng.wait_ge(scattered, 16 * NT * K)

        @block.scalar
        def _(eng):
            a = nc.scalar
            for q in range(NG):
                eng.wait_ge(xt_done, q + 1)
                for c in range(DC):
                    last = a.activation(x2t[q % 2][:, c, :], xt_bank[q % 2][c][:, :], ACT.Copy)
                last.then_inc(xt_out, 1)
            eng.wait_ge(b1t_done, 1)
            a.activation(b1_turned[:, :], lt_bank[:, 0:E * FJ], ACT.Copy).then_inc(b1t_out, 1)
            eng.wait_ge(centred, 1)
            a.activation(prob[:, :, :], prob[:, :, :], ACT.Exp).then_inc(exped, 1)
            eng.wait_ge(gap_c, 1)
            a.activation(weight[1][:, :], weight[1][:, :], ACT.Exp).then_inc(gap_e, 1)

        @block.tensor
        def _(eng):
            pe = nc.tensor
            eng.wait_ge(const, 5)
            eng.wait_ge(ld, 48)
            eng.wait_ge(ldx, 64)
            for q in range(NG):
                wait(eng, xt_out, q - 1)
                for c in range(DC):
                    for i in range(GT):
                        last = pe.transpose(xt_bank[q % 2][c][:, i * P:(i + 1) * P],
                                            x2_sb[:, q * GT + i, c * P:(c + 1) * P], ident[:, :])
                last.then_inc(xt_done, 1)
                for r in ([q - 1] if q else []) + ([q] if q == NG - 1 else []):
                    eng.wait_ge(xt_out, r + 1)
                    wait(eng, lt_out, r)
                    for c in range(DC):
                        last = pe.matmul(lt_bank[0:E, :], rw_sb[:, c, :], x2t[r % 2][:, c, :],
                                         start=(c == 0), stop=(c == DC - 1))
                    last.then_inc(lt_done, 1)
                    eng.wait_ge(lt_out, r + 1)
                    for i in range(GT):
                        last = pe.transpose(lg_bank[:, (r * GT + i) * E:(r * GT + i + 1) * E],
                                            logits_t[r % 2][:, i * P:(i + 1) * P], ident[0:E, 0:E])
                    last.then_inc(lg_done, 1)
            pe.transpose(lt_bank[:, 0:E * FJ], b1_rows[:, :], ident[0:E * FJ, 0:E * FJ]).then_inc(b1t_done, 1)
            eng.wait_ge(both_done, 1)
            every = both[:, :, :].rearrange("p n e -> p (n e)")
            pe.matmul(prefix_bank[:, 0:NT * E], tri[:, :], every, start=True, stop=True)
            pe.matmul(total_bank[:, 0:NT * E], ones[:, :], every, start=True, stop=True).then_inc(counted, 1)

        @block.vector
        def _(eng):
            v = nc.vector
            n_done = [0]

            def then(ins):
                n_done[0] += 1
                ins.then_inc(dv, 1)
                eng.wait_ge(dv, n_done[0])

            v.memset(zero_rows[:, :], 0.0).then_inc(zero_made, 1)
            eng.wait_ge(ld, 48)
            for q in range(NG):
                eng.wait_ge(lt_done, q + 1)
                v.tensor_scalar(logits_t[q % 2][:, :], lt_bank[0:E, :], rb_sb[:, 0:1], None, ALU.add).then_inc(lt_out, 1)
            eng.wait_ge(const, 5)
            eng.wait_ge(lg_done, NG)
            wide = [P, NT, E]
            then(v.tensor_copy(lg[:, :, :].rearrange("p n e -> p (n e)"), lg_bank[:, 0:NT * E]))
            then(v.tensor_reduce(mx[:, :], lg[:, :, :], axis=AX.X, op=ALU.max))
            v.tensor_tensor(prob[:, :, :], lg[:, :, :], mx[:, :].unsqueeze(2).to_broadcast(wide), ALU.subtract).then_inc(centred, 1)
            eng.wait_ge(exped, 1)
            then(v.tensor_reduce(sm[:, :], prob[:, :, :], axis=AX.X, op=ALU.add))
            then(v.reciprocal(sm[:, :], sm[:, :]))
            then(v.tensor_tensor(prob[:, :, :], prob[:, :, :], sm[:, :].unsqueeze(2).to_broadcast(wide), ALU.mult))
            src = prob
            for k in range(K):
                then(v.tensor_reduce(top[k][:, :], src[:, :, :], axis=AX.X, op=ALU.max))
                then(v.tensor_tensor(score[:, :, :], src[:, :, :], top[k][:, :].unsqueeze(2).to_broadcast(wide), ALU.is_ge))
                then(v.tensor_tensor(score[:, :, :], score[:, :, :], rank_w[:, :].unsqueeze(1).to_broadcast(wide), ALU.mult))
                then(v.tensor_reduce(pick[k][:, :], score[:, :, :], axis=AX.X, op=ALU.max))
                then(v.tensor_tensor(chosen[k][:, :, :], score[:, :, :], pick[k][:, :].unsqueeze(2).to_broadcast(wide), ALU.is_equal))
                if k == 0:
                    then(v.scalar_tensor_tensor(out=rest[:, :, :], in0=chosen[0][:, :, :], scalar=-2.0, in1=prob[:, :, :],
                                                op0=ALU.mult, op1=ALU.add))
                    src = rest
            v.tensor_tensor(both[:, :, :], chosen[0][:, :, :], chosen[1][:, :, :], ALU.add).then_inc(both_done, 1)
            v.tensor_tensor(weight[1][:, :], top[1][:, :], top[0][:, :], ALU.subtract).then_inc(gap_c, 1)
            eng.wait_ge(gap_e, 1)
            then(v.tensor_scalar(sm[:, :], weight[1][:, :], 1.0, None, ALU.add))
            then(v.reciprocal(weight[0][:, :], sm[:, :]))
            then(v.tensor_tensor(weight[1][:, :], weight[1][:, :], weight[0][:, :], ALU.mult))
            eng.wait_ge(counted, 1)
            then(v.tensor_copy(totals[:, :, :].rearrange("p n e -> p (n e)"), total_bank[:, 0:NT * E]))
            at, step = totals, 1
            n = 0
            while step < NT:
                to = scan[n % 2]
                v.tensor_copy(to[:, 0:step, :], at[:, 0:step, :])
                then(v.tensor_tensor(to[:, step:NT, :], at[:, step:NT, :], at[:, 0:NT - step, :], ALU.add))
                at, step, n = to, step * 2, n + 1
            then(v.tensor_scalar(cap_i[:, :], at[:, NT - 1, :], float(BLK - 1), None, ALU.add))
            then(v.tensor_scalar(cap_i[:, :], cap_i[:, :], LOGB, LOGB, ALU.logical_shift_right, ALU.logical_shift_left))
            then(v.tensor_copy(cap[:, :], cap_i[:, :]))
            end, step, m = cap, 1, 0
            while step < E:
                to = ends[m % 2]
                v.tensor_copy(to[:, 0:step], end[:, 0:step])
                then(v.tensor_tensor(to[:, step:E], end[:, step:E], end[:, 0:E - step], ALU.add))
                end, step, m = to, step * 2, m + 1
            then(v.tensor_tensor(starts[:, :], end[:, :], cap[:, :], ALU.subtract))
            then(v.tensor_tensor(place[:, :, :], at[:, :, :], totals[:, :, :], ALU.subtract))
            then(v.tensor_tensor(place[:, :, :].rearrange("p n e -> p (n e)"), prefix_bank[:, 0:NT * E],
                                 place[:, :, :].rearrange("p n e -> p (n e)"), ALU.add))
            then(v.tensor_tensor(place[:, :, :], place[:, :, :], starts[:, :].unsqueeze(1).to_broadcast(wide), ALU.add))
            for k in range(K):
                then(v.tensor_tensor(score[:, :, :], place[:, :, :], chosen[k][:, :, :], ALU.mult))
                then(v.tensor_reduce(slot_f[k][:, :], score[:, :, :], axis=AX.X, op=ALU.add))
                then(v.tensor_copy(slot[k][:, :], slot_f[k][:, :]))
            then(v.tensor_tensor(past[:, :, :], blk_at[:, :, :], end[0:1, :].unsqueeze(1).to_broadcast([1, NBLK, E]), ALU.is_ge))
            then(v.tensor_reduce(count_f[:, :], past[:, :, :], axis=AX.X, op=ALU.add))
            v.tensor_scalar(expert_of[:, :], count_f[:, :], float(E - 1), None, ALU.min).then_inc(slots_done, 1)


class Turn:

    def __init__(self, i, pair, parity):
        self.i, self.pair, self.parity = i, pair, parity

    def count(self, per, n, extra):
        at = per * (2 * self.pair + self.parity + n) + extra
        return min(at, per * NBLK) if self.i is None else affine(self.i, 2 * per, at)

    def of_parity(self, per, extra=0):
        return affine(self.i, per, per * self.pair + extra)

    def block(self, n):
        at = 2 * self.pair + self.parity + n
        return Turn(self.i, at // 2, at % 2)

    @property
    def number(self):
        return affine(self.i, 2, 2 * self.pair + self.parity)

    def exists(self):
        return self.i is not None or 0 <= self.number < NBLK


def run_blocks(eng, body):
    end = (NBLK - 2) // 2
    for n in range(-2, 2):
        body(Turn(None, n // 2, n % 2))
    with eng.Fori(0, end - 1) as i:
        body(Turn(i, 1, 0))
        body(Turn(i, 1, 1))
    for n in range(2 * end, NBLK + 1):
        body(Turn(None, n // 2, n % 2))


def experts(nc, w1, w2, b2, expert_of, ident, sorted_x, sorted_y, b1_cols):
    stack = ExitStack()
    with stack:
        def sb(name, shape, dt=F32):
            return stack.enter_context(nc.sbuf_tensor(name, shape, dt))

        def sem(name):
            return stack.enter_context(nc.semaphore(name))

        def two(make, name, *a):
            return [make(f"{name}{k}", *a) for k in range(2)]

        HS = 4
        PIECE = WCOLS // FJ
        w_raw = sb("w_raw", [P, WCOLS])
        wh = two(sb, "wh", [P, WCOLS], F32R)
        wl = two(sb, "wl", [P, WCOLS], F32R)
        x_rows = two(sb, "x_rows", [P, BT, D])
        xh = two(sb, "xh", [P, DC, BLK], F32R)
        xl = two(sb, "xl", [P, DC, BLK], F32R)
        b1_sb = two(sb, "b1_sb", [P, FJ])
        b2_sb = two(sb, "b2_sb", [P, D])
        h = [sb(f"h{k}", [P, BLK]) for k in range(2)]
        hh = [sb(f"hh{k}", [P, BLK], F32R) for k in range(HS)]
        hl = [sb(f"hl{k}", [P, BLK], F32R) for k in range(HS)]
        y_rows = sb("y_rows", [P, BT, D])

        def bank(name):
            return stack.enter_context(nc.psum_tensor(name, [P, 512], F32))
        h_bank = [bank(f"h_bank{k}") for k in range(2)]
        y_bank = [bank(f"y_bank{k}") for k in range(BT)]
        x_bank = [bank(f"x_bank{k}") for k in range(DC)]

        ld_w1, ld_w2 = two(sem, "m_ldw1"), two(sem, "m_ldw2")
        ld_x, ld_b1, ld_b2 = two(sem, "m_ldx"), two(sem, "m_ldb1"), two(sem, "m_ldb2")
        y_stored = sem("m_stored")
        pe_x, pe_h, pe_y = sem("m_pe_x"), sem("m_pe_h"), sem("m_pe_y")
        act_w, act_x, act_h = sem("m_act_w"), sem("m_act_x"), sem("m_act_h")
        dve_w, dve_x, dve_hh, dve_hl, dve_y = (sem(f"m_dve_{n}") for n in ("w", "x", "hh", "hl", "y"))

        block = stack.enter_context(nc.Block())

        def piece(t, k):
            return t[:, k * PIECE:(k + 1) * PIECE]

        @block.sync
        def _(eng):
            def expert(b):
                return eng.value_load(expert_of[0:1, bass.ds(b.number, 1)], min_val=0, max_val=E - 1)

            def cycle(c):
                far, near, now, was = (c.block(n) for n in (2, 1, 0, -1))
                if near.exists():
                    e = expert(near)
                    wait(eng, act_h, c.count(FJ, 0, 0))
                    eng.dma_start(b1_sb[near.parity][:, :], b1_cols[:, e, :]).then_inc(ld_b1[near.parity], 16)
                if now.exists():
                    e = expert(now)
                    wait(eng, dve_y, c.count(1, -1, 0))
                    eng.dma_start(b2_sb[now.parity][:, :], b2[e].partition_broadcast(P)).then_inc(ld_b2[now.parity], 16)
                if was.exists():
                    eng.wait_ge(dve_y, c.count(1, -1, 1))
                    eng.dma_start(sorted_y.rearrange("(n t p) d -> n p t d", p=P, t=BT)[was.number],
                                  y_rows[:, :, :]).then_inc(y_stored, 16)
                if far.exists():
                    e = expert(far)
                    wait(eng, dve_w, c.count(FJ, 1, FJ // 2))
                    eng.dma_start(w_raw[:, 0:DC * FF].rearrange("p (a f) -> p a f", a=DC),
                                  w1[e].rearrange("(a p) f -> p a f", p=P)).then_inc(ld_w1[far.parity], 16)
                    wait(eng, pe_x, c.count(1, 0, 1))
                    eng.dma_start(x_rows[far.parity][:, :, :],
                                  sorted_x.rearrange("(n t p) d -> n p t d", p=P, t=BT)[far.number]).then_inc(ld_x[far.parity], 16)
                    wait(eng, dve_w, c.count(FJ, 1, FJ))
                    eng.dma_start(w_raw[:, DC * FF:WCOLS].rearrange("p (j d) -> p j d", j=FJ),
                                  w2[e].rearrange("(j p) d -> p j d", p=P)).then_inc(ld_w2[far.parity], 16)
            run_blocks(eng, cycle)
            eng.wait_ge(y_stored, 16 * NBLK)

        @block.scalar
        def _(eng):
            a = nc.scalar

            def cycle(c):
                near, now = c.block(1), c.block(0)
                j2 = c.parity
                for j in range(FJ):
                    if now.exists():
                        if j == 0:
                            eng.wait_ge(ld_b1[j2], now.of_parity(16, 16))
                        eng.wait_ge(pe_h, c.count(FJ, 0, j + 1))
                        wait(eng, dve_hl, c.count(FJ, 0, j - 1))
                        a.activation(h[j % 2][:, :], h_bank[j % 2][:, :], ACT.Gelu,
                                     bias=b1_sb[j2][:, j:j + 1]).then_inc(act_h, 1)
                    if near.exists():
                        if j == 0:
                            eng.wait_ge(ld_w1[near.parity], near.of_parity(16, 16))
                            wait(eng, pe_h, c.count(FJ, 0, 0))
                        if j == FJ // 2:
                            eng.wait_ge(ld_w2[near.parity], near.of_parity(16, 16))
                            wait(eng, pe_y, c.count(FJ, 0, 0))
                        a.activation(piece(wh[near.parity], j), piece(w_raw, j), ACT.Copy).then_inc(act_w, 1)
                        if j == 3:
                            eng.wait_ge(pe_x, c.count(1, 1, 1))
                            for k in range(DC):
                                last = a.activation(xh[near.parity][:, k, :], x_bank[k][:, :], ACT.Copy)
                            last.then_inc(act_x, 1)
            run_blocks(eng, cycle)

        @block.vector
        def _(eng):
            v = nc.vector

            def cycle(c):
                near, now, was = c.block(1), c.block(0), c.block(-1)
                for j in range(FJ):
                    if now.exists():
                        eng.wait_ge(act_h, c.count(FJ, 0, j + 1))
                        wait(eng, pe_y, c.count(FJ, 0, j + 1 - HS))
                        v.tensor_copy(hh[j % HS][:, :], h[j % 2][:, :]).then_inc(dve_hh, 1)
                        eng.wait_ge(dve_hh, c.count(FJ, 0, j + 1))
                        v.tensor_tensor(hl[j % HS][:, :], h[j % 2][:, :], hh[j % HS][:, :].bitcast(F32),
                                        ALU.subtract).then_inc(dve_hl, 1)
                    if j == LAG and was.exists():
                        eng.wait_ge(pe_y, c.count(FJ, -1, FJ))
                        eng.wait_ge(ld_b2[was.parity], was.of_parity(16, 16))
                        wait(eng, y_stored, c.count(16, -1, 0))
                        for t in range(BT):
                            last = v.tensor_tensor(y_rows[:, t, :], y_bank[t][:, 0:D], b2_sb[was.parity][:, :], ALU.add)
                        last.then_inc(dve_y, 1)
                    if near.exists():
                        wait(eng, pe_h if j < FJ // 2 else pe_y, c.count(FJ, 0, 0))
                        eng.wait_ge(act_w, c.count(FJ, 1, j + 1))
                        v.tensor_tensor(piece(wl[near.parity], j), piece(w_raw, j), piece(wh[near.parity], j).bitcast(F32),
                                        ALU.subtract).then_inc(dve_w, 1)
                        if j == 3:
                            eng.wait_ge(act_x, c.count(1, 1, 1))
                            for k in range(DC):
                                last = v.tensor_tensor(xl[near.parity][:, k, :], x_bank[k][:, :],
                                                       xh[near.parity][:, k, :].bitcast(F32), ALU.subtract)
                            last.then_inc(dve_x, 1)
            run_blocks(eng, cycle)

        @block.tensor
        def _(eng):
            pe = nc.tensor

            def second(c, back, m):
                b = c.block(-back)
                w = [t[b.parity][:, DC * FF + m * D:DC * FF + (m + 1) * D] for t in (wh, wl)]
                eng.wait_ge(dve_hl, c.count(FJ, -back, m + 1))
                if m == 0:
                    wait(eng, dve_y, c.count(1, -1, 1))
                    eng.wait_ge(dve_w, c.count(FJ, 0, FJ))
                for t in range(BT):
                    ts = slice(t * P, (t + 1) * P)
                    for n, (l, r) in enumerate(((hh, w[0]), (hh, w[1]), (hl, w[0]))):
                        last = pe.matmul(y_bank[t][:, 0:D], l[m % HS][:, ts], r,
                                         start=(m == 0 and n == 0), stop=(m == FJ - 1 and n == 2))
                last.then_inc(pe_y, 1)

            def cycle(c):
                near, now, was = c.block(1), c.block(0), c.block(-1)
                p = c.parity
                for j in range(FJ):
                    if now.exists():
                        if j == 0:
                            eng.wait_ge(dve_w, c.count(FJ, 0, FJ // 2))
                            eng.wait_ge(dve_x, c.count(1, 0, 1))
                        wait(eng, act_h, c.count(FJ, 0, j - 1))
                        n = 0
                        for a in range(DC):
                            cols = slice(a * FF + j * P, a * FF + (j + 1) * P)
                            for l, r in ((wh, xh), (wh, xl), (wl, xh)):
                                last = pe.matmul(h_bank[j % 2][:, :], l[p][:, cols], r[p][:, a, :],
                                                 start=(n == 0), stop=(n == 3 * DC - 1))
                                n += 1
                        last.then_inc(pe_h, 1)
                    if j < LAG:
                        if was.exists():
                            second(c, 1, FJ - LAG + j)
                    elif now.exists():
                        second(c, 0, j - LAG)
                    if j == 2 and near.exists():
                        eng.wait_ge(ld_x[near.parity], near.of_parity(16, 16))
                        wait(eng, dve_x, c.count(1, 0, 1))
                        for a in range(DC):
                            for t in range(BT):
                                last = pe.transpose(x_bank[a][:, t * P:(t + 1) * P],
                                                    x_rows[near.parity][:, t, a * P:(a + 1) * P], ident[:, :])
                        last.then_inc(pe_x, 1)
            run_blocks(eng, cycle)


def combine(nc, x2_sb, slot, weight, sorted_y, g3, b3, out):
    stack = ExitStack()
    with stack:
        def sb(name, shape, dt=F32):
            return stack.enter_context(nc.sbuf_tensor(name, shape, dt))

        def sem(name):
            return stack.enter_context(nc.semaphore(name))

        R = 4
        g_row, b_row = sb("g3_row", [P, D]), sb("b3_row", [P, D])
        got = [[sb(f"got{r}{k}", [P, ST, D]) for k in range(K)] for r in range(R)]
        stats = sb("stats3", [P, ST, 6])
        mv = [sb(f"mv3{k}", [P, ST, 2]) for k in range(2)]
        ve, rstd = sb("ve3", [P, ST]), [sb(f"rstd3{k}", [P, ST]) for k in range(2)]
        shift = [sb(f"shift3{k}", [P, ST]) for k in range(2)]
        eps, half = sb("eps3", [P, ST]), sb("half3", [P, ST])
        o = [sb(f"o3{k}", [P, ST, D]) for k in range(2)]
        ld, const = sem("f_ld"), sem("f_const")
        landed = [sem(f"f_landed{r}") for r in range(R)]
        normed, scaled, ve_done, rs = (sem(f"f_{n}") for n in ("norm", "scale", "ve", "rs"))
        stored = [sem(f"f_stored{k}") for k in range(2)]
        add0, add1, st_d, mean_d, gained = (sem(f"f_{n}") for n in ("add0", "add1", "st", "mean", "gain"))
        block = stack.enter_context(nc.Block())

        @block.sync
        def _(eng):
            eng.dma_start(g_row[:, :], g3.partition_broadcast(P)).then_inc(ld, 16)
            eng.dma_start(b_row[:, :], b3.partition_broadcast(P)).then_inc(ld, 16)
            for b in range(B):
                eng.wait_ge(scaled, b + 1)
                eng.dma_start(out[b].rearrange("(t p) d -> p t d", p=P), o[b % 2][:, :, :]).then_inc(stored[b % 2], 16)
            for k in range(2):
                eng.wait_ge(stored[k], 16 * B // 2)

        @block.gpsimd
        def _(eng):
            g = nc.gpsimd
            g.memset(eps[:, :], EPS).then_inc(const, 1)
            g.memset(half[:, :], -0.5).then_inc(const, 1)
            eng.wait_ge(const, 2)

            def gather(b):
                if b >= R:
                    eng.wait_ge(normed, b - R + 1)
                for t in range(ST):
                    for k in range(K):
                        g.indirect_dma_start(got[b % R][k][:, t, :], None, sorted_y,
                                             bass.IndirectOffsetOnAxis(ap=slot[k][:, b * ST + t:b * ST + t + 1], axis=0),
                                             bounds_check=NBLK * BLK - 1).then_inc(landed[b % R], 16)
            for b in range(B + 1):
                if b < B:
                    gather(b)
                if b >= 1:
                    d = b - 1
                    eng.wait_ge(mean_d, d + 1)
                    wait(eng, rs, d)
                    g.tensor_tensor(ve[:, :], mv[d % 2][:, :, 1], eps[:, :], ALU.add).then_inc(ve_done, 1)
                    eng.wait_ge(ve_done, d + 1)
                    g.tensor_tensor(rstd[d % 2][:, :], ve[:, :], half[:, :], ALU.pow).then_inc(rs, 1)

        @block.vector
        def _(eng):
            v = nc.vector
            eng.wait_ge(ld, 32)

            def first(b):
                eng.wait_ge(landed[b % R], 64 * (b // R + 1))
                y = got[b % R][0]
                for t in range(ST):
                    i = b * ST + t
                    last = v.scalar_tensor_tensor(out=y[:, t, :], in0=y[:, t, :], scalar=weight[0][:, i:i + 1],
                                                  in1=x2_sb[:, i, :], op0=ALU.mult, op1=ALU.add)
                last.then_inc(add0, 1)
                eng.wait_ge(add0, b + 1)
                for t in range(ST):
                    i = b * ST + t
                    last = v.scalar_tensor_tensor(out=y[:, t, :], in0=got[b % R][1][:, t, :], scalar=weight[1][:, i:i + 1],
                                                  in1=y[:, t, :], op0=ALU.mult, op1=ALU.add)
                last.then_inc(add1, 1)
                eng.wait_ge(add1, b + 1)
                for t in range(ST):
                    last = v.bn_stats(stats[:, t, :], y[:, t, :])
                last.then_inc(st_d, 1)
                eng.wait_ge(st_d, b + 1)
                for t in range(ST):
                    last = v.bn_aggr(mv[b % 2][:, t, :], stats[:, t, :])
                last.then_inc(mean_d, 1)

            def second(b):
                y = got[b % R][0]
                eng.wait_ge(rs, b + 1)
                if b >= 2:
                    eng.wait_ge(stored[b % 2], 16 * (b // 2))
                for t in range(ST):
                    last = v.tensor_scalar(o[b % 2][:, t, :], y[:, t, :], mv[b % 2][:, t, 0:1], rstd[b % 2][:, t:t + 1],
                                           ALU.subtract, ALU.mult)
                last.then_inc(normed, 1)
                eng.wait_ge(normed, b + 1)
                wide = [P, ST, D]
                v.tensor_tensor(o[b % 2][:, :, :], o[b % 2][:, :, :], g_row[:, :].unsqueeze(1).to_broadcast(wide), ALU.mult).then_inc(gained, 1)
                eng.wait_ge(gained, b + 1)
                v.tensor_tensor(o[b % 2][:, :, :], o[b % 2][:, :, :], b_row[:, :].unsqueeze(1).to_broadcast(wide), ALU.add).then_inc(scaled, 1)

            for b in range(B + 1):
                if b < B:
                    first(b)
                if b >= 1:
                    second(b - 1)


def layer_program(nc, x, ctxt, sa, ca, norms, router, expert_w, out):
    x2 = nc.dram_tensor("x2_scratch", (B, P, ST, D), F32, kind="Internal").ap()
    attention_program(nc, x, ctxt, sa, ca, norms[0], norms[1], x2)
    moe_program(nc, x2, *router, *expert_w, *norms[2], out)


_PRE = "L0_xattn_"
_ATT = ["wq", "bq", "wk", "bk", "wv", "bv", "wo", "bo"]
_OUTS = [((B, S, D), "float32")]


def kernel(**inputs):
    import numpy as _np
    import concourse.bacc as _bacc
    from concourse import mybir as _mybir
    from concourse.bass_utils import run_bass_kernel_spmd as _run

    nc = _bacc.Bacc("TRN2", target_bir_lowering=False, num_devices=1)
    arrays = {}

    def given(name):
        a = _np.ascontiguousarray(inputs[name])
        arrays[f"in_{name}_dram"] = a
        return nc.dram_tensor(f"in_{name}_dram", a.shape, _mybir.dt.from_np(a.dtype), kind="ExternalInput").ap()

    x, ctxt = given("x"), given("ctx_1024")
    sa = [given(_PRE + "sa_" + n) for n in _ATT]
    ca = [given(_PRE + "ca_" + n) for n in _ATT]
    norms = [(given(f"{_PRE}ln{k}_g"), given(f"{_PRE}ln{k}_b")) for k in (1, 2, 3)]
    router = [given(_PRE + "router_w"), given(_PRE + "router_b")]
    expert_w = [given(_PRE + n) for n in ("e_w1", "e_b1", "e_w2", "e_b2")]
    out = nc.dram_tensor("out_0_dram", _OUTS[0][0], F32, kind="ExternalOutput").ap()
    layer_program(nc, x, ctxt, sa, ca, norms, router, expert_w, out)
    r = _run(nc, [arrays], core_ids=[0])
    return r.results[0]["out_0_dram"]
```

```python
import concourse.bass as bass
from concourse import mybir
from contextlib import ExitStack

F32 = mybir.dt.float32
F32R = mybir.dt.float32r
BF16 = mybir.dt.bfloat16
I32 = mybir.dt.int32
ALU = mybir.AluOpType
ACT = mybir.ActivationFunctionType
AX = mybir.AxisListType

P = 128
B, S, D, H = 16, 256, 256, 16
HD = D // H
ST = S // P
DC = D // P
HC = P // HD
G = 4
GH = H // G
VW = 32
ITEMS = 2 * B
PARTS = 3
MROW = P - 1
SCALE = float(HD) ** -0.5
MASKED = -1.0e30
EPS = 1e-5


E, FF, K = 8, 1024, 2
T = B * S
NT = T // P
BLK = 256
BT = BLK // P
FJ = FF // P
NBLK = (T * K + E * (BLK - 1)) // BLK
LOGB = BLK.bit_length() - 1
NH = NBLK * BT
LAG = 2
WCOLS = DC * FF + FJ * D


def affine(i, times, plus):
    return plus if i is None else i * times + plus


class Item:

    def __init__(self, i, pair, parity, cross):
        self.i, self.pair, self.parity, self.cross = i, pair, parity, cross

    def of_parity(self, per, extra=0):
        return affine(self.i, per, per * self.pair + extra)

    def of_cross(self, per, extra=0):
        return self.of_parity(per, extra - per * B // 2)

    @property
    def batch(self):
        return affine(self.i, 2, 2 * self.pair + self.parity - (B if self.cross else 0))

    def exists(self):
        return self.i is not None or 0 <= 2 * self.pair + self.parity < ITEMS

    def is_number(self, n):
        return self.i is None and 2 * self.pair + self.parity == n


class Cycle:

    def __init__(self, i, pair, parity, cross=None):
        self.i, self.pair, self.parity, self.cross = i, pair, parity, cross

    def is_number(self, n):
        return self.i is None and 2 * self.pair + self.parity == n

    def item(self, n):
        at = 2 * self.pair + self.parity + n
        return Item(self.i, at // 2, at % 2, at >= B if self.i is None else self.cross)

    def count(self, per, n, extra):
        at = per * (2 * self.pair + self.parity + n) + extra
        return min(at, per * ITEMS) if self.i is None else affine(self.i, 2 * per, at)


def wait(eng, sem, value):
    if not isinstance(value, int) or value > 0:
        eng.wait_ge(sem, value)


def run_cycles(eng, body):
    for c in range(-3, 4):
        body(Cycle(None, c // 2, c % 2))
    with eng.Fori(0, 4) as i:
        body(Cycle(i, 2, 0, False))
        body(Cycle(i, 2, 1, False))
    for c in range(12, 18):
        body(Cycle(None, c // 2, c % 2))
    with eng.Fori(0, 5) as i:
        body(Cycle(i, 9, 0, True))
        body(Cycle(i, 9, 1, True))
    for c in range(28, ITEMS + 2):
        body(Cycle(None, c // 2, c % 2))


def attention_program(nc, x, ctxt, sa, ca, ln1, ln2, router, tables, out):
    stack = ExitStack()
    with stack:
        def sb(name, shape, dt=F32):
            return stack.enter_context(nc.sbuf_tensor(name, shape, dt))

        def sem(name):
            return stack.enter_context(nc.semaphore(name))

        def two(make, name, *a):
            return [make(f"{name}{k}", *a) for k in range(2)]

        x1 = nc.dram_tensor("x1_scratch", (B, P, ST, D), F32, kind="Internal").ap()
        bounce = nc.dram_tensor("qk_bounce", (2, 2, 2, HD, HC * DC * S), F32, kind="Internal").ap()

        names = ["sq", "sk", "sv", "so", "cq", "ck", "cv", "co"]
        w_in = [sb(f"w_in{k}", [P, DC, D]) for k in range(2)]
        w_hi = {n: sb(f"w_{n}_hi", [P, DC, D], F32R) for n in names}
        w_lo = {n: sb(f"w_{n}_lo", [P, DC, D], F32R) for n in names}
        qk_bias = {n: sb(f"b_{n}", [P, DC]) for n in ("sq", "sk", "cq", "ck")}
        row = {n: sb(f"row_{n}", [P, D]) for n in ("sv", "so", "cv", "co", "g1", "b1", "g2", "b2")}
        rw_sb = sb("rw_sb", [P, DC, E])
        rb_sb = sb("rb_sb", [E, 1])
        ident = tables.ident
        ident_bf = sb("ident_bf", [P, P], BF16)
        mask_qk = sb("mask_qk", [P, ST, P], BF16)
        mask_kq = sb("mask_kq", [P, ST, P], BF16)
        eps = sb("eps", [P, ST])
        minus_half = sb("minus_half", [P, ST])

        x_in = two(sb, "x_in", [P, ST, D])
        c_in = two(sb, "c_in", [P, ST, D])
        staged = w_in + c_in + w_in + w_in
        staging = [0, 1, 2, 3, 0, 1, 0, 1]
        landing = [1, 1, 1, 1, 2, 2, 3, 3]
        x_res = two(sb, "x_res", [P, ST, D])
        xt_hi = two(sb, "xt_hi", [P, DC, S], F32R)
        xt_lo = two(sb, "xt_lo", [P, DC, S], F32R)
        ct_hi = two(sb, "ct_hi", [P, DC, S], F32R)
        ct_lo = two(sb, "ct_lo", [P, DC, S], F32R)
        proj_hi = {n: sb(f"{n}_hi", [P, DC, S], F32R) for n in "qk"}
        proj_lo = {n: sb(f"{n}_lo", [P, DC, S], F32R) for n in "qk"}
        q_stack = two(sb, "q_stack", [P, H, S], F32R)
        k_stack = two(sb, "k_stack", [P, H, S], F32R)
        v_aug = two(sb, "v_aug", [P, ST, H, VW])
        maxima3 = two(sb, "maxima3", [P, 3, H])
        maxima = two(sb, "maxima", [P, ST, H])
        ones_row = sb("ones_row", [H, S])
        m_neg = [two(sb, f"m_neg{half}", [H // 2, S], F32R) for half in range(2)]
        probs = two(sb, "probs", [P, GH, ST, S])
        heads_t = [sb(f"heads_t{g}", [P, S]) for g in range(G)]
        inv_sum = sb("inv_sum", [P, 16])
        heads = sb("heads", [P, ST, D])
        ot_hi = sb("ot_hi", [P, DC, S], F32R)
        ot_lo = sb("ot_lo", [P, DC, S], F32R)
        y = two(sb, "y", [P, ST, D])
        stats = sb("stats", [P, ST, 6])
        counted = sb("counted", [P, ST])
        mean_var = two(sb, "mean_var", [P, ST, 2])
        var_eps = sb("var_eps", [P, ST])
        rstd = two(sb, "rstd", [P, ST])
        minus_mean = sb("minus_mean", [P, ST])
        minus_one = sb("minus_one", [P, ST])
        shift = two(sb, "shift", [P, ST])
        z = two(sb, "z", [P, ST, D])
        x_out = two(sb, "x_out", [P, ST, D])
        x2t = sb("x2t", [P, DC, S])
        logits_t = sb("logits_t", [E, S])

        def bank(name):
            return stack.enter_context(nc.psum_tensor(name, [P, 512], F32))

        s_bank = [bank("s_bank0"), bank("s_bank1")]
        t_bank = [bank("t_bank0"), bank("t_bank1")]
        av_bank = bank("av_bank")
        misc = [bank("misc0"), bank("misc1"), bank("misc2")]

        ld_w, w_split, w_halved = [sem(f"ld_w{k}") for k in range(4)], sem("w_split"), sem("w_halved")
        ld_qk_bias, ld_rows, const_made = sem("ld_qk_bias"), sem("ld_rows"), sem("const_made")
        zeroed, ones_made, ones_placed = two(sem, "zeroed"), sem("ones_made"), sem("ones_placed")
        pool_chain = sem("pool_chain")
        ld_x, ld_c, ld_r = two(sem, "ld_x"), two(sem, "ld_c"), two(sem, "ld_r")
        bounced = two(sem, "bounced")
        stacked = [two(sem, f"stacked{half}") for half in range(2)]
        m_placed = [two(sem, f"m_placed{half}") for half in range(2)]
        stored = two(sem, "stored")
        pe_xt, pe_ct, pe_q, pe_k, pe_v = sem("pe_xt"), sem("pe_ct"), sem("pe_q"), sem("pe_k"), sem("pe_v")
        pe_s, pe_t, pe_av, pe_mt = sem("pe_s"), sem("pe_t"), sem("pe_av"), sem("pe_mt")
        pe_tr, pe_ot, pe_wo = sem("pe_tr"), sem("pe_ot"), sem("pe_wo")
        act_xt, act_ct, act_q, act_k = sem("act_xt"), sem("act_ct"), sem("act_q"), sem("act_k")
        act_exp, act_av, act_ot = sem("act_exp"), sem("act_av"), sem("act_ot")
        act_m, act_z = sem("act_m"), sem("act_z")
        dve_xt, dve_ct, dve_q, dve_k, dve_v = (sem(f"dve_{n}") for n in ("xt", "ct", "q", "k", "v"))
        dve_max, dve_joined, dve_inv = sem("dve_max"), sem("dve_joined"), sem("dve_inv")
        dve_tr, dve_ot, dve_y = sem("dve_tr"), sem("dve_ot"), sem("dve_y")
        dve_stats, dve_mean = sem("dve_stats"), sem("dve_mean")
        pool_res, pool_eps, pool_rstd = sem("pool_res"), sem("pool_eps"), sem("pool_rstd")
        pool_shift = sem("pool_shift")
        pe_x2t, pe_lt, pe_lg = sem("pe_x2t"), sem("pe_lt"), sem("pe_lg")
        act_x2t, act_lt, act_lg = sem("act_x2t"), sem("act_lt"), sem("act_lg")
        tables_chain = sem("tables_chain")
        pool_gain, pool_out = sem("pool_gain"), sem("pool_out")

        w_dram = {"sq": sa[0], "sk": sa[2], "sv": sa[4], "so": sa[6],
                  "cq": ca[0], "ck": ca[2], "cv": ca[4], "co": ca[6]}
        b_dram = {"sq": sa[1], "sk": sa[3], "cq": ca[1], "ck": ca[3]}
        row_dram = {"sv": sa[5], "so": sa[7], "cv": ca[5], "co": ca[7],
                    "g1": ln1[0], "b1": ln1[1], "g2": ln2[0], "b2": ln2[1]}

        def by_head(ap, n):
            return ap.rearrange("p a (g c d) -> p a c g d", c=DC, d=HD) if n[1] in "qk" else ap

        block = stack.enter_context(nc.Block())

        @block.sync
        def _(eng):
            def load_weight(k):
                eng.dma_start(staged[k][:, :, :], w_dram[names[k]].rearrange("(a p) n -> p a n", p=P)).then_inc(ld_w[staging[k]], 16)

            def load_bias(n, ready):
                for i in range(DC):
                    eng.dma_start(qk_bias[n][:, i:i + 1], b_dram[n].rearrange("(g c d) -> c g d", c=DC, d=HD)[i],
                                  allow_slow_non_contiguous=True).then_inc(ready, 16)

            eng.dma_start(x_in[0][:, :, :], x[0].rearrange("(t p) d -> p t d", p=P)).then_inc(ld_x[0], 16)
            for k in range(4):
                load_weight(k)
            load_bias("sq", ld_qk_bias)
            load_bias("sk", ld_qk_bias)

            def cycle(c):
                load, proj, now, smax, done = (c.item(n) for n in (3, 2, 0, 1, -2))
                j = c.parity
                if c.is_number(-2):
                    for n in row:
                        eng.dma_start(row[n][:, :], row_dram[n].partition_broadcast(P)).then_inc(ld_rows, 16)
                    load_bias("cq", ld_rows)
                    load_bias("ck", ld_rows)
                    eng.dma_start(rw_sb[:, :, :], router[0].rearrange("(c p) e -> p c e", p=P)).then_inc(ld_rows, 16)
                    eng.dma_start(rb_sb[:, :], router[1].rearrange("(e a) -> e a", a=1), allow_slow_non_contiguous=True).then_inc(ld_rows, 16)
                if c.is_number(-1) or c.is_number(0):
                    eng.wait_ge(w_split, 4)
                    load_weight(4 if c.is_number(-1) else 5)
                if c.is_number(2) or c.is_number(3):
                    k = 6 if c.is_number(2) else 7
                    eng.wait_ge(w_split, k - 1)
                    load_weight(k)
                if load.exists() and not load.is_number(0):
                    if load.cross:
                        wait(eng, pe_ct, c.count(1, 1 - B, 1))
                        eng.dma_start(c_in[load.parity][:, :, :],
                                      ctxt[load.batch].rearrange("(t p) d -> p t d", p=P)).then_inc(ld_c[load.parity], 16)
                        if c.i is None:
                            wait(eng, pe_xt, c.count(1, 1, 1))
                        eng.wait_ge(stored[load.parity], load.of_cross(16, 16))
                        eng.dma_start(x_in[load.parity][:, :, :], x1[load.batch]).then_inc(ld_x[load.parity], 16)
                    else:
                        wait(eng, pe_xt, c.count(1, 1, 1))
                        eng.dma_start(x_in[load.parity][:, :, :],
                                      x[load.batch].rearrange("(t p) d -> p t d", p=P)).then_inc(ld_x[load.parity], 16)
                if now.exists():
                    wait(eng, dve_y, c.count(1, -2, 1))
                    eng.dma_start(x_res[j][:, :, :], x1[now.batch] if now.cross else
                                  x[now.batch].rearrange("(t p) d -> p t d", p=P)).then_inc(ld_r[j], 16)
                if now.exists():
                    eng.wait_ge(act_m, c.count(2, 0, 2))
                    eng.dma_start(q_stack[j][MROW:P, H // 2:H, :].bitcast(F32),
                                  m_neg[1][j][:, :].bitcast(F32)).then_inc(m_placed[1][j], 16)
                if proj.exists():
                    for n, (q, ready) in enumerate((("q", dve_q), ("k", dve_k))):
                        eng.wait_ge(ready, c.count(1, 2, 1))
                        for part, src in enumerate((proj_hi, proj_lo)):
                            if n and part:
                                wait(eng, pe_t, c.count(H, 0, H // 2))
                            eng.dma_start(bounce[j, n, part].rearrange("d (g t) -> g d t", g=HC),
                                          src[q][:, :, :].rearrange("p c t -> p (c t)").bitcast(F32)).then_inc(bounced[j], 16)
                    eng.wait_ge(bounced[j], proj.of_parity(64, 64))
                    if proj.is_number(0) or proj.is_number(1):
                        eng.wait_ge(zeroed[j], 2)
                        eng.wait_ge(ones_made, 1)
                        eng.dma_start(k_stack[j][MROW:P, :, :].bitcast(F32), ones_row[:, :]).then_inc(ones_placed, 16)
                for half in range(2):
                    if half == 1:
                        if smax.exists():
                            eng.wait_ge(act_m, c.count(2, 1, 1))
                            eng.dma_start(q_stack[1 - j][MROW:P, 0:H // 2, :].bitcast(F32),
                                          m_neg[0][1 - j][:, :].bitcast(F32)).then_inc(m_placed[0][1 - j], 16)
                        if done.exists():
                            eng.wait_ge(pool_out, c.count(1, -2, 1))
                            eng.dma_start(out[done.batch] if done.cross else x1[done.batch],
                                          x_out[j][:, :, :]).then_inc(stored[j], 16)
                    if proj.exists():
                        if half == 1:
                            wait(eng, pe_t, c.count(H, 0, H))
                        hs = slice(half * H // 2, (half + 1) * H // 2)
                        for n, (dst, parts) in enumerate(((q_stack[j], ((0, 1, 1), (HD, 0, 1), (2 * HD, 0, 1))),
                                                          (k_stack[j], ((0, 0, 1), (HD, 0, 2))))):
                            for at, part, m in parts:
                                eng.dma_start(dst[at:at + m * HD, hs, :].rearrange("p h t -> p (h t)").bitcast(F32),
                                              bounce[j, n, part:part + m, :, half * (H // 2) * S:(half + 1) * (H // 2) * S]
                                              .rearrange("a d t -> (a d) t")).then_inc(stacked[half][j], 16)

            run_cycles(eng, cycle)
            for k in range(2):
                eng.wait_ge(stored[k], ITEMS // 2 * 16)

        @block.gpsimd
        def _(eng):
            g = nc.gpsimd
            g.memset(ident[:, :], 0.0).then_inc(pool_chain, 1)
            g.memset(mask_qk[:, :, :], 0.0).then_inc(pool_chain, 1)
            g.memset(mask_kq[:, :, :], 0.0).then_inc(pool_chain, 1)
            g.memset(eps[:, :], EPS).then_inc(const_made, 1)
            g.memset(minus_half[:, :], -0.5).then_inc(const_made, 1)
            g.memset(minus_one[:, :], -1.0).then_inc(const_made, 1)
            eng.wait_ge(pool_chain, 3)
            g.affine_select(out=ident[:, :], in_=ident[:, :], compare_op=ALU.not_equal, fill=1.0, base=0,
                            pattern=[[-1, P]], channel_multiplier=1).then_inc(pool_chain, 1)
            g.affine_select(out=mask_qk[:, :, :], in_=mask_qk[:, :, :], compare_op=ALU.is_ge, fill=MASKED, base=0,
                            pattern=[[0, ST], [-1, P]], channel_multiplier=1).then_inc(const_made, 1)
            g.affine_select(out=mask_kq[:, :, :], in_=mask_kq[:, :, :], compare_op=ALU.is_ge, fill=MASKED, base=0,
                            pattern=[[0, ST], [1, P]], channel_multiplier=-1).then_inc(const_made, 1)
            eng.wait_ge(pool_chain, 4)
            g.tensor_copy(ident_bf[:, :], ident[:, :]).then_inc(const_made, 1)
            g.memset(ones_row[:, :], 1.0).then_inc(ones_made, 1)
            g.memset(q_stack[0][:, :, :].bitcast(F32), 0.0).then_inc(zeroed[0], 1)
            g.memset(q_stack[1][:, :, :].bitcast(F32), 0.0).then_inc(zeroed[1], 1)
            eng.wait_ge(const_made, 6)
            eng.wait_ge(ld_rows, 14 * 16)

            def cycle(c):
                now, fin, done = c.item(0), c.item(-1), c.item(-2)
                j = c.parity
                if c.is_number(3):
                    tables.fill(g, eng, tables_chain)
                if done.exists():
                    k = "2" if done.cross else "1"
                    eng.wait_ge(act_z, c.count(1, -2, 1))
                    for t in range(ST):
                        last = g.tensor_tensor(z[j][:, t, :], z[j][:, t, :], row["g" + k][:, :], ALU.mult)
                    last.then_inc(pool_gain, 1)
                    eng.wait_ge(pool_gain, c.count(1, -2, 1))
                    if not (done.is_number(0) or done.is_number(1)):
                        eng.wait_ge(stored[j], done.of_parity(16))
                    for t in range(ST):
                        last = g.tensor_tensor(x_out[j][:, t, :], z[j][:, t, :], row["b" + k][:, :], ALU.add)
                    last.then_inc(pool_out, 1)
                if now.exists():
                    eng.wait_ge(ld_r[j], now.of_parity(16, 16))
                    bo = row["co" if now.cross else "so"]
                    for t in range(ST):
                        last = g.tensor_tensor(x_res[j][:, t, :], x_res[j][:, t, :], bo[:, :], ALU.add)
                    last.then_inc(pool_res, 1)
                if fin.exists():
                    k = 1 - j
                    eng.wait_ge(dve_mean, c.count(1, -1, 1))
                    g.tensor_tensor(var_eps[:, :], mean_var[k][:, :, 1], eps[:, :], ALU.add).then_inc(pool_eps, 1)
                    g.tensor_tensor(minus_mean[:, :], mean_var[k][:, :, 0], minus_one[:, :], ALU.mult)
                    eng.wait_ge(pool_eps, c.count(1, -1, 1))
                    g.tensor_tensor(rstd[k][:, :], var_eps[:, :], minus_half[:, :], ALU.pow).then_inc(pool_rstd, 1)
                    eng.wait_ge(pool_rstd, c.count(1, -1, 1))
                    g.tensor_tensor(shift[k][:, :], minus_mean[:, :], rstd[k][:, :], ALU.mult).then_inc(pool_shift, 1)

            run_cycles(eng, cycle)

        @block.scalar
        def _(eng):
            a = nc.scalar

            def halve(k):
                n = names[k]
                eng.wait_ge(ld_w[staging[k]], 16 * landing[k])
                for i in range(DC):
                    if n[1] in "qk":
                        last = a.activation(w_hi[n][:, i:i + 1, :].rearrange("p a (c g d) -> p a c g d", c=DC, d=HD)[:, 0],
                                            by_head(staged[k][:, i:i + 1, :], n)[:, 0], ACT.Copy)
                    else:
                        last = a.activation(w_hi[n][:, i, :], staged[k][:, i, :], ACT.Copy)
                last.then_inc(w_halved, 1)

            halve(0)
            halve(1)

            def cycle(c):
                proj, smax, now, fin, done = (c.item(n) for n in (2, 1, 0, -1, -2))
                j = c.parity
                p = proj.parity
                for k in range(4):
                    if c.is_number(k):
                        halve(4 + k)

                def from_values(n, g):
                    eng.wait_ge(pe_av, c.count(G, n, g + 1))
                    wait(eng, pe_tr, c.count(2, n - 1, 1 + g // 2))
                    a.activation(heads_t[g][:, :], av_bank[:, 0:S], ACT.Copy).then_inc(act_av, 1)

                def minus_max(half, n):
                    eng.wait_ge(pe_mt, c.count(2, n, 1 + half))
                    it = c.item(n)
                    if not (it.is_number(0) or it.is_number(1)):
                        eng.wait_ge(m_placed[half][it.parity], it.of_parity(16))
                    a.activation(m_neg[half][it.parity][:, :], misc[0][0:H // 2, 0:S], ACT.Copy, scale=-1.0).then_inc(act_m, 1)

                def project(q, bk, ready, done):
                    w = "c" if proj.cross else "s"
                    eng.wait_ge(ready, c.count(1, 2, 1))
                    if q == "q" and not proj.is_number(0):
                        prev = c.item(1)
                        eng.wait_ge(bounced[prev.parity], prev.of_parity(64, 64))
                    for i in range(DC):
                        last = a.activation(proj_hi[q][:, i, :], misc[bk][:, i * S:(i + 1) * S], ACT.Identity,
                                            bias=qk_bias[w + q][:, i:i + 1])
                    last.then_inc(done, 1)

                for h in range(H):
                    if now.exists():
                        cols = S + P if not now.cross else 2 * S
                        if h % GH == 0:
                            wait(eng, pe_av, c.count(G, 0, h // GH - 1))
                        eng.wait_ge(pe_t, c.count(H, 0, h + 1))
                        pr = probs[h // GH % 2][:, h % GH].rearrange("p a s -> p (a s)")
                        a.activation(pr[:, 0:cols], t_bank[h % 2][:, 0:cols], ACT.Exp, scale=SCALE).then_inc(act_exp, 1)
                    if h == 0 and proj.exists():
                        eng.wait_ge(pe_xt, c.count(1, 2, 1))
                        wait(eng, pe_v, c.count(1, 0, 1))
                        a.activation(xt_hi[p][:, :, :], misc[1][:, :].rearrange("p (c t) -> p c t", c=DC), ACT.Copy).then_inc(act_xt, 1)
                    if h in (2, 3) and proj.is_number(0):
                        halve(h)
                    if h == 1 and proj.exists() and proj.cross:
                        eng.wait_ge(pe_ct, c.count(1, 2 - B, 1))
                        a.activation(ct_hi[p][:, :, :], misc[2][:, :].rearrange("p (c t) -> p c t", c=DC), ACT.Copy).then_inc(act_ct, 1)
                    if h == 1 and done.exists():
                        eng.wait_ge(pool_shift, c.count(1, -2, 1))
                        for t in range(ST):
                            last = a.activation(z[j][:, t, :], y[j][:, t, :], ACT.Identity, scale=rstd[j][:, t:t + 1],
                                                bias=shift[j][:, t:t + 1])
                        last.then_inc(act_z, 1)
                    if h == 2 and now.exists():
                        minus_max(1, 0)
                    if h == 2 and fin.exists():
                        from_values(-1, G - 1)
                    if h == 4 and proj.exists():
                        if proj.is_number(0):
                            eng.wait_ge(ld_qk_bias, 64)
                        project("q", 1, pe_q, act_q)
                    if h == 6 and proj.exists():
                        project("k", 2, pe_k, act_k)
                    if h == 7 and now.exists():
                        from_values(0, 0)
                    if h == 8 and done.exists() and done.cross:
                        eng.wait_ge(pe_x2t, c.count(1, -2 - B, 1))
                        a.activation(x2t[:, :, :], misc[0][:, :].rearrange("p (c t) -> p c t", c=DC), ACT.Copy).then_inc(act_x2t, 1)
                    if h == 9 and fin.exists():
                        eng.wait_ge(pe_ot, c.count(1, -1, 1))
                        wait(eng, pe_wo, c.count(1, -2, 1))
                        a.activation(ot_hi[:, :, :], misc[1][:, :].rearrange("p (c t) -> p c t", c=DC), ACT.Copy).then_inc(act_ot, 1)
                    if h == 10 and done.exists() and done.cross:
                        eng.wait_ge(pe_lt, c.count(1, -2 - B, 1))
                        a.activation(logits_t[:, :], misc[0][0:E, 0:S], ACT.Identity, bias=rb_sb[:, 0:1]).then_inc(act_lt, 1)
                    if h == 11 and now.exists():
                        from_values(0, 1)
                    if h == 12 and smax.exists():
                        minus_max(0, 1)
                    if h == 12 and done.exists() and done.cross:
                        eng.wait_ge(pe_lg, c.count(1, -2 - B, 1))
                        a.activation(tables.lg[:, bass.ds(done.batch * ST, ST), :],
                                     misc[0][:, S:S + ST * E].rearrange("p (t e) -> p t e", e=E), ACT.Copy).then_inc(act_lg, 1)
                    if h == 15 and now.exists():
                        from_values(0, 2)

            run_cycles(eng, cycle)

        @block.vector
        def _(eng):
            v = nc.vector

            def split(k):
                n = names[k]
                eng.wait_ge(w_halved, k + 1)
                for i in range(DC):
                    hi = w_hi[n][:, i:i + 1, :].bitcast(F32)
                    lo = w_lo[n][:, i:i + 1, :]
                    src = staged[k][:, i:i + 1, :]
                    if n[1] in "qk":
                        hi = hi.rearrange("p a (c g d) -> p a c g d", c=DC, d=HD)[:, 0]
                        lo = lo.rearrange("p a (c g d) -> p a c g d", c=DC, d=HD)[:, 0]
                        src = by_head(src, n)[:, 0]
                    last = v.tensor_tensor(lo, src, hi, ALU.subtract)
                last.then_inc(w_split, 1)

            split(0)
            split(1)

            def cycle(c):
                proj, smax, now, fin = (c.item(n) for n in (2, 1, 0, -1))
                p, s = proj.parity, smax.parity
                for k in range(4):
                    if c.is_number(k):
                        split(4 + k)

                def divide(n, pair):
                    eng.wait_ge(pe_tr, c.count(2, n, pair + 1))
                    got = misc[0][:, :].rearrange("p (k w) -> p k w", w=VW)
                    v.reciprocal(inv_sum[:, :], got[:, :, HD]).then_inc(dve_inv, 1)
                    eng.wait_ge(dve_inv, c.count(2, n, pair + 1))
                    wait(eng, pe_ot, c.count(1, n, 0))
                    for t in range(ST):
                        last = v.tensor_tensor(
                            heads[:, t, pair * P:(pair + 1) * P].rearrange("p (k d) -> p k d", d=HD),
                            got[:, 8 * t:8 * t + 8, 0:HD],
                            inv_sum[:, 8 * t:8 * t + 8].unsqueeze(2).to_broadcast([P, 8, HD]), ALU.mult)
                    last.then_inc(dve_tr, 1)

                def low_part(q, bk, ready, fine):
                    w = "c" if proj.cross else "s"
                    eng.wait_ge(ready, c.count(1, 2, 1))
                    if q == "q" and not proj.is_number(0):
                        prev = c.item(1)
                        eng.wait_ge(bounced[prev.parity], prev.of_parity(64, 64))
                    for i in range(DC):
                        last = v.scalar_tensor_tensor(
                            out=proj_lo[q][:, i, :], in0=misc[bk][:, i * S:(i + 1) * S],
                            scalar=qk_bias[w + q][:, i:i + 1], in1=proj_hi[q][:, i, :].bitcast(F32),
                            op0=ALU.add, op1=ALU.subtract)
                    last.then_inc(fine, 1)

                for h in range(H):
                    if smax.exists():
                        eng.wait_ge(pe_s, c.count(H, 1, h + 1))
                        if smax.cross:
                            v.tensor_reduce(maxima[s][:, :, h], s_bank[h % 2][:, :].rearrange("p (q k) -> p q k", q=ST),
                                            axis=AX.X, op=ALU.max).then_inc(dve_max, 1)
                        else:
                            v.tensor_reduce(maxima3[s][:, :, h], s_bank[h % 2][:, 0:3 * P].rearrange("p (q k) -> p q k", q=3),
                                            axis=AX.X, op=ALU.max).then_inc(dve_max, 1)
                        if h % (H // 2) == H // 2 - 1 and not smax.cross:
                            hs = slice(h + 1 - H // 2, h + 1)
                            eng.wait_ge(dve_max, c.count(H, 1, h + 1))
                            v.tensor_copy(maxima[s][:, 0, hs], maxima3[s][:, 2, hs])
                            v.tensor_tensor(maxima[s][:, 1, hs], maxima3[s][:, 0, hs], maxima3[s][:, 1, hs],
                                            ALU.max).then_inc(dve_joined, 1)
                    if h == 1 and proj.exists():
                        eng.wait_ge(act_xt, c.count(1, 2, 1))
                        wait(eng, pe_v, c.count(1, 0, 1))
                        v.tensor_tensor(xt_lo[p][:, :, :], misc[1][:, :].rearrange("p (c t) -> p c t", c=DC),
                                        xt_hi[p][:, :, :].bitcast(F32), ALU.subtract).then_inc(dve_xt, 1)
                    if h == 2 and proj.exists() and proj.cross:
                        eng.wait_ge(act_ct, c.count(1, 2 - B, 1))
                        v.tensor_tensor(ct_lo[p][:, :, :], misc[2][:, :].rearrange("p (c t) -> p c t", c=DC),
                                        ct_hi[p][:, :, :].bitcast(F32), ALU.subtract).then_inc(dve_ct, 1)
                    if h == 5 and proj.exists():
                        low_part("q", 1, act_q, dve_q)
                    if proj.is_number(0):
                        if h == 3:
                            v.memset(k_stack[0][:, :, :].bitcast(F32), 0.0).then_inc(zeroed[0], 1)
                        if h == 8:
                            split(2)
                            for k in range(2):
                                v.memset(v_aug[k][:, :, :, :], 1.0)
                            split(3)
                            v.memset(k_stack[1][:, :, :].bitcast(F32), 0.0).then_inc(zeroed[1], 1)
                    if h == 6 and fin.exists():
                        divide(-1, 1)
                    if h == 7 and proj.exists():
                        low_part("k", 2, act_k, dve_k)
                    if h == 10 and fin.exists():
                        eng.wait_ge(act_ot, c.count(1, -1, 1))
                        wait(eng, pe_wo, c.count(1, -2, 1))
                        v.tensor_tensor(ot_lo[:, :, :], misc[1][:, :].rearrange("p (c t) -> p c t", c=DC),
                                        ot_hi[:, :, :].bitcast(F32), ALU.subtract).then_inc(dve_ot, 1)
                    if h == 12 and smax.exists():
                        if smax.is_number(0):
                            eng.wait_ge(ld_rows, 14 * 16)
                        bv = row["cv" if smax.cross else "sv"]
                        eng.wait_ge(pe_v, c.count(1, 1, 1))
                        wait(eng, pe_av, c.count(G, 0, 0))
                        for t in range(ST):
                            last = v.tensor_tensor(v_aug[s][:, t, :, 0:HD],
                                                   misc[2][:, t * D:(t + 1) * D].rearrange("p (h d) -> p h d", d=HD),
                                                   bv[:, :].rearrange("p (h d) -> p h d", d=HD), ALU.add)
                        last.then_inc(dve_v, 1)
                    if fin.exists():
                        k = fin.parity
                        if h == 13:
                            eng.wait_ge(pe_wo, c.count(1, -1, 1))
                            eng.wait_ge(pool_res, c.count(1, -1, 1))
                            wait(eng, act_z, c.count(1, -3, 1))
                            v.tensor_tensor(y[k][:, :, :], misc[1][:, :].rearrange("p (t d) -> p t d", t=ST),
                                            x_res[k][:, :, :], ALU.add).then_inc(dve_y, 1)
                        if h == 14:
                            eng.wait_ge(dve_y, c.count(1, -1, 1))
                            for t in range(ST):
                                last = v.bn_stats(stats[:, t, :], y[k][:, t, :])
                            last.then_inc(dve_stats, 1)
                        if h == 15:
                            eng.wait_ge(dve_stats, c.count(1, -1, 1))
                            v.tensor_copy(counted[:, :], stats[:, :, 0])
                            for t in range(ST):
                                last = v.bn_aggr(mean_var[k][:, t, :], stats[:, t, :])
                            last.then_inc(dve_mean, 1)
                    if h == 14 and now.exists():
                        divide(0, 0)

            run_cycles(eng, cycle)

        @block.tensor
        def _(eng):
            pe = nc.tensor
            eng.wait_ge(const_made, 6)

            def split_product(dst, left_hi, left_lo, right_hi, right_lo):
                for i in range(DC):
                    for n, (l, r) in enumerate(((left_hi, right_hi), (left_hi, right_lo), (left_lo, right_hi))):
                        last = pe.matmul(dst, l(i), r(i), start=(i == 0 and n == 0), stop=(i == DC - 1 and n == 2))
                return last

            def cycle(c):
                proj, smax, now, fin, done = (c.item(n) for n in (2, 1, 0, -1, -2))
                j = c.parity
                p, s = proj.parity, smax.parity

                def values(n, g):
                    it = c.item(n)
                    k = it.parity
                    eng.wait_ge(act_exp, c.count(H, n, GH * (g + 1)))
                    wait(eng, act_av, c.count(G, n, g))
                    if g == 0:
                        eng.wait_ge(dve_v, c.count(1, n, 1))
                    for t in range(ST):
                        q0 = P * t if not it.cross else 0
                        for hh in range(GH):
                            pr = probs[g % 2][:, hh].rearrange("p a s -> p (a s)")
                            pr = pr[:, t * S:(t + 1) * S] if it.cross else (pr[:, P:P + S], pr[:, 0:P])[t]
                            last = pe.matmul(av_bank[VW * hh:VW * hh + VW, q0:S], v_aug[k][:, t, GH * g + hh, :],
                                             pr, start=(t == 0), stop=(t == ST - 1), tile_position=(0, VW * hh))
                    last.then_inc(pe_av, 1)

                def max_rows(n, half, free, count):
                    it = c.item(n)
                    eng.wait_ge(dve_max, c.count(H, n, H // 2 * (half + 1)))
                    if not it.cross:
                        eng.wait_ge(dve_joined, c.count(2, n, half + 1))
                    wait(eng, free, count)
                    for t in range(ST):
                        last = pe.transpose(misc[0][0:H // 2, t * P:(t + 1) * P],
                                            maxima[it.parity][:, t, half * H // 2:(half + 1) * H // 2], ident[:, :])
                    last.then_inc(pe_mt, 1)

                def head_rows(n, pair, count):
                    eng.wait_ge(act_av, c.count(G, n, 2 * pair + 2))
                    wait(eng, act_m, count)
                    wait(eng, dve_tr, c.count(2, n, pair))
                    for t in range(ST):
                        for gi in range(2):
                            last = pe.transpose(misc[0][:, (2 * t + gi) * P:(2 * t + gi + 1) * P],
                                                heads_t[2 * pair + gi][:, t * P:(t + 1) * P], ident[:, :])
                    last.then_inc(pe_tr, 1)

                for h in range(H):
                    if smax.exists():
                        if h % (H // 2) == 0:
                            eng.wait_ge(stacked[h // (H // 2)][s], smax.of_parity(80, 80))
                        wait(eng, dve_max, c.count(H, 1, h - 1))
                        qs, ks, sbk = q_stack[s], k_stack[s], s_bank[h % 2]
                        if smax.cross:
                            for t in range(ST):
                                last = pe.matmul(sbk[:, t * S:(t + 1) * S], qs[0:MROW, h, t * P:(t + 1) * P],
                                                 ks[0:MROW, h, :], start=True, stop=True)
                        else:
                            pe.matmul(sbk[:, 0:S], qs[0:MROW, h, P:S], ks[0:MROW, h, :], start=True, stop=False)
                            pe.matmul(sbk[:, S:S + P], qs[0:MROW, h, 0:P], ks[0:MROW, h, 0:P], start=False, stop=False)
                            last = pe.matmul(sbk[:, P:P + S], ident_bf[:, :], mask_qk[:, :, :].rearrange("p t k -> p (t k)"),
                                             start=False, stop=True)
                        last.then_inc(pe_s, 1)
                    if now.exists():
                        if h % (H // 2) == 0:
                            if now.is_number(0) or now.is_number(1):
                                eng.wait_ge(ones_placed, 16 * (j + 1))
                            eng.wait_ge(m_placed[h // (H // 2)][j], now.of_parity(16, 16))
                        wait(eng, act_exp, c.count(H, 0, h - 1))
                        qs, ks, tbk = q_stack[j], k_stack[j], t_bank[h % 2]
                        if now.cross:
                            for t in range(ST):
                                last = pe.matmul(tbk[:, t * S:(t + 1) * S], ks[:, h, t * P:(t + 1) * P], qs[:, h, :],
                                                 start=True, stop=True)
                        else:
                            pe.matmul(tbk[:, P:P + S], ks[:, h, 0:P], qs[:, h, :], start=True, stop=False)
                            pe.matmul(tbk[:, 0:P], ks[:, h, P:S], qs[:, h, P:S], start=False, stop=False)
                            last = pe.matmul(tbk[:, 0:ST * P], ident_bf[:, :], mask_kq[:, :, :].rearrange("p t q -> p (t q)"),
                                             start=False, stop=True)
                        last.then_inc(pe_t, 1)
                    w = "c" if proj.cross else "s"
                    kv_hi, kv_lo = (ct_hi[p], ct_lo[p]) if proj.cross else (xt_hi[p], xt_lo[p])
                    if h == 0 and proj.exists():
                        eng.wait_ge(ld_x[p], proj.of_parity(16, 16))
                        wait(eng, dve_y, c.count(1, -2, 1))
                        for i in range(DC):
                            for t in range(ST):
                                last = pe.transpose(misc[1][:, i * S + t * P:i * S + (t + 1) * P],
                                                    x_in[p][:, t, i * P:(i + 1) * P], ident[:, :])
                        last.then_inc(pe_xt, 1)
                        if proj.cross:
                            eng.wait_ge(ld_c[p], proj.of_cross(16, 16))
                            wait(eng, dve_v, c.count(1, 0, 1))
                            for i in range(DC):
                                for t in range(ST):
                                    last = pe.transpose(misc[2][:, i * S + t * P:i * S + (t + 1) * P],
                                                        c_in[p][:, t, i * P:(i + 1) * P], ident[:, :])
                            last.then_inc(pe_ct, 1)
                    if h == 1 and now.exists():
                        max_rows(0, 1, dve_tr, c.count(2, -1, 1))
                    if h == 1 and fin.exists():
                        values(-1, G - 1)
                    if h in (2, 3) and proj.exists():
                        i = h - 2
                        if (proj.is_number(0) or proj.is_number(B)) and i == 0:
                            eng.wait_ge(w_split, 1 if proj.is_number(0) else 8)
                        if i == 0:
                            eng.wait_ge(dve_xt, c.count(1, 2, 1))
                        last = split_product(
                            misc[1][:, i * S:(i + 1) * S],
                            lambda a: w_hi[w + "q"][:, a, i * P:(i + 1) * P], lambda a: w_lo[w + "q"][:, a, i * P:(i + 1) * P],
                            lambda a: xt_hi[p][:, a, :], lambda a: xt_lo[p][:, a, :])
                        if i == DC - 1:
                            last.then_inc(pe_q, 1)
                    if h in (4, 5) and proj.exists():
                        i = h - 4
                        if i == 0:
                            if proj.is_number(0):
                                eng.wait_ge(w_split, 2)
                            if proj.cross:
                                eng.wait_ge(dve_ct, c.count(1, 2 - B, 1))
                            wait(eng, dve_v, c.count(1, 0, 1))
                        last = split_product(
                            misc[2][:, i * S:(i + 1) * S],
                            lambda a: w_hi[w + "k"][:, a, i * P:(i + 1) * P], lambda a: w_lo[w + "k"][:, a, i * P:(i + 1) * P],
                            lambda a: kv_hi[:, a, :], lambda a: kv_lo[:, a, :])
                        if i == DC - 1:
                            last.then_inc(pe_k, 1)
                    if h == 5 and fin.exists():
                        head_rows(-1, 1, c.count(2, 0, 2))
                    if h == 6 and now.exists():
                        values(0, 0)
                    if h == 7 and done.exists() and done.cross:
                        eng.wait_ge(pool_out, c.count(1, -2, 1))
                        wait(eng, dve_tr, c.count(2, -1, 2))
                        if c.i is None:
                            wait(eng, act_lg, c.count(1, -3 - B, 1))
                        for i in range(DC):
                            for t in range(ST):
                                last = pe.transpose(misc[0][:, i * S + t * P:i * S + (t + 1) * P],
                                                    x_out[j][:, t, i * P:(i + 1) * P], ident[:, :])
                        last.then_inc(pe_x2t, 1)
                    if h == 8 and fin.exists():
                        eng.wait_ge(dve_tr, c.count(2, -1, 2))
                        wait(eng, dve_q, c.count(1, 2, 1))
                        wait(eng, dve_y, c.count(1, -2, 1))
                        for i in range(DC):
                            for t in range(ST):
                                last = pe.transpose(misc[1][:, i * S + t * P:i * S + (t + 1) * P],
                                                    heads[:, t, i * P:(i + 1) * P], ident[:, :])
                        last.then_inc(pe_ot, 1)
                    if h in (9, 10) and smax.exists():
                        w = "c" if smax.cross else "s"
                        kv_hi, kv_lo = (ct_hi[s], ct_lo[s]) if smax.cross else (xt_hi[s], xt_lo[s])
                        t = h - 9
                        if t == 0:
                            if smax.is_number(0):
                                eng.wait_ge(w_split, 3)
                            wait(eng, dve_k, c.count(1, 2, 1))
                            wait(eng, dve_v, c.count(1, 0, 1))
                        last = split_product(
                            misc[2][:, t * D:(t + 1) * D],
                            lambda a: kv_hi[:, a, t * P:(t + 1) * P], lambda a: kv_lo[:, a, t * P:(t + 1) * P],
                            lambda a: w_hi[w + "v"][:, a, :], lambda a: w_lo[w + "v"][:, a, :])
                        if t == ST - 1:
                            last.then_inc(pe_v, 1)
                    if h == 10 and now.exists():
                        values(0, 1)
                    if h == 9 and done.exists() and done.cross:
                        eng.wait_ge(act_x2t, c.count(1, -2 - B, 1))
                        for i in range(DC):
                            last = pe.matmul(misc[0][0:E, 0:S], rw_sb[:, i, :], x2t[:, i, :], start=(i == 0), stop=(i == DC - 1))
                        last.then_inc(pe_lt, 1)
                    if h == 11 and done.exists() and done.cross:
                        eng.wait_ge(act_lt, c.count(1, -2 - B, 1))
                        for t in range(ST):
                            last = pe.matmul(misc[0][:, S + t * E:S + (t + 1) * E], logits_t[:, t * P:(t + 1) * P],
                                             ident[0:E, 0:E], start=True, stop=True)
                        last.then_inc(pe_lg, 1)
                    if h == 11 and smax.exists():
                        max_rows(1, 0, dve_tr, c.count(2, -1, 2))
                    if h in (11, 12) and fin.exists():
                        w = "c" if fin.cross else "s"
                        t = h - 11
                        if t == 0:
                            if fin.is_number(0):
                                eng.wait_ge(w_split, 4)
                            eng.wait_ge(dve_ot, c.count(1, -1, 1))
                        last = split_product(
                            misc[1][:, t * D:(t + 1) * D],
                            lambda a: ot_hi[:, a, t * P:(t + 1) * P], lambda a: ot_lo[:, a, t * P:(t + 1) * P],
                            lambda a: w_hi[w + "o"][:, a, :], lambda a: w_lo[w + "o"][:, a, :])
                        if t == ST - 1:
                            last.then_inc(pe_wo, 1)
                    if h == 13 and now.exists():
                        if done.exists() and done.cross:
                            eng.wait_ge(act_lg, c.count(1, -2 - B, 1))
                        head_rows(0, 0, c.count(2, 1, 1))
                    if h == 14 and now.exists():
                        values(0, 2)

            run_cycles(eng, cycle)


class Tables:

    def __init__(self, sb):
        self.lg = sb("lg", [P, NT, E])
        self.ident = sb("ident", [P, P])
        self.rank_w = sb("rank_w", [P, E])
        self.tri_f = sb("tri_f", [P, P])
        self.tri = sb("tri", [P, P], BF16)
        self.ones = sb("ones", [P, P], BF16)
        self.blk_at = sb("blk_at", [1, NBLK, E])
        self.lane = sb("lane", [P, P], BF16)
        self.tile = sb("tile", [P, NH], BF16)
        self.choice = sb("choice", [P, K, NT])
        self.spare = sb("spare", [P, NH])
        self.part = sb("part", [P, 1])

    def fill(self, g, eng, chain):
        g.memset(self.ones[:, :], 1.0)
        g.memset(self.tri_f[:, :], 0.0).then_inc(chain, 1)
        g.iota(self.blk_at[:, :, :], [[BLK, NBLK], [0, E]], base=0, channel_multiplier=0, allow_small_or_imprecise_dtypes=True)
        g.iota(self.rank_w[:, :], [[-1, E]], base=E, channel_multiplier=0, allow_small_or_imprecise_dtypes=True)
        g.iota(self.lane[:, :], [[1, P]], base=0, channel_multiplier=0, allow_small_or_imprecise_dtypes=True)
        g.iota(self.tile[:, :], [[1, NH]], base=0, channel_multiplier=0, allow_small_or_imprecise_dtypes=True)
        g.iota(self.choice[:, :, :], [[1, K], [K, NT]], base=1, channel_multiplier=0, allow_small_or_imprecise_dtypes=True)
        g.iota(self.spare[:, :], [[P, NH]], base=T * K + 1, channel_multiplier=1, allow_small_or_imprecise_dtypes=True)
        g.iota(self.part[:, :], [[0, 1]], base=0, channel_multiplier=1, allow_small_or_imprecise_dtypes=True)
        eng.wait_ge(chain, 1)
        g.affine_select(out=self.tri_f[:, :], in_=self.tri_f[:, :], compare_op=ALU.is_ge, fill=1.0, base=0,
                        pattern=[[-1, P]], channel_multiplier=1).then_inc(chain, 1)
        eng.wait_ge(chain, 2)
        g.tensor_copy(self.tri[:, :], self.tri_f[:, :])


def moe_program(nc, x2, tables, b1, w1, w2, b2, g3, b3, out):
    by_token = nc.dram_tensor("by_token", (T * K + NBLK * BLK, D), F32, kind="Internal").ap()
    b1_cols = nc.dram_tensor("b1_cols", (P, E, FJ), F32, kind="Internal").ap()
    outer = ExitStack()
    with outer:
        def keep(name, shape, dt=F32):
            return outer.enter_context(nc.sbuf_tensor(name, shape, dt))
        x2_sb = keep("x2_sb", [P, NT, D])
        weight = [keep(f"weight{k}", [P, NT]) for k in range(K)]
        expert_of = keep("expert_of", [1, NBLK], I32)
        from_row = keep("from_row", [P, NH], I32)
        to_row = keep("to_row", [P, NH], I32)
        w_raw = [keep(f"w_raw{k}", [P, WCOLS]) for k in range(2)]
        ld_w1 = [outer.enter_context(nc.semaphore(f"m_ldw1{k}")) for k in range(2)]
        ld_w2 = [outer.enter_context(nc.semaphore(f"m_ldw2{k}")) for k in range(2)]
        x2_back = outer.enter_context(nc.semaphore("x2_back"))

        def load_w1(eng, e, parity):
            eng.dma_start(w_raw[parity][:, 0:DC * FF].rearrange("p (a f) -> p a f", a=DC),
                          w1[e].rearrange("(a p) f -> p a f", p=P)).then_inc(ld_w1[parity], 16)

        def load_w2(eng, e, parity):
            eng.dma_start(w_raw[parity][:, DC * FF:WCOLS].rearrange("p (j d) -> p j d", j=FJ),
                          w2[e].rearrange("(j p) d -> p j d", p=P)).then_inc(ld_w2[parity], 16)

        route(nc, b1, tables, weight, expert_of, from_row, to_row, b1_cols, load_w1, load_w2)
        experts(nc, x2, x2_sb, x2_back, w_raw, ld_w1, ld_w2, load_w1, load_w2, b2, expert_of, tables.ident,
                from_row, to_row, by_token, b1_cols)
        combine(nc, x2_sb, x2_back, weight, tables.ident, by_token, g3, b3, out)


def route(nc, b1, tables, weight, expert_of, from_row, to_row, b1_cols, load_w1, load_w2):
    stack = ExitStack()
    with stack:
        def sb(name, shape, dt=F32):
            return stack.enter_context(nc.sbuf_tensor(name, shape, dt))

        def sem(name):
            return stack.enter_context(nc.semaphore(name))

        b1_rows = sb("b1_rows", [E * FJ, P])
        b1_turned = sb("b1_turned", [P, E * FJ])
        prob = sb("prob", [P, NT, E])
        rest = sb("rest", [P, NT, E])
        top = [sb(f"top{k}", [P, NT]) for k in range(K)]
        pick = [sb(f"pick{k}", [P, NT]) for k in range(K)]
        chosen = sb("chosen", [P, K, NT, E])
        both = sb("both", [P, NT, E], BF16)
        score = sb("score", [P, NT, E])
        scores = sb("scores", [P, K, NT, E])
        mx = sb("mx", [P, NT])
        sm = sb("sm", [P, NT])
        scan = [sb(f"scan{k}", [P, NT, E]) for k in range(2)]
        totals = sb("totals", [P, NT, E])
        place = sb("place", [P, NT, E])
        cap = sb("cap", [P, E])
        cap_i = sb("cap_i", [P, E], I32)
        ends = [sb(f"ends{k}", [P, E]) for k in range(2)]
        starts = sb("starts", [P, E])
        slot_f = sb("slot_f", [P, K * NT])
        slot = sb("slot", [P, K * NT], I32)
        lane_i = sb("lane_i", [P, K * NT], I32)
        tile_i = sb("tile_i", [P, K * NT], I32)
        lane_f = sb("lane_f", [P, K * NT], BF16)
        tile_f = sb("tile_f", [P, K * NT], BF16)
        past = sb("past", [1, NBLK, E])
        count_f = sb("count_f", [1, NBLK])
        at_lane = sb("at_lane", [P, K * NT, P], BF16)
        at_tile = sb("at_tile", [P, K * NT, NH], BF16)
        what = sb("what", [P, K * NT, 2, NH], BF16)
        found = sb("found", [P, 2 * NH])
        empty = sb("empty", [P, NH])
        to_f = sb("to_f", [P, NH])
        number = sb("number", [P, NH], I32)
        batch_i = sb("batch_i", [P, NH], I32)
        half_i = sb("half_i", [P, NH], I32)
        twice = sb("twice", [P, NH])
        from_f = sb("from_f", [P, NH])

        def bank(name):
            return stack.enter_context(nc.psum_tensor(name, [P, 512], F32))
        b1_bank, prefix_bank, total_bank, found_bank = bank("b1_bank"), bank("prefix_bank"), bank("total_bank"), bank("found_bank")

        ld = sem("r_ld")
        centred, exped, both_done, counted, known = (sem(f"r_{n}") for n in ("cen", "exp", "both", "cnt", "known"))
        gap_c, gap_e = sem("r_gap_c"), sem("r_gap_e")
        b1t_done, b1t_out, b1_stored = sem("r_b1t"), sem("r_b1o"), sem("r_b1s")
        tiles_done, lanes_done = sem("r_tiles"), sem("r_lanes")
        numbered, parted, inverted = sem("r_numbered"), sem("r_parted"), sem("r_inverted")
        dv = sem("r_dv")
        CH = 8
        CW = K * NT // CH

        block = stack.enter_context(nc.Block())

        @block.sync
        def _(eng):
            eng.dma_start(b1_rows[:, :], b1.rearrange("e (j p) -> (e j) p", p=P)).then_inc(ld, 16)
            eng.wait_ge(b1t_out, 1)
            eng.dma_start(b1_cols.rearrange("p e j -> p (e j)"), b1_turned[:, :]).then_inc(b1_stored, 16)
            eng.wait_ge(known, 1)
            for n in range(2):
                e = eng.value_load(expert_of[0:1, n:n + 1], min_val=0, max_val=E - 1)
                load_w1(eng, e, n)
                load_w2(eng, e, n)
            eng.wait_ge(b1_stored, 16)

        @block.gpsimd
        def _(eng):
            g = nc.gpsimd
            for c in range(CH):
                cs = slice(c * CW, (c + 1) * CW)
                eng.wait_ge(tiles_done, c + 1)
                g.tensor_tensor(what[:, cs, 0, :], at_tile[:, cs, :],
                                tables.choice[:, :, :].rearrange("p k n -> p (k n)")[:, cs].unsqueeze(2).to_broadcast([P, CW, NH]),
                                ALU.mult).then_inc(numbered, 1)

        @block.scalar
        def _(eng):
            a = nc.scalar
            eng.wait_ge(b1t_done, 1)
            a.activation(b1_turned[:, :], b1_bank[:, 0:E * FJ], ACT.Copy).then_inc(b1t_out, 1)
            eng.wait_ge(centred, 1)
            a.activation(prob[:, :, :], prob[:, :, :], ACT.Exp).then_inc(exped, 1)
            eng.wait_ge(gap_c, 1)
            a.activation(weight[1][:, :], weight[1][:, :], ACT.Exp).then_inc(gap_e, 1)
            for c in range(CH):
                cs = slice(c * CW, (c + 1) * CW)
                eng.wait_ge(tiles_done, c + 1)
                a.activation(what[:, cs, 1, :], at_tile[:, cs, :], ACT.Identity, scale=tables.part[:, 0:1]).then_inc(parted, 1)

        @block.tensor
        def _(eng):
            pe = nc.tensor
            eng.wait_ge(ld, 16)
            pe.transpose(b1_bank[:, 0:E * FJ], b1_rows[:, :], tables.ident[0:E * FJ, 0:E * FJ]).then_inc(b1t_done, 1)
            eng.wait_ge(both_done, 1)
            every = both[:, :, :].rearrange("p n e -> p (n e)")
            pe.matmul(prefix_bank[:, 0:NT * E], tables.tri[:, :], every, start=True, stop=True)
            pe.matmul(total_bank[:, 0:NT * E], tables.ones[:, :], every, start=True, stop=True).then_inc(counted, 1)
            for c in range(CH):
                eng.wait_ge(lanes_done, c + 1)
                eng.wait_ge(numbered, c + 1)
                eng.wait_ge(parted, c + 1)
                for n in range(c * CW, (c + 1) * CW):
                    last = pe.matmul(found_bank[:, 0:2 * NH], at_lane[:, n, :], what[:, n, :, :].rearrange("p a h -> p (a h)"),
                                     start=(n == 0), stop=(n == K * NT - 1))
            last.then_inc(inverted, 1)

        @block.vector
        def _(eng):
            v = nc.vector
            n_done = [0]

            def then(ins):
                n_done[0] += 1
                ins.then_inc(dv, 1)
                eng.wait_ge(dv, n_done[0])

            lg = tables.lg
            wide = [P, NT, E]
            then(v.tensor_reduce(mx[:, :], lg[:, :, :], axis=AX.X, op=ALU.max))
            v.tensor_tensor(prob[:, :, :], lg[:, :, :], mx[:, :].unsqueeze(2).to_broadcast(wide), ALU.subtract).then_inc(centred, 1)
            eng.wait_ge(exped, 1)
            then(v.tensor_reduce(sm[:, :], prob[:, :, :], axis=AX.X, op=ALU.add))
            then(v.reciprocal(sm[:, :], sm[:, :]))
            then(v.tensor_tensor(prob[:, :, :], prob[:, :, :], sm[:, :].unsqueeze(2).to_broadcast(wide), ALU.mult))
            src = prob
            for k in range(K):
                then(v.tensor_reduce(top[k][:, :], src[:, :, :], axis=AX.X, op=ALU.max))
                then(v.tensor_tensor(score[:, :, :], src[:, :, :], top[k][:, :].unsqueeze(2).to_broadcast(wide), ALU.is_ge))
                then(v.tensor_tensor(score[:, :, :], score[:, :, :], tables.rank_w[:, :].unsqueeze(1).to_broadcast(wide), ALU.mult))
                then(v.tensor_reduce(pick[k][:, :], score[:, :, :], axis=AX.X, op=ALU.max))
                then(v.tensor_tensor(chosen[:, k], score[:, :, :], pick[k][:, :].unsqueeze(2).to_broadcast(wide), ALU.is_equal))
                if k == 0:
                    then(v.scalar_tensor_tensor(out=rest[:, :, :], in0=chosen[:, 0], scalar=-2.0, in1=prob[:, :, :],
                                                op0=ALU.mult, op1=ALU.add))
                    src = rest
            v.tensor_tensor(both[:, :, :], chosen[:, 0], chosen[:, 1], ALU.add).then_inc(both_done, 1)
            v.tensor_tensor(weight[1][:, :], top[1][:, :], top[0][:, :], ALU.subtract).then_inc(gap_c, 1)
            eng.wait_ge(counted, 1)
            then(v.tensor_copy(totals[:, :, :].rearrange("p n e -> p (n e)"), total_bank[:, 0:NT * E]))
            at, step = totals, 1
            n = 0
            while step < NT:
                to = scan[n % 2]
                v.tensor_copy(to[:, 0:step, :], at[:, 0:step, :])
                then(v.tensor_tensor(to[:, step:NT, :], at[:, step:NT, :], at[:, 0:NT - step, :], ALU.add))
                at, step, n = to, step * 2, n + 1
            then(v.tensor_scalar(cap_i[:, :], at[:, NT - 1, :], float(BLK - 1), None, ALU.add))
            then(v.tensor_scalar(cap_i[:, :], cap_i[:, :], LOGB, LOGB, ALU.logical_shift_right, ALU.logical_shift_left))
            then(v.tensor_copy(cap[:, :], cap_i[:, :]))
            end, step, m = cap, 1, 0
            while step < E:
                to = ends[m % 2]
                v.tensor_copy(to[:, 0:step], end[:, 0:step])
                then(v.tensor_tensor(to[:, step:E], end[:, step:E], end[:, 0:E - step], ALU.add))
                end, step, m = to, step * 2, m + 1
            then(v.tensor_tensor(past[:, :, :], tables.blk_at[:, :, :], end[0:1, :].unsqueeze(1).to_broadcast([1, NBLK, E]), ALU.is_ge))
            then(v.tensor_reduce(count_f[:, :], past[:, :, :], axis=AX.X, op=ALU.add))
            v.tensor_scalar(expert_of[:, :], count_f[:, :], float(E - 1), None, ALU.min).then_inc(known, 1)
            then(v.tensor_tensor(starts[:, :], end[:, :], cap[:, :], ALU.subtract))
            then(v.tensor_tensor(place[:, :, :], at[:, :, :], totals[:, :, :], ALU.subtract))
            then(v.tensor_tensor(place[:, :, :].rearrange("p n e -> p (n e)"), prefix_bank[:, 0:NT * E],
                                 place[:, :, :].rearrange("p n e -> p (n e)"), ALU.add))
            then(v.tensor_tensor(place[:, :, :], place[:, :, :], starts[:, :].unsqueeze(1).to_broadcast(wide), ALU.add))
            for k in range(K):
                last = v.tensor_tensor(scores[:, k], place[:, :, :], chosen[:, k], ALU.mult)
            then(last)
            then(v.tensor_reduce(slot_f[:, :], scores[:, :, :, :].rearrange("p k n e -> p (k n) e"), axis=AX.X, op=ALU.add))
            then(v.tensor_copy(slot[:, :], slot_f[:, :]))
            v.tensor_scalar(lane_i[:, :], slot[:, :], P - 1, None, ALU.bitwise_and)
            then(v.tensor_scalar(tile_i[:, :], slot[:, :], P.bit_length() - 1, None, ALU.logical_shift_right))
            v.tensor_copy(lane_f[:, :], lane_i[:, :])
            then(v.tensor_copy(tile_f[:, :], tile_i[:, :]))
            for c in range(CH + 1):
                if c < CH:
                    cs = slice(c * CW, (c + 1) * CW)
                    v.tensor_tensor(at_tile[:, cs, :], tables.tile[:, :].unsqueeze(1).to_broadcast([P, CW, NH]),
                                    tile_f[:, cs].unsqueeze(2).to_broadcast([P, CW, NH]), ALU.is_equal).then_inc(tiles_done, 1)
                if c >= 1:
                    cs = slice((c - 1) * CW, c * CW)
                    v.tensor_tensor(at_lane[:, cs, :], tables.lane[:, :].unsqueeze(1).to_broadcast([P, CW, P]),
                                    lane_f[:, cs].unsqueeze(2).to_broadcast([P, CW, P]), ALU.is_equal).then_inc(lanes_done, 1)
            eng.wait_ge(gap_e, 1)
            then(v.tensor_scalar(sm[:, :], weight[1][:, :], 1.0, None, ALU.add))
            then(v.reciprocal(weight[0][:, :], sm[:, :]))
            v.tensor_tensor(weight[1][:, :], weight[1][:, :], weight[0][:, :], ALU.mult)
            eng.wait_ge(inverted, 1)
            then(v.tensor_copy(found[:, :], found_bank[:, 0:2 * NH]))
            plus_1, part = found[:, 0:NH], found[:, NH:2 * NH]
            v.tensor_scalar(twice[:, :], part, float(ST), None, ALU.mult)
            v.tensor_scalar(empty[:, :], plus_1, 0.0, None, ALU.is_equal)
            then(v.scalar_tensor_tensor(out=to_f[:, :], in0=part, scalar=float(NT * K), in1=plus_1, op0=ALU.mult, op1=ALU.add))
            v.scalar_tensor_tensor(out=number[:, :], in0=plus_1, scalar=-1.0, in1=empty[:, :], op0=ALU.add, op1=ALU.add)
            then(v.tensor_tensor(empty[:, :], empty[:, :], tables.spare[:, :], ALU.mult))
            then(v.tensor_tensor(to_f[:, :], to_f[:, :], empty[:, :], ALU.add))
            v.tensor_scalar(to_row[:, :], to_f[:, :], -1.0, None, ALU.add)
            v.tensor_scalar(batch_i[:, :], number[:, :], 2, 8, ALU.logical_shift_right, ALU.logical_shift_left)
            then(v.tensor_scalar(half_i[:, :], number[:, :], 1, 1, ALU.logical_shift_right, ALU.bitwise_and))
            then(v.tensor_tensor(from_f[:, :], batch_i[:, :], half_i[:, :], ALU.add))
            v.tensor_tensor(from_row[:, :], from_f[:, :], twice[:, :], ALU.add)


class Turn:

    def __init__(self, i, pair, parity):
        self.i, self.pair, self.parity = i, pair, parity

    def count(self, per, n, extra):
        at = per * (2 * self.pair + self.parity + n) + extra
        return min(at, per * NBLK) if self.i is None else affine(self.i, 2 * per, at)

    def of_parity(self, per, extra=0):
        return affine(self.i, per, per * self.pair + extra)

    def block(self, n):
        at = 2 * self.pair + self.parity + n
        return Turn(self.i, at // 2, at % 2)

    @property
    def number(self):
        return affine(self.i, 2, 2 * self.pair + self.parity)

    def exists(self):
        return self.i is not None or 0 <= self.number < NBLK

    def is_number(self, n):
        return self.i is None and self.number == n


def run_blocks(eng, body):
    end = (NBLK - 2) // 2
    for n in range(-2, 2):
        body(Turn(None, n // 2, n % 2))
    with eng.Fori(0, end - 1) as i:
        body(Turn(i, 1, 0))
        body(Turn(i, 1, 1))
    for n in range(2 * end, NBLK + 1):
        body(Turn(None, n // 2, n % 2))


def experts(nc, x2, x2_sb, x2_back, w_raw, ld_w1, ld_w2, load_w1, load_w2, b2, expert_of, ident,
            from_row, to_row, by_token, b1_cols):
    stack = ExitStack()
    with stack:
        def sb(name, shape, dt=F32):
            return stack.enter_context(nc.sbuf_tensor(name, shape, dt))

        def sem(name):
            return stack.enter_context(nc.semaphore(name))

        def two(make, name, *a):
            return [make(f"{name}{k}", *a) for k in range(2)]

        HS = 4
        PIECE = WCOLS // FJ
        wh = two(sb, "wh", [P, WCOLS], F32R)
        wl = two(sb, "wl", [P, WCOLS], F32R)
        x_rows = two(sb, "x_rows", [P, BT, D])
        xh = two(sb, "xh", [P, DC, BLK], F32R)
        xl = two(sb, "xl", [P, DC, BLK], F32R)
        b1_sb = two(sb, "b1_sb", [P, FJ])
        b2_sb = two(sb, "b2_sb", [P, D])
        h = [sb(f"h{k}", [P, BLK]) for k in range(HS)]
        hh = [sb(f"hh{k}", [P, BLK], F32R) for k in range(HS)]
        hl = [sb(f"hl{k}", [P, BLK], F32R) for k in range(HS)]
        y_rows = sb("y_rows", [P, BT, D])
        from_now = two(sb, "from_now", [P, BT], I32)
        to_now = sb("to_now", [P, BT], I32)
        carrier = sb("carrier", [P, 1], I32)

        def bank(name):
            return stack.enter_context(nc.psum_tensor(name, [P, 512], F32))
        HB = 4
        h_bank = [bank(f"h_bank{k}") for k in range(HB)]
        y_bank = [[bank(f"y_bank{k}{n}") for n in range(BT // 2)] for k in range(2)]
        x_bank = bank("x_bank")

        ld_x, ld_b1, ld_b2 = two(sem, "m_ldx"), two(sem, "m_ldb1"), two(sem, "m_ldb2")
        y_stored, from_copied, to_copied = sem("m_stored"), sem("m_from"), sem("m_to")
        pe_x, pe_h, pe_y = sem("m_pe_x"), sem("m_pe_h"), sem("m_pe_y")
        act_w, act_x, act_h = sem("m_act_w"), sem("m_act_x"), sem("m_act_h")
        dve_w, dve_x, dve_hl, dve_y = (sem(f"m_dve_{n}") for n in ("w", "x", "hl", "y"))

        block = stack.enter_context(nc.Block())

        def piece(t, k):
            return t[:, k * PIECE:(k + 1) * PIECE]

        @block.sync
        def _(eng):
            def expert(b):
                return eng.value_load(expert_of[0:1, bass.ds(b.number, 1)], min_val=0, max_val=E - 1)

            def cycle(c):
                far, near, now = (c.block(n) for n in (2, 1, 0))
                if near.exists():
                    e = expert(near)
                    wait(eng, act_h, c.count(FJ, 0, 0))
                    eng.dma_start(b1_sb[near.parity][:, :], b1_cols[:, e, :]).then_inc(ld_b1[near.parity], 16)
                if now.exists():
                    e = expert(now)
                    wait(eng, dve_y, c.count(1, -1, 0))
                    eng.dma_start(b2_sb[now.parity][:, :], b2[e].partition_broadcast(P)).then_inc(ld_b2[now.parity], 16)
                if now.is_number(0):
                    for q in range(4):
                        eng.dma_start(x2_sb[:, q * NT // 4:(q + 1) * NT // 4, :].rearrange("p (b t) d -> p b t d", t=ST),
                                      x2[q * B // 4:(q + 1) * B // 4].rearrange("b p t d -> p b t d")).then_inc(x2_back, 16)
                if far.exists() and not (far.is_number(0) or far.is_number(1)):
                    e = expert(far)
                    wait(eng, dve_w, c.count(FJ, 0, FJ))
                    load_w1(eng, e, far.parity)
                    load_w2(eng, e, far.parity)
            run_blocks(eng, cycle)

        @block.gpsimd
        def _(eng):
            g = nc.gpsimd

            def cycle(c):
                far, was = c.block(2), c.block(-1)
                if was.exists():
                    wait(eng, y_stored, c.count(16 * BT, -1, 0))
                    g.tensor_copy(to_now[:, :], to_row[:, bass.ds(was.number * BT, BT)]).then_inc(to_copied, 1)
                    eng.wait_ge(dve_y, c.count(1, -1, 1))
                    eng.wait_ge(to_copied, c.count(1, -1, 1))
                    g.tensor_tensor(carrier[:, :], to_row[:, 0:1], to_row[:, 1:2], ALU.add)
                    for t in range(BT):
                        g.indirect_dma_start(by_token, bass.IndirectOffsetOnAxis(ap=to_now[:, t:t + 1], axis=0),
                                             y_rows[:, t, :], None, bounds_check=T * K + NBLK * BLK - 1).then_inc(y_stored, 16)
                if far.exists():
                    wait(eng, ld_x[far.parity], far.of_parity(16 * BT))
                    g.tensor_copy(from_now[far.parity][:, :], from_row[:, bass.ds(far.number * BT, BT)]).then_inc(from_copied, 1)
                    wait(eng, pe_x, c.count(1, 0, 1))
                    eng.wait_ge(from_copied, c.count(1, 2, 1))
                    g.tensor_tensor(carrier[:, :], from_row[:, 0:1], from_row[:, 1:2], ALU.add)
                    for t in range(BT):
                        g.indirect_dma_start(x_rows[far.parity][:, t, :], None, x2.rearrange("b p t d -> (b p t) d"),
                                             bass.IndirectOffsetOnAxis(ap=from_now[far.parity][:, t:t + 1], axis=0),
                                             bounds_check=T - 1).then_inc(ld_x[far.parity], 16)
            run_blocks(eng, cycle)
            eng.wait_ge(y_stored, 16 * BT * NBLK)

        @block.scalar
        def _(eng):
            a = nc.scalar

            def cycle(c):
                near, now = c.block(1), c.block(0)
                j2 = c.parity
                for j in range(FJ):
                    if now.exists():
                        if j == 0:
                            eng.wait_ge(ld_b1[j2], now.of_parity(16, 16))
                        eng.wait_ge(pe_h, c.count(FJ, 0, j + 1))
                        wait(eng, dve_hl, c.count(FJ, 0, j + 1 - HS))
                        wait(eng, pe_y, c.count(FJ, 0, j + 1 - HS))
                        for to in (hh, h):
                            last = a.activation(to[j % HS][:, :], h_bank[j % HB][:, 0:BLK], ACT.Gelu, bias=b1_sb[j2][:, j:j + 1])
                        last.then_inc(act_h, 1)
                    if near.exists():
                        if j == 0:
                            eng.wait_ge(ld_w1[near.parity], near.of_parity(16, 16))
                            wait(eng, pe_h, c.count(FJ, 0, 0))
                        if j == FJ // 2:
                            eng.wait_ge(ld_w2[near.parity], near.of_parity(16, 16))
                            wait(eng, pe_y, c.count(FJ, 0, 0))
                        a.activation(piece(wh[near.parity], j), piece(w_raw[near.parity], j), ACT.Copy).then_inc(act_w, 1)
                        if j == 3:
                            eng.wait_ge(pe_x, c.count(1, 1, 1))
                            a.activation(xh[near.parity][:, :, :], x_bank[:, :].rearrange("p (c t) -> p c t", c=DC),
                                         ACT.Copy).then_inc(act_x, 1)
            run_blocks(eng, cycle)

        @block.vector
        def _(eng):
            v = nc.vector

            def cycle(c):
                near, now, was = c.block(1), c.block(0), c.block(-1)
                for j in range(FJ):
                    if j == LAG and was.exists():
                        eng.wait_ge(pe_y, c.count(FJ, -1, FJ))
                        eng.wait_ge(ld_b2[was.parity], was.of_parity(16, 16))
                        wait(eng, y_stored, c.count(16 * BT, -1, 0))
                        for n in range(BT // 2):
                            last = v.tensor_tensor(y_rows[:, 2 * n:2 * n + 2, :],
                                                   y_bank[was.parity][n][:, :].rearrange("p (t d) -> p t d", d=D),
                                                   b2_sb[was.parity][:, :].unsqueeze(1).to_broadcast([P, 2, D]), ALU.add)
                        last.then_inc(dve_y, 1)
                    if now.exists():
                        eng.wait_ge(act_h, c.count(FJ, 0, j + 1))
                        wait(eng, pe_y, c.count(FJ, 0, j + 1 - HS))
                        v.tensor_tensor(hl[j % HS][:, :], h[j % HS][:, :], hh[j % HS][:, :].bitcast(F32),
                                        ALU.subtract).then_inc(dve_hl, 1)
                    if near.exists():
                        wait(eng, pe_h if j < FJ // 2 else pe_y, c.count(FJ, 0, 0))
                        eng.wait_ge(act_w, c.count(FJ, 1, j + 1))
                        v.tensor_tensor(piece(wl[near.parity], j), piece(w_raw[near.parity], j), piece(wh[near.parity], j).bitcast(F32),
                                        ALU.subtract).then_inc(dve_w, 1)
                        if j == 3:
                            eng.wait_ge(act_x, c.count(1, 1, 1))
                            v.tensor_tensor(xl[near.parity][:, :, :], x_bank[:, :].rearrange("p (c t) -> p c t", c=DC),
                                            xh[near.parity][:, :, :].bitcast(F32), ALU.subtract).then_inc(dve_x, 1)
            run_blocks(eng, cycle)

        @block.tensor
        def _(eng):
            pe = nc.tensor

            def second(c, back, m):
                b = c.block(-back)
                w = [t[b.parity][:, DC * FF + m * D:DC * FF + (m + 1) * D] for t in (wh, wl)]
                eng.wait_ge(dve_hl, c.count(FJ, -back, m + 1))
                if m == 0:
                    wait(eng, dve_y, c.count(1, -2, 1))
                    eng.wait_ge(dve_w, c.count(FJ, 0, FJ))
                for t in range(BT):
                    ts = slice(t * P, (t + 1) * P)
                    for n, (l, r) in enumerate(((hh, w[0]), (hh, w[1]), (hl, w[0]))):
                        last = pe.matmul(y_bank[b.parity][t // 2][:, t % 2 * D:(t % 2 + 1) * D], l[m % HS][:, ts], r,
                                         start=(m == 0 and n == 0 and t % 2 == 0), stop=(m == FJ - 1 and n == 2 and t % 2 == 1))
                last.then_inc(pe_y, 1)

            def cycle(c):
                near, now, was = c.block(1), c.block(0), c.block(-1)
                p = c.parity
                for j in range(FJ):
                    if now.exists():
                        if j == 0:
                            eng.wait_ge(dve_w, c.count(FJ, 0, FJ // 2))
                            eng.wait_ge(dve_x, c.count(1, 0, 1))
                        wait(eng, act_h, c.count(FJ, 0, j + 1 - HB))
                        n = 0
                        for a in range(DC):
                            cols = slice(a * FF + j * P, a * FF + (j + 1) * P)
                            for l, r in ((wh, xh), (wh, xl), (wl, xh)):
                                last = pe.matmul(h_bank[j % HB][:, 0:BLK], l[p][:, cols], r[p][:, a, :],
                                                 start=(n == 0), stop=(n == 3 * DC - 1))
                                n += 1
                        last.then_inc(pe_h, 1)
                    if j < LAG:
                        if was.exists():
                            second(c, 1, FJ - LAG + j)
                    elif now.exists():
                        second(c, 0, j - LAG)
                    if j == 2 and near.exists():
                        eng.wait_ge(ld_x[near.parity], near.of_parity(16 * BT, 16 * BT))
                        wait(eng, dve_x, c.count(1, 0, 1))
                        for a in range(DC):
                            for t in range(BT):
                                last = pe.transpose(x_bank[:, a * BLK + t * P:a * BLK + (t + 1) * P],
                                                    x_rows[near.parity][:, t, a * P:(a + 1) * P], ident[:, :])
                        last.then_inc(pe_x, 1)
            run_blocks(eng, cycle)


def combine(nc, x2_sb, x2_back, weight, ident, by_token, g3, b3, out):
    stack = ExitStack()
    with stack:
        def sb(name, shape, dt=F32):
            return stack.enter_context(nc.sbuf_tensor(name, shape, dt))

        def sem(name):
            return stack.enter_context(nc.semaphore(name))

        R = 5
        g_row, b_row = sb("g3_row", [P, D]), sb("b3_row", [P, D])
        got = [sb(f"got{r}", [P, ST, K, D]) for r in range(R)]
        diagonal = [sb(f"diagonal{k}", [P, ST, K, P]) for k in range(4)]
        y = [stack.enter_context(nc.psum_tensor(f"y3{k}", [P, ST, D], F32)) for k in range(4)]
        y_last = [sb(f"y_last{k}", [P, D]) for k in range(4)]
        stats = [sb(f"stats3{k}", [P, ST, 6]) for k in range(2)]
        mv = [sb(f"mv3{k}", [P, ST, 2]) for k in range(4)]
        ve, minus_mean = sb("ve3", [P, ST]), sb("minus_mean3", [P, ST])
        rstd = [sb(f"rstd3{k}", [P, ST]) for k in range(2)]
        shift = [sb(f"shift3{k}", [P, ST]) for k in range(2)]
        eps, half, minus_one = sb("eps3", [P, ST]), sb("half3", [P, ST]), sb("minus_one3", [P, ST])
        O = 4
        o = [sb(f"o3{k}", [P, ST, D]) for k in range(O)]
        ld, const = sem("f_ld"), sem("f_const")
        landed = [sem(f"f_landed{r}") for r in range(R)]
        normed, scaled, ve_done, rs, shifted = (sem(f"f_{n}") for n in ("norm", "scale", "ve", "rs", "shift"))
        stored = [sem(f"f_stored{k}") for k in range(O)]
        mixed = sem("f_mixed")
        spread, summed, st_d, mean_d, gained = (sem(f"f_{n}") for n in ("spread", "summed", "st", "mean", "gain"))
        block = stack.enter_context(nc.Block())
        rows = by_token[0:T * K, :].rearrange("(p n k) d -> p n k d", p=P, k=K)
        wide = [P, ST, D]

        @block.sync
        def _(eng):
            def load(b):
                eng.dma_start(got[b % R][:, :, :, :], rows[:, b * ST:(b + 1) * ST]).then_inc(landed[b % R], 16)

            load(0)
            eng.dma_start(g_row[:, :], g3.partition_broadcast(P)).then_inc(ld, 16)
            eng.dma_start(b_row[:, :], b3.partition_broadcast(P)).then_inc(ld, 16)
            for b in range(1, R):
                load(b)
            for b in range(B):
                if b + R < B:
                    eng.wait_ge(mixed, b + 1)
                    load(b + R)
                if b >= 1:
                    eng.wait_ge(scaled, b)
                    eng.dma_start(out[b - 1].rearrange("(t p) d -> p t d", p=P), o[(b - 1) % O][:, :, :]).then_inc(stored[(b - 1) % O], 16)
            eng.wait_ge(scaled, B)
            eng.dma_start(out[B - 1].rearrange("(t p) d -> p t d", p=P), o[(B - 1) % O][:, :, :]).then_inc(stored[(B - 1) % O], 16)
            for k in range(O):
                eng.wait_ge(stored[k], 16 * B // O)

        @block.gpsimd
        def _(eng):
            g = nc.gpsimd
            g.memset(eps[:, :], EPS).then_inc(const, 1)
            g.memset(half[:, :], -0.5).then_inc(const, 1)
            g.memset(minus_one[:, :], -1.0).then_inc(const, 1)
            eng.wait_ge(const, 3)
            eng.wait_ge(ld, 32)
            for b in range(B + 1):
                if b < B:
                    k = b % 2
                    wait(eng, shifted, b)
                    eng.wait_ge(mean_d, b + 1)
                    g.tensor_tensor(ve[:, :], mv[b % 4][:, :, 1], eps[:, :], ALU.add).then_inc(ve_done, 1)
                    g.tensor_tensor(minus_mean[:, :], mv[b % 4][:, :, 0], minus_one[:, :], ALU.mult)
                    eng.wait_ge(ve_done, b + 1)
                    g.tensor_tensor(rstd[k][:, :], ve[:, :], half[:, :], ALU.pow).then_inc(rs, 1)
                    eng.wait_ge(rs, b + 1)
                    g.tensor_tensor(shift[k][:, :], minus_mean[:, :], rstd[k][:, :], ALU.mult).then_inc(shifted, 1)
                if b >= 1:
                    eng.wait_ge(normed, b)
                    g.tensor_tensor(o[(b - 1) % O][:, :, :], o[(b - 1) % O][:, :, :], g_row[:, :].unsqueeze(1).to_broadcast(wide),
                                    ALU.mult).then_inc(gained, 1)

        @block.scalar
        def _(eng):
            a = nc.scalar
            for b in range(B + 2):
                if b < B:
                    wait(eng, summed, b - 3)
                    for t in range(ST):
                        for k in range(K if t < ST - 1 else K - 1):
                            last = a.activation(diagonal[b % 4][:, t, k, :], ident[:, :], ACT.Identity,
                                                scale=weight[k][:, b * ST + t:b * ST + t + 1])
                    last.then_inc(spread, 1)
                if b >= 2:
                    d = b - 2
                    eng.wait_ge(shifted, d + 1)
                    if d >= O:
                        eng.wait_ge(stored[d % O], 16 * (d // O))
                    for t in range(ST):
                        last = a.activation(o[d % O][:, t, :], y[d % 4][:, t, :] if t < ST - 1 else y_last[d % 4][:, :], ACT.Identity, scale=rstd[d % 2][:, t:t + 1],
                                            bias=shift[d % 2][:, t:t + 1])
                    last.then_inc(normed, 1)

        @block.tensor
        def _(eng):
            pe = nc.tensor
            eng.wait_ge(x2_back, 64)
            for b in range(B):
                eng.wait_ge(landed[b % R], 16 * (b // R + 1))
                eng.wait_ge(spread, b + 1)
                wait(eng, normed, b - 3)
                pe.matmul(y[b % 4][:, :, :].rearrange("p t d -> p (t d)"), ident[:, :],
                          x2_sb[:, b * ST:(b + 1) * ST, :].rearrange("p t d -> p (t d)"), start=True, stop=False)
                for t in range(ST):
                    ks = range(K if t < ST - 1 else K - 1)
                    for k in ks:
                        last = pe.matmul(y[b % 4][:, t, :], diagonal[b % 4][:, t, k, :], got[b % R][:, t, k, :],
                                         start=False, stop=(t == ST - 1 and k == ks[-1]))
                last.then_inc(summed, 1)

        @block.vector
        def _(eng):
            v = nc.vector
            eng.wait_ge(ld, 32)
            for b in range(B + 2):
                if b < B:
                    eng.wait_ge(summed, b + 1)
                    i = b * ST + ST - 1
                    v.scalar_tensor_tensor(out=y_last[b % 4][:, :], in0=got[b % R][:, ST - 1, K - 1, :],
                                           scalar=weight[K - 1][:, i:i + 1], in1=y[b % 4][:, ST - 1, :],
                                           op0=ALU.mult, op1=ALU.add).then_inc(mixed, 1)
                    wait(eng, mean_d, b - 1)
                    for t in range(ST - 1):
                        v.bn_stats(stats[b % 2][:, t, :], y[b % 4][:, t, :])
                    eng.wait_ge(mixed, b + 1)
                    v.bn_stats(stats[b % 2][:, ST - 1, :], y_last[b % 4][:, :]).then_inc(st_d, 1)
                    eng.wait_ge(st_d, b + 1)
                    for t in range(ST):
                        last = v.bn_aggr(mv[b % 4][:, t, :], stats[b % 2][:, t, :])
                    last.then_inc(mean_d, 1)
                if b >= 2:
                    eng.wait_ge(gained, b - 1)
                    k = (b - 2) % O
                    v.tensor_tensor(o[k][:, :, :], o[k][:, :, :], b_row[:, :].unsqueeze(1).to_broadcast(wide), ALU.add).then_inc(scaled, 1)


def layer_program(nc, x, ctxt, sa, ca, norms, router, expert_w, out):
    x2 = nc.dram_tensor("x2_scratch", (B, P, ST, D), F32, kind="Internal").ap()
    outer = ExitStack()
    with outer:
        tables = Tables(lambda name, shape, dt=F32: outer.enter_context(nc.sbuf_tensor(name, shape, dt)))
        attention_program(nc, x, ctxt, sa, ca, norms[0], norms[1], router, tables, x2)
        b1 = expert_w[1]
        moe_program(nc, x2, tables, b1, expert_w[0], expert_w[2], expert_w[3], *norms[2], out)


_PRE = "L0_xattn_"
_ATT = ["wq", "bq", "wk", "bk", "wv", "bv", "wo", "bo"]
_OUTS = [((B, S, D), "float32")]


def kernel(**inputs):
    import numpy as _np
    import concourse.bacc as _bacc
    from concourse import mybir as _mybir
    from concourse.bass_utils import run_bass_kernel_spmd as _run

    nc = _bacc.Bacc("TRN2", target_bir_lowering=False, num_devices=1)
    arrays = {}

    def given(name):
        a = _np.ascontiguousarray(inputs[name])
        arrays[f"in_{name}_dram"] = a
        return nc.dram_tensor(f"in_{name}_dram", a.shape, _mybir.dt.from_np(a.dtype), kind="ExternalInput").ap()

    x, ctxt = given("x"), given("ctx_1024")
    sa = [given(_PRE + "sa_" + n) for n in _ATT]
    ca = [given(_PRE + "ca_" + n) for n in _ATT]
    norms = [(given(f"{_PRE}ln{k}_g"), given(f"{_PRE}ln{k}_b")) for k in (1, 2, 3)]
    router = [given(_PRE + "router_w"), given(_PRE + "router_b")]
    expert_w = [given(_PRE + n) for n in ("e_w1", "e_b1", "e_w2", "e_b2")]
    out = nc.dram_tensor("out_0_dram", _OUTS[0][0], F32, kind="ExternalOutput").ap()
    layer_program(nc, x, ctxt, sa, ca, norms, router, expert_w, out)
    r = _run(nc, [arrays], core_ids=[0])
    return r.results[0]["out_0_dram"]
```
